# Optimizing a Trainium2 kernel written in Bass

```python
import numpy as np
import jax
import jax.numpy as jnp

def _softmax(x, axis=-1):
    return jax.nn.softmax(x, axis=axis)

def _gelu(x):
    return jax.nn.gelu(x, approximate=True)

def _silu(x):
    return jax.nn.silu(x)

def _sigmoid(x):
    return jax.nn.sigmoid(x)

def _layernorm(x, axis=-1, eps=1e-05):
    m = jnp.mean(x, axis=axis, keepdims=True)
    v = jnp.var(x, axis=axis, keepdims=True)
    return (x - m) / jnp.sqrt(v + eps)

def _scatter_add(tgt, idx, src, axis=0):
    return tgt.at[idx].add(src)

def _segment_sum(src, seg, n):
    return jax.ops.segment_sum(src, seg, n)
kernel_name = 'mk_gnn_resnorm_d1_gnn_r8_84e603'

def setup_inputs(seed: int=0):
    np.random.seed(seed)
    _w = jnp.asarray

    def _rec_inputs():
        import jax
        import jax.numpy as jnp
        _gk = jax.random.key(seed)
        x = -0.0003713 + 1 * jax.random.normal(jax.random.fold_in(_gk, 1), (6250, 128), jnp.float32)
        _s = jax.random.randint(jax.random.fold_in(_gk, 2), (50000,), 0, 6250, jnp.int32)
        _d = jax.random.randint(jax.random.fold_in(_gk, 3), (50000,), 0, 6250, jnp.int32)
        _loop = jnp.arange(6250, dtype=jnp.int32)
        src = jnp.concatenate([_s, _d, _loop])
        dst = jnp.concatenate([_d, _s, _loop])
        _o = jnp.argsort(dst, stable=True)
        src = src[_o]
        dst = dst[_o]
        edge_attr_128 = 9.41057e-06 + 1 * jax.random.normal(jax.random.fold_in(_gk, 11), (106250, 128), jnp.float32)
        return (x, src, dst, edge_attr_128)
    x, src, dst, edge_attr_128 = _rec_inputs()

    def _L0_gnn_setup():
        import jax, jax.numpy as jnp
        import numpy as np
        HIDDEN = 128
        HEADS = 8
        HEAD_DIM = HIDDEN // HEADS
        N_NODES = 12500
        N_EDGES = 200000
        key = jax.random.key(seed)
        ks = jax.random.split(key, 12)
        s = 1.0 / np.sqrt(HIDDEN)
        inp = {'x': jax.random.normal(ks[0], (N_NODES, HIDDEN), dtype=jnp.float32), 'edge_index': jax.random.randint(ks[1], (2, N_EDGES), 0, N_NODES, dtype=jnp.int32), 'edge_emb': jax.random.normal(ks[2], (N_EDGES, HIDDEN), dtype=jnp.float32), 'q_w': jax.random.uniform(ks[3], (HIDDEN, HIDDEN), jnp.float32, -s, s), 'q_b': jax.random.uniform(ks[4], (HIDDEN,), jnp.float32, -s, s), 'k_w': jax.random.uniform(ks[5], (HIDDEN, HIDDEN), jnp.float32, -s, s), 'k_b': jax.random.uniform(ks[6], (HIDDEN,), jnp.float32, -s, s), 'v_w': jax.random.uniform(ks[7], (HIDDEN, HIDDEN), jnp.float32, -s, s), 'v_b': jax.random.uniform(ks[8], (HIDDEN,), jnp.float32, -s, s), 'out_w': jax.random.uniform(ks[9], (HIDDEN, HIDDEN), jnp.float32, -s, s), 'out_b': jax.random.uniform(ks[10], (HIDDEN,), jnp.float32, -s, s), 'eb_w': jax.random.uniform(ks[11], (HEADS, HIDDEN), jnp.float32, -s, s), 'eb_b': jnp.zeros((HEADS,), dtype=jnp.float32)}
        return inp
    _L0_gnn_all = _L0_gnn_setup()
    _L0_gnn_in = {k: v for k, v in _L0_gnn_all.items() if k in ('q_w', 'q_b', 'k_w', 'k_b', 'v_w', 'v_b', 'out_w', 'out_b', 'eb_w', 'eb_b')}
    del _L0_gnn_all
    return {'x': x, 'src': src, 'dst': dst, 'edge_attr_128': edge_attr_128, 'L0_gnn_q_w': _L0_gnn_in['q_w'], 'L0_gnn_q_b': _L0_gnn_in['q_b'], 'L0_gnn_k_w': _L0_gnn_in['k_w'], 'L0_gnn_k_b': _L0_gnn_in['k_b'], 'L0_gnn_v_w': _L0_gnn_in['v_w'], 'L0_gnn_v_b': _L0_gnn_in['v_b'], 'L0_gnn_out_w': _L0_gnn_in['out_w'], 'L0_gnn_out_b': _L0_gnn_in['out_b'], 'L0_gnn_eb_w': _L0_gnn_in['eb_w'], 'L0_gnn_eb_b': _L0_gnn_in['eb_b']}

def reference(x, src, dst, edge_attr_128, L0_gnn_q_w, L0_gnn_q_b, L0_gnn_k_w, L0_gnn_k_b, L0_gnn_v_w, L0_gnn_v_b, L0_gnn_out_w, L0_gnn_out_b, L0_gnn_eb_w, L0_gnn_eb_b):
    import jax
    import jax.numpy as jnp

    def _L0_gnn_ref(x, edge_index, edge_emb, q_w, q_b, k_w, k_b, v_w, v_b, out_w, out_b, eb_w, eb_b):
        import jax, jax.numpy as jnp
        import numpy as np
        HIDDEN = 128
        HEADS = 8
        HEAD_DIM = HIDDEN // HEADS
        N_NODES = 12500
        N_EDGES = 200000
        n = x.shape[0]
        q = (x @ q_w.T + q_b).reshape(n, HEADS, HEAD_DIM)
        k = (x @ k_w.T + k_b).reshape(n, HEADS, HEAD_DIM)
        v = (x @ v_w.T + v_b).reshape(n, HEADS, HEAD_DIM)
        row, col = (edge_index[0], edge_index[1])
        scores = jnp.einsum('ehd,ehd->eh', q[row], k[col]) / jnp.sqrt(jnp.float32(HEAD_DIM))
        scores = scores + edge_emb @ eb_w.T + eb_b
        seg_max = jax.ops.segment_max(scores, row, num_segments=n)
        exp_scores = jnp.exp(scores - seg_max[row])
        seg_sum = jax.ops.segment_sum(exp_scores, row, num_segments=n)
        attn = exp_scores / (seg_sum[row] + 1e-10)
        weighted_v = attn[..., None] * v[col]
        out = jax.ops.segment_sum(weighted_v, row, num_segments=n)
        out = out.reshape(n, HIDDEN)
        return out @ out_w.T + out_b
    edge_index = jnp.stack([src, dst])
    x = _layernorm(x + _L0_gnn_ref(x, edge_index, edge_attr_128, L0_gnn_q_w, L0_gnn_q_b, L0_gnn_k_w, L0_gnn_k_b, L0_gnn_v_w, L0_gnn_v_b, L0_gnn_out_w, L0_gnn_out_b, L0_gnn_eb_w, L0_gnn_eb_b), axis=-1)
    return x

_drawn_inputs = setup_inputs


def setup_inputs(seed=0):
    import zlib

    import numpy as np

    out = dict(_drawn_inputs(seed))
    spreads = {'L0_gnn_eb_b': (0.0, 0.8)}
    factors = {'L0_gnn_q_b': 8.0, 'L0_gnn_k_b': 8.0}
    for name, (base, spread) in spreads.items():
        noise = np.random.default_rng([zlib.crc32(name.encode()), seed]).standard_normal(out[name].shape)
        drawn = base * np.exp(spread * noise) if base else spread * noise
        out[name] = jnp.asarray(drawn.astype(out[name].dtype))
    for name, factor in factors.items():
        out[name] = (out[name] * factor).astype(out[name].dtype)
    return out
```

```python
from contextlib import ExitStack

import concourse.bass as bass
import concourse.mybir as mybir

P = 128
F32, BF16, I32 = mybir.dt.float32, mybir.dt.bfloat16, mybir.dt.int32
ALU = mybir.AluOpType
ACT = mybir.ActivationFunctionType
AX = mybir.AxisListType
ds = bass.ds

N, D = 6250, 128
E = 106250
H = 8
DH = D // H
EPS = 1e-5
BN = P - 1
B = -(-N // BN)
BC = B + 2
G = 8
EC = E // P
REST = E - EC * P
SI = -(-(EC + 1) // (2 * G)) * 2
CI = SI * G
T = -(-((E + B * (P - 1)) // P) // (2 * G)) * (2 * G)
ST = T // G
ROWS = T * P + G * P
RW = 16
W = H + D
MT = -(-T // P)
MW = H + W
TRASH = B * P + P
BIG = 1.0e30
FB = 5
assert B % (2 * FB) == 0 and 2 * P * (CI - EC) < ROWS - T * P and SI * G >= EC + 1


def bcast(ap, dim, count):
    shape = list(ap.shape)
    return ap.unsqueeze(dim).broadcast_to(shape[:dim] + [count] + shape[dim:])


def build(nc, x, src, dst, edge, q_w, q_b, k_w, k_b, v_w, v_b, out_w, out_b, eb_w, eb_b, out):
    kv_dram = nc.dram_tensor("kv_rows", [N, 2 * D], F32, kind="Internal").ap()
    rec_dram = nc.dram_tensor("sorted_records", [ROWS, RW], I32, kind="Internal").ap()
    piece_dram = nc.dram_tensor("pieces", [T, W], F32, kind="Internal").ap()
    ends_dram = nc.dram_tensor("segment_ends", [T, H, 4], F32, kind="Internal").ap()
    merge_dram = nc.dram_tensor("merge_rows", [TRASH + MT * P, MW], F32, kind="Internal").ap()

    with ExitStack() as keep:
        sb = lambda name, shape, dt: keep.enter_context(nc.sbuf_tensor(name, shape, dt))
        c = {
            "ident": sb("ident", [P, P], F32), "identb": sb("identb", [P, P], BF16),
            "iota": sb("iota", [P, P], F32), "iotab": sb("iotab", [P, P], BF16),
            "rown": sb("rown", [P, 1], F32), "ones": sb("ones", [P, P], F32),
            "below": sb("below", [P, P], BF16), "belowf": sb("belowf", [P, P], F32),
            "shift": sb("shift", [G * H, G * H], F32), "wrap": sb("wrap", [G * H, G * H], F32),
            "w_kvq": sb("w_kvq", [P, 3 * D], F32), "b_kvq": sb("b_kvq", [1, 3 * D], F32),
            "w_out": sb("w_out", [P, D], F32), "b_out": sb("b_out", [1, D], F32),
            "w_eb": sb("w_eb", [P, H], F32), "b_eb": sb("b_eb", [1, H], F32),
            "bucket_of": sb("bucket_of", [1, T], I32),
        }
        q3 = sb("q3", [P, B, 3, D], BF16)
        with ExitStack() as ranks:
            rsb = lambda name, shape, dt: ranks.enter_context(nc.sbuf_tensor(name, shape, dt))
            r = {
                "meta": rsb("meta", [P, CI, 3], I32),
                "lo": rsb("lo", [P, CI], F32), "hi": rsb("hi", [P, CI], BF16),
                "start_a": rsb("start_a", [P, BC], BF16), "start_r": rsb("start_r", [P, BC], BF16),
            }
            constants(nc, c, x, q_w, q_b, k_w, k_b, v_w, v_b, out_w, out_b, eb_w, eb_b)
            fill(nc, rec_dram, merge_dram)
            project(nc, c, q3, x, kv_dram)
            count(nc, c, r, src, dst)
            rank(nc, c, r, edge, rec_dram)
        acc = sb("acc", [P, B, W], F32)
        attend(nc, c, q3, acc, kv_dram, rec_dram, piece_dram, ends_dram)
        merge(nc, c, piece_dram, ends_dram, merge_dram)
        finish(nc, c, acc, x, merge_dram, out)


def allocators(nc, ctx, stage):
    return (lambda name, shape, dt: ctx.enter_context(nc.sbuf_tensor(f"{stage}_{name}", shape, dt)),
            lambda name, shape, dt: ctx.enter_context(nc.psum_tensor(f"{stage}_{name}", shape, dt)),
            lambda name: ctx.enter_context(nc.semaphore(f"{stage}_{name}")))


def constants(nc, c, x, q_w, q_b, k_w, k_b, v_w, v_b, out_w, out_b, eb_w, eb_b):
    with ExitStack() as ctx:
        sb, psum, sem = allocators(nc, ctx, "constants")
        w_raw = sb("w_raw", [P, 5, D], F32)
        b_raw = sb("b_raw", [1, 3 * D], F32)
        w_ps = psum("w_ps", [P, 8, P], F32)
        w_in = sem("w_in")
        filled = sem("filled")
        const_done = sem("const_done")
        w_turned = sem("w_turned")
        block = ctx.enter_context(nc.Block())
        @block.sync
        def _(sp):
            for k, w in enumerate((k_w, v_w, q_w, out_w)):
                sp.dma_start(w_raw[:, k, :], w).then_inc(w_in, 16)
            sp.dma_start(w_raw[0:H, 4, :], eb_w).then_inc(w_in, 16)
            sp.dma_start(b_raw[0:1, 0:D], k_b.rearrange("(a n) -> a n", a=1)).then_inc(w_in, 16)
            sp.dma_start(b_raw[0:1, D:2 * D], v_b.rearrange("(a n) -> a n", a=1)).then_inc(w_in, 16)
            sp.dma_start(b_raw[0:1, 2 * D:3 * D], q_b.rearrange("(a n) -> a n", a=1)).then_inc(w_in, 16)
            sp.dma_start(c["b_out"][:], out_b.rearrange("(a n) -> a n", a=1)).then_inc(w_in, 16)
            sp.dma_start(c["b_eb"][:], eb_b.rearrange("(a n) -> a n", a=1)).then_inc(w_in, 16)
            sp.wait_ge(w_in, 16 * 10)

        @block.gpsimd
        def _(pool):
            pool.memset(c["ident"][:], 0.0).then_inc(filled, 1)
            pool.memset(c["ones"][:], 1.0).then_inc(filled, 1)
            pool.memset(c["shift"][:], 0.0).then_inc(filled, 1)
            pool.memset(c["wrap"][:], 0.0).then_inc(filled, 1)
            pool.iota(c["iota"][:], [[1, P]], base=0, channel_multiplier=0,
                      allow_small_or_imprecise_dtypes=True).then_inc(const_done, 1)
            pool.iota(c["iotab"][:], [[1, P]], base=0, channel_multiplier=0,
                      allow_small_or_imprecise_dtypes=True).then_inc(const_done, 1)
            pool.iota(c["rown"][:], [[0, 1]], base=0, channel_multiplier=1,
                      allow_small_or_imprecise_dtypes=True).then_inc(const_done, 1)
            pool.wait_ge(filled, 4)
            pool.affine_select(out=c["ident"][:], in_=c["ident"][:], compare_op=ALU.not_equal, fill=1.0,
                               base=0, pattern=[[-1, P]], channel_multiplier=1).then_inc(const_done, 1)
            pool.affine_select(out=c["belowf"][:], in_=c["ones"][:], compare_op=ALU.is_ge, fill=0.0,
                               base=-1, pattern=[[1, P]], channel_multiplier=-1).then_inc(const_done, 1)
            pool.affine_select(out=c["shift"][:], in_=c["shift"][:], compare_op=ALU.not_equal, fill=1.0,
                               base=H, pattern=[[-1, G * H]], channel_multiplier=1).then_inc(const_done, 1)
            pool.affine_select(out=c["wrap"][:], in_=c["wrap"][:], compare_op=ALU.not_equal, fill=1.0,
                               base=H - G * H, pattern=[[-1, G * H]], channel_multiplier=1).then_inc(const_done, 1)

        @block.tensor
        def _(pe):
            pe.wait_ge(w_in, 16 * 10)
            pe.wait_ge(const_done, 7)
            for k in range(4):
                pe.transpose(w_ps[:, k, :], w_raw[:, k, :], c["ident"][:])
            pe.transpose(w_ps[:, 4, 0:H], w_raw[0:H, 4, :], c["ident"][0:H, 0:H]).then_inc(w_turned, 1)

        @block.vector
        def _(dve):
            dve.wait_ge(const_done, 7)
            dve.tensor_copy(c["identb"][:], c["ident"][:])
            dve.tensor_copy(c["below"][:], c["belowf"][:])
            dve.wait_ge(w_in, 16 * 10)
            heads_in = lambda ap: ap.rearrange("p (h d) -> p d h", h=H)
            heads_out = lambda ap: ap.rearrange("p (d h) -> p d h", h=H)
            dve.tensor_copy(c["b_kvq"][:, 0:D], b_raw[:, 0:D])
            dve.tensor_copy(heads_out(c["b_kvq"][:, D:2 * D]), heads_in(b_raw[:, D:2 * D]))
            dve.tensor_scalar(c["b_kvq"][:, 2 * D:], b_raw[:, 2 * D:], DH ** -0.5, None, ALU.mult)
            dve.wait_ge(w_turned, 1)
            dve.tensor_copy(c["w_kvq"][:, 0:D], w_ps[:, 0, :])
            dve.tensor_copy(heads_out(c["w_kvq"][:, D:2 * D]), heads_in(w_ps[:, 1, :]))
            dve.tensor_scalar(c["w_kvq"][:, 2 * D:], w_ps[:, 2, :], DH ** -0.5, None, ALU.mult)
            dve.tensor_copy(c["w_eb"][:], w_ps[:, 4, 0:H])

    with ExitStack() as ctx:
        sb, psum, sem = allocators(nc, ctx, "constants2")
        w_perm = sb("w_perm", [P, D], F32)
        w_rows = sb("w_rows", [P, D], F32)
        wo_ps = psum("wo_ps", [P, D], F32)
        wo_in = sem("wo_in")
        wo_perm = sem("wo_perm")
        wo_turned = sem("wo_turned")
        block = ctx.enter_context(nc.Block())
        @block.sync
        def _(sp):
            sp.dma_start(w_rows[:], out_w).then_inc(wo_in, 16)

        @block.vector
        def _(dve):
            dve.wait_ge(wo_in, 16)
            dve.tensor_copy(w_perm[:].rearrange("p (d h) -> p d h", h=H),
                            w_rows[:].rearrange("p (h d) -> p d h", h=H)).then_inc(wo_perm, 1)
            dve.wait_ge(wo_turned, 1)
            dve.tensor_copy(c["w_out"][:], wo_ps[:])

        @block.tensor
        def _(pe):
            pe.wait_ge(wo_perm, 1)
            pe.transpose(wo_ps[:], w_perm[:], c["ident"][:]).then_inc(wo_turned, 1)


def fill(nc, rec_dram, merge_dram):
    per = ROWS // P // G
    mper = B * P // P // 2
    assert ROWS == P * per * G and B % 2 == 0
    with ExitStack() as ctx:
        sb, psum, sem = allocators(nc, ctx, "fill")
        blank = sb("blank", [P, per, RW], I32)
        zero = sb("zero", [P, mper, MW], F32)
        zeroed = sem("zeroed")
        blank_ready = sem("blank_ready")
        blanks_out = sem("blanks_out")
        zeros_out = sem("zeros_out")
        block = ctx.enter_context(nc.Block())
        @block.vector
        def _(dve):
            dve.memset(blank[:], 0).then_inc(zeroed, 1)
            dve.wait_ge(zeroed, 1)
            dve.memset(blank[:, :, H], -1).then_inc(blank_ready, 1)
            dve.memset(blank[:, :, H + 1], 200).then_inc(blank_ready, 1)
            dve.memset(zero[:], 0.0).then_inc(blank_ready, 1)

        @block.sync
        def _(sp):
            sp.wait_ge(blank_ready, 3)
            for k in range(G):
                sp.dma_start(rec_dram[k * P * per:(k + 1) * P * per, :].rearrange("(p r) w -> p r w", p=P),
                             blank[:]).then_inc(blanks_out, 16)
            for k in range(2):
                sp.dma_start(merge_dram[k * P * mper:(k + 1) * P * mper, :].rearrange("(p r) w -> p r w", p=P),
                             zero[:]).then_inc(zeros_out, 16)
            sp.wait_ge(blanks_out, 16 * G)
            sp.wait_ge(zeros_out, 32)


def bucket_rows(dram, k, tail):
    whole = FB - 1 if tail else FB
    by_row = dram[ds(k * (FB * BN), whole * BN), :].rearrange("(j p) d -> p j d", p=BN)
    parts = [(slice(1, 65), by_row[0:64], slice(0, whole)), (slice(65, P), by_row[64:BN], slice(0, whole))]
    if tail:
        at = (B - 1) * BN
        parts.append((slice(1, 1 + N - at), dram[at:N, :].rearrange("(j p) d -> p j d", j=1), slice(FB - 1, FB)))
    return parts


def in_pairs(eng, step, steps):
    step(0, 0)
    step(0, 1)
    with eng.Fori(1, steps // 2 - 1) as k:
        step(k, 0)
        step(k, 1)
    step(steps // 2 - 1, 0)
    step(steps // 2 - 1, 1)


def project(nc, c, q3, x, kv_dram):
    S = B // FB
    first = lambda k: isinstance(k, int) and k == 0
    end = lambda k, u: isinstance(k, int) and k == S // 2 - 1 and u == 1
    with ExitStack() as ctx:
        sb, psum, sem = allocators(nc, ctx, "project")
        x_rows = sb("x_rows", [P, 2, FB, D], F32)
        x_t = sb("x_t", [P, FB, P], F32)
        kv_out = sb("kv_out", [P, 2, FB, 2 * D], F32)
        q_left = sb("q_left", [P, FB, D], F32)
        turn_ps = psum("turn_ps", [P, 8, P], F32)
        kv_ps = psum("kv_ps", [P, 6, 2 * D], F32)
        q_ps = psum("q_ps", [P, 8, D], F32)
        x_in = [sem(f"x_in{u}") for u in range(2)]
        kv_stored = [sem(f"kv_stored{u}") for u in range(2)]
        x_zeroed, x_turned, x_kept, kv_ready, q_ready, kv_kept, q_part0, q_rest, q_part1, q_part2 = map(
            sem, ("x_zeroed", "x_turned", "x_kept", "kv_ready", "q_ready", "kv_kept", "q_part0", "q_rest", "q_part1", "q_part2"))
        block = ctx.enter_context(nc.Block())
        @block.sync
        def _(sp):
            sp.wait_ge(x_zeroed, 1)

            def step(k, u):
                if not first(k):
                    sp.wait_ge(x_turned, 2 * k + u - 1)
                for p, rows, j in bucket_rows(x, 2 * k + u, end(k, u)):
                    sp.dma_start(x_rows[p, u, j, :], rows).then_inc(x_in[u], 16)

            in_pairs(sp, step, S)

        @block.tensor
        def _(pe):
            def step(k, u):
                s = 2 * k + u
                pe.wait_ge(x_in[u], 32 * (k + 1) + (16 if end(k, u) else 0))
                if not (first(k) and u == 0):
                    pe.wait_ge(x_kept, s)
                for j in range(FB):
                    mm = pe.transpose(turn_ps[:, j, :], x_rows[:, u, j, :], c["ident"][:])
                mm.then_inc(x_turned, 1)
                pe.wait_ge(x_kept, s + 1)
                if not (first(k) and u == 0):
                    pe.wait_ge(q_rest, s)
                for j in range(FB):
                    pe.matmul(q_ps[:, j, :], x_t[:, j, :], c["w_kvq"][:, 2 * D:], start=True, stop=False)
                    mm = pe.matmul(q_ps[:, j, :], c["ones"][0:1, :], c["b_kvq"][:, 2 * D:], start=False, stop=True)
                mm.then_inc(q_ready, 1)
                if not (first(k) and u == 0):
                    pe.wait_ge(kv_kept, s)
                for j in range(FB):
                    pe.matmul(kv_ps[:, j, :], x_t[:, j, :], c["w_kvq"][:, 0:2 * D], start=True, stop=False)
                    mm = pe.matmul(kv_ps[:, j, :], c["ones"][0:1, :], c["b_kvq"][:, 0:2 * D], start=False, stop=True)
                mm.then_inc(kv_ready, 1)

            in_pairs(pe, step, S)

        @block.scalar
        def _(act):
            def step(k, u):
                s = 2 * k + u
                act.wait_ge(x_turned, s + 1)
                if not (first(k) and u == 0):
                    act.wait_ge(kv_ready, s)
                act.copy(x_t[:], turn_ps[:, 0:FB, :]).then_inc(x_kept, 1)
                act.wait_ge(q_ready, s + 1)
                act.copy(q3[:, ds(s * FB, FB), 0, :], q_ps[:, 0:FB, :]).then_inc(q_part0, 1)
                act.wait_ge(kv_ready, s + 1)
                if not first(k):
                    act.wait_ge(kv_stored[u], k * 32)
                act.copy(kv_out[:, u], kv_ps[:, 0:FB, :]).then_inc(kv_kept, 1)
                act.wait_ge(kv_kept, s + 1)
                for p, rows, j in bucket_rows(kv_dram, s, end(k, u)):
                    act.dma_start(rows, kv_out[p, u, j, :]).then_inc(kv_stored[u], 16)

            in_pairs(act, step, S)
            act.wait_ge(kv_stored[0], 16 * S)
            act.wait_ge(kv_stored[1], 16 * S + 16)

        @block.vector
        def _(dve):
            def step(k, u):
                s = 2 * k + u
                part = lambda m: q3[:, ds(s * FB, FB), m, :]
                dve.wait_ge(q_part0, s + 1)
                if not (first(k) and u == 0):
                    dve.wait_ge(q_part2, s)
                dve.tensor_tensor(q_left[:], q_ps[:, 0:FB, :], part(0), ALU.subtract).then_inc(q_rest, 1)
                dve.wait_ge(q_rest, s + 1)
                dve.tensor_copy(part(1), q_left[:]).then_inc(q_part1, 1)
                dve.wait_ge(q_part1, s + 1)
                dve.tensor_tensor(part(2), q_left[:], part(1), ALU.subtract).then_inc(q_part2, 1)

            dve.memset(x_rows[:], 0.0).then_inc(x_zeroed, 1)
            in_pairs(dve, step, S)


def one_hot_lo(dve, out, iotab, lo, col):
    for t in range(G):
        ins = dve.tensor_scalar(out[:, t, :], iotab, lo[:, ds(col + t, 1)], None, ALU.is_equal)
    return ins


def one_hot_hi(dve, out, iotab, hi, col):
    return dve.tensor_tensor(out, bcast(iotab[:, 0:BC], 1, G), bcast(hi[:, ds(col, G)], 2, BC), ALU.is_equal)


def count(nc, c, r, src, dst):
    with ExitStack() as ctx:
        sb, psum, sem = allocators(nc, ctx, "count")
        src_c = sb("src_c", [P, CI], I32)
        dst_c = sb("dst_c", [P, CI], I32)
        srcf = sb("srcf", [P, CI], F32)
        hif = sb("hif", [P, CI], F32)
        hii = sb("hii", [P, CI], I32)
        off = sb("off", [P, CI], F32)
        low = sb("low", [P, CI], F32)
        hot_lo = sb("hot_lo", [P, 2, G, P], BF16)
        hot_hi = sb("hot_hi", [P, 2, G, BC], BF16)
        cnt = sb("cnt", [P, BC], F32)
        toti = sb("toti", [P, BC], I32)
        tiles = sb("tiles", [P, B], F32)
        last = sb("last", [P, B], F32)
        first = sb("first", [P, BC], F32)
        onesb = sb("onesb", [P, B], F32)
        lastc = sb("lastc", [P, 1], F32)
        iota_t = sb("iota_t", [P, T], F32)
        ended = sb("ended", [P, T], F32)
        zerob = sb("zerob", [P, P], BF16)
        cnt_ps = psum("cnt_ps", [P, 512], F32)
        tot_ps = psum("tot_ps", [P, 512], F32)
        turn_ps = psum("turn_ps", [P, 512], F32)
        bkt_ps = psum("bkt_ps", [P, 2, 512], F32)
        idx_in = sem("idx_in")
        blank_src = sem("blank_src")
        rest_in = sem("rest_in")
        split = sem("split")
        hot_ready = sem("hot_ready")
        hot_used = sem("hot_used")
        counted = sem("counted")
        step_done = sem("step_done")
        summed = sem("summed")
        aux = sem("aux")
        block = ctx.enter_context(nc.Block())
        half = T // 2

        @block.sync
        def _(sp):
            sp.dma_start(src_c[:, 0:EC], src[0:EC * P].rearrange("(p j) -> p j", p=P)).then_inc(idx_in, 16)
            sp.dma_start(dst_c[:, 0:EC], dst[0:EC * P].rearrange("(p j) -> p j", p=P)).then_inc(idx_in, 16)
            sp.wait_ge(blank_src, 2)
            sp.dma_start(src_c[0:REST, EC:EC + 1], src[EC * P:E].rearrange("(p j) -> p j", j=1)).then_inc(rest_in, 16)
            sp.dma_start(dst_c[0:REST, EC:EC + 1], dst[EC * P:E].rearrange("(p j) -> p j", j=1)).then_inc(rest_in, 16)

        @block.gpsimd
        def _(pool):
            pool.iota(src_c[:, EC:CI], [[0, CI - EC]], base=B * BN, channel_multiplier=1).then_inc(blank_src, 1)
            pool.memset(dst_c[:, EC:CI], 0).then_inc(blank_src, 1)
            pool.iota(iota_t[:], [[1, T]], base=0, channel_multiplier=0,
                      allow_small_or_imprecise_dtypes=True).then_inc(aux, 1)
            pool.memset(onesb[:], 1.0).then_inc(aux, 1)
            pool.memset(zerob[:], 0.0).then_inc(aux, 1)
            pool.iota(first[:, B:BC], [[P * (CI - EC), BC - B]], base=T * P, channel_multiplier=CI - EC,
                      allow_small_or_imprecise_dtypes=True).then_inc(aux, 1)

        @block.vector
        def _(dve):
            n = [0]

            def then(ins):
                n[0] += 1
                ins.then_inc(split, 1)
                dve.wait_ge(split, n[0])

            dve.wait_ge(idx_in, 32)
            dve.wait_ge(rest_in, 32)
            then(dve.tensor_copy(srcf[:], src_c[:]))
            then(dve.tensor_scalar(hii[:], srcf[:], 1.0 / BN, 0.5 / BN - 0.5, ALU.mult, ALU.add))
            then(dve.tensor_copy(hif[:], hii[:]))
            then(dve.scalar_tensor_tensor(off[:], hif[:], -float(BN), srcf[:], ALU.mult, ALU.add))
            dve.tensor_scalar(low[:], off[:], 0.0, None, ALU.is_lt)
            then(dve.tensor_scalar(off[:], off[:], float(BN), None, ALU.is_ge))
            then(dve.tensor_tensor(off[:], off[:], low[:], ALU.subtract))
            then(dve.tensor_tensor(hif[:], hif[:], off[:], ALU.add))
            dve.tensor_copy(r["hi"][:], hif[:])
            then(dve.scalar_tensor_tensor(low[:], hif[:], -float(BN), srcf[:], ALU.mult, ALU.add))
            then(dve.tensor_scalar(r["lo"][:], low[:], 1.0, None, ALU.add))
            dve.tensor_copy(r["meta"][:, :, 0], src_c[:])
            dve.tensor_copy(r["meta"][:, :, 1], r["lo"][:])
            then(dve.tensor_copy(r["meta"][:, :, 2], dst_c[:]))

            def hot(k, u):
                one_hot_lo(dve, hot_lo[:, u], c["iotab"][:], r["lo"], (2 * k + u) * G)
                one_hot_hi(dve, hot_hi[:, u], c["iotab"], r["hi"], (2 * k + u) * G).then_inc(hot_ready, 1)

            hot(0, 0)
            hot(0, 1)
            with dve.Fori(1, SI // 2) as k:
                for u in range(2):
                    dve.wait_ge(hot_used, 2 * k + u - 1)
                    hot(k, u)
            dve.wait_ge(counted, 1)
            then(dve.tensor_copy(cnt[:], cnt_ps[:, 0:BC]))
            dve.wait_ge(summed, 1)
            dve.wait_ge(aux, 4)
            then(dve.tensor_scalar(toti[:], tot_ps[:, 0:BC], float(P - 1), None, ALU.add))
            then(dve.tensor_scalar(toti[:], toti[:], 7, None, ALU.logical_shift_right))
            then(dve.tensor_copy(tiles[:], toti[:, 0:B]))
            then(dve.tensor_tensor_scan(last[:], onesb[:], tiles[:], 0.0, ALU.mult, ALU.add))
            then(dve.tensor_tensor(tiles[:], last[:], tiles[:], ALU.subtract))
            then(dve.scalar_tensor_tensor(first[:, 0:B], tiles[:], float(P), tot_ps[:, 256:256 + B], ALU.mult, ALU.add))
            then(dve.tensor_copy(r["start_a"][:], first[:]))
            then(dve.tensor_tensor(r["start_r"][:], first[:], r["start_a"][:], ALU.subtract))
            dve.wait_ge(summed, 2)
            then(dve.tensor_copy(lastc[0:B, :], turn_ps[0:B, 0:1]))
            then(dve.tensor_scalar(ended[0:B, :], iota_t[0:B, :], lastc[0:B, 0:1], None, ALU.is_ge))
            dve.sem_inc(step_done, 1)
            dve.wait_ge(summed, 3)
            then(dve.tensor_scalar(c["bucket_of"][:].rearrange("a (k t) -> a k t", k=2), bkt_ps[0:1, :, 0:half],
                                   float(B - 1), None, ALU.min))

        @block.tensor
        def _(pe):
            pe.wait_ge(aux, 4)
            pe.matmul(cnt_ps[:, 0:BC], zerob[:], zerob[:, 0:BC], start=True, stop=False)
            with pe.Fori(0, SI // 2) as k:
                for u in range(2):
                    pe.wait_ge(hot_ready, 2 * k + u + 1)
                    for t in range(G):
                        mm = pe.matmul(cnt_ps[:, 0:BC], hot_lo[:, u, t, :], hot_hi[:, u, t, :], start=False, stop=False)
                    mm.then_inc(hot_used, 1)
            pe.matmul(cnt_ps[:, 0:BC], zerob[:], zerob[:, 0:BC], start=False, stop=True).then_inc(counted, 1)
            pe.wait_ge(split, COUNT_COPIED)
            pe.matmul(tot_ps[:, 0:BC], c["ones"][:], cnt[:], start=True, stop=True)
            pe.matmul(tot_ps[:, 256:256 + BC], c["belowf"][:], cnt[:], start=True, stop=True).then_inc(summed, 1)
            pe.wait_ge(split, LAST_TILE)
            pe.transpose(turn_ps[0:B, 0:P], last[:], c["ident"][:]).then_inc(summed, 1)
            pe.wait_ge(step_done, 1)
            for k in range(2):
                mm = pe.matmul(bkt_ps[0:1, k, 0:half], c["ones"][0:B, 0:1], ended[0:B, k * half:(k + 1) * half],
                               start=True, stop=True)
            mm.then_inc(summed, 1)


COUNT_COPIED = 11
LAST_TILE = COUNT_COPIED + 4


def rank(nc, c, r, edge, rec_dram):
    with ExitStack() as ctx:
        sb, psum, sem = allocators(nc, ctx, "rank")
        edges = sb("edges", [P, 2, G, D], F32)
        edges_t = sb("edges_t", [P, 2, G // 2, P], F32)
        hot_lo = sb("hot_lo", [P, 2, G, P], BF16)
        hot_hi = sb("hot_hi", [P, 2, G, BC], BF16)
        hot_lo_t = sb("hot_lo_t", [P, 2, G, P], BF16)
        before = sb("before", [P, 2, G, P], BF16)
        next_a = sb("next_a", [P, 2, G + 1, BC], BF16)
        next_r = sb("next_r", [P, 2, G + 1, BC], BF16)
        picked = sb("picked", [P, G, BC], F32)
        slotf = sb("slotf", [P, G], F32)
        slot = sb("slot", [P, G], I32)
        within = sb("within", [P, G], I32)
        tile8 = sb("tile8", [P, G], I32)
        group = sb("group", [P, G], I32)
        row = sb("row", [P, 2, G], I32)
        record = sb("record", [P, 2, G, RW], I32)
        turn_ps = psum("turn_ps", [P, G, P], BF16)
        edge_ps = psum("edge_ps", [P, 2, 4, P], F32)
        next_ps = psum("next_ps", [P, 512], F32)
        same_ps = psum("same_ps", [P, 2, 4, P], F32)
        slot_ps = psum("slot_ps", [P, 512], F32)
        bias_ps = psum("bias_ps", [P, 512], F32)
        opened = sem("opened")
        edges_in = [sem(f"edges_in{u}") for u in range(2)]
        scattered = [sem(f"scattered{u}") for u in range(2)]
        edges_turned, edges_kept, bias_ready, bias_kept = map(sem, ("edges_turned", "edges_kept", "bias_ready", "bias_kept"))
        hot_ready, lo_turned, lo_kept, same_ready, before_ready = map(
            sem, ("hot_ready", "lo_turned", "lo_kept", "same_ready", "before_ready"))
        next_ready, next_a_kept, next_r_kept, slots_ready = map(
            sem, ("next_ready", "next_a_kept", "next_r_kept", "slots_ready"))
        picked_ready, slotf_ready, slot_ready, bits_ready, joined, rows_ready, meta_kept, table_ready = map(
            sem, ("picked_ready", "slotf_ready", "slot_ready", "bits_ready", "joined", "rows_ready", "meta_kept", "table_ready"))
        block = ctx.enter_context(nc.Block())
        LAST = SI - 1
        tail = EC - LAST * G
        assert 0 < tail < G

        first = lambda k: isinstance(k, int) and k == 0
        end = lambda k, u: isinstance(k, int) and k == SI // 2 - 1 and u == 1

        @block.sync
        def _(sp):
            by_col = edge[0:EC * P, :].rearrange("(p j) d -> p j d", p=P)

            def step(k, u):
                if not first(k):
                    sp.wait_ge(edges_turned, 2 * (2 * (k - 1) + u) + 2)
                if end(k, u):
                    sp.dma_start(edges[:, u, 0:tail, :], by_col[:, LAST * G:EC, :]).then_inc(edges_in[u], 16)
                    sp.dma_start(edges[0:REST, u, tail, :], edge[EC * P:E, :]).then_inc(edges_in[u], 16)
                else:
                    sp.dma_start(edges[:, u, :, :], by_col[:, ds((2 * k + u) * G, G), :]).then_inc(edges_in[u], 16)

            in_pairs(sp, step, SI)

        @block.gpsimd
        def _(pool):
            def step(k, u):
                s = 2 * k + u
                pool.wait_ge(rows_ready, s + 1)
                pool.wait_ge(meta_kept, s + 1)
                pool.wait_ge(bias_kept, s + 1)
                pool.sem_inc(opened, 1)
                for t in range(G):
                    pool.indirect_dma_start(rec_dram[:, :], bass.IndirectOffsetOnAxis(ap=row[:, u, t:t + 1], axis=0),
                                            record[:, u, t, :], None).then_inc(scattered[u], 16)

            in_pairs(pool, step, SI)
            for u in range(2):
                pool.wait_ge(scattered[u], 16 * G * (SI // 2))

        @block.tensor
        def _(pe):
            def turn_lo(s, u):
                pe.wait_ge(hot_ready, s + 1)
                if not (isinstance(s, int) and s == 0):
                    pe.wait_ge(lo_kept, s)
                for t in range(G):
                    mm = pe.transpose(turn_ps[:, t, :], hot_lo[:, u, t, :], c["identb"][:])
                mm.then_inc(lo_turned, 1)

            def step(k, u):
                s = 2 * k + u
                if first(k) and u == 0:
                    pe.wait_ge(table_ready, 2)
                else:
                    pe.wait_ge(next_r_kept, s)
                base = lambda part: bcast(part[:, 1 - u, G, :], 1, G + 1)
                table = next_ps[:, 0:(G + 1) * BC].rearrange("p (t b) -> p t b", t=G + 1)
                pe.matmul(table, c["identb"][:], base(next_a), start=True, stop=False)
                pe.matmul(table, c["identb"][:], base(next_r), start=False, stop=False)
                for t in range(G):
                    mm = pe.matmul(table[:, t + 1:, :], hot_lo[:, u, t, :], bcast(hot_hi[:, u, t, :], 1, G - t),
                                   start=False, stop=(t == G - 1))
                mm.then_inc(next_ready, 1)
                pe.wait_ge(lo_kept, s + 1)
                for q in range(2):
                    if not (first(k) and u == 0):
                        pe.wait_ge(before_ready, 2 * s - 1 + q)
                    for t in range(4):
                        mm = pe.matmul(same_ps[:, q, t, :], hot_lo_t[:, u, 4 * q + t, :], hot_lo_t[:, u, 4 * q + t, :],
                                       start=True, stop=True)
                    mm.then_inc(same_ready, 1)
                pe.wait_ge(edges_in[u], 16 * (k + 1) + (16 if end(k, u) else 0))
                for q in range(2):
                    if not (first(k) and u == 0):
                        pe.wait_ge(edges_kept, 2 * s - 1 + q)
                    for t in range(4):
                        mm = pe.transpose(edge_ps[:, q, t, :], edges[:, u, 4 * q + t, :], c["ident"][:])
                    mm.then_inc(edges_turned, 1)
                if not end(k, u):
                    turn_lo(s + 1, 1 - u)
                if not (first(k) and u == 0):
                    pe.wait_ge(bias_kept, s)
                for t in range(G):
                    if t % 4 == 0:
                        pe.wait_ge(edges_kept, 2 * s + t // 4 + 1)
                    o = bias_ps[:, t * H:(t + 1) * H]
                    pe.matmul(o, c["ones"][0:1, :], c["b_eb"][:], start=True, stop=False)
                    mm = pe.matmul(o, edges_t[:, t // 4, t % 4, :], c["w_eb"][:], start=False, stop=True)
                mm.then_inc(bias_ready, 1)
                pe.wait_ge(next_r_kept, s + 1)
                if not (first(k) and u == 0):
                    pe.wait_ge(picked_ready, s)
                for t in range(G):
                    if t % 4 == 0:
                        pe.wait_ge(before_ready, 2 * s + t // 4 + 1)
                    o = slot_ps[:, t * BC:(t + 1) * BC]
                    pe.matmul(o, hot_lo_t[:, u, t, :], next_a[:, u, t, :], start=True, stop=False)
                    pe.matmul(o, hot_lo_t[:, u, t, :], next_r[:, u, t, :], start=False, stop=False)
                    mm = pe.matmul(o, before[:, u, t, :], hot_hi[:, u, t, :], start=False, stop=True)
                mm.then_inc(slots_ready, 1)

            turn_lo(0, 0)
            in_pairs(pe, step, SI)

        @block.scalar
        def _(act):
            def keep_lo(s, u):
                act.wait_ge(lo_turned, s + 1)
                act.copy(hot_lo_t[:, u], turn_ps[:]).then_inc(lo_kept, 1)

            def step(k, u):
                s = 2 * k + u
                act.wait_ge(next_ready, s + 1)
                if not first(k):
                    act.wait_ge(slots_ready, s - 1)
                act.copy(next_a[:, u].rearrange("p t b -> p (t b)"), next_ps[:, 0:(G + 1) * BC]).then_inc(next_a_kept, 1)
                for q in range(2):
                    act.wait_ge(edges_turned, 2 * s + q + 1)
                    if not (first(k) and u == 0):
                        act.wait_ge(bias_ready, s)
                    act.copy(edges_t[:, q], edge_ps[:, q]).then_inc(edges_kept, 1)
                if not end(k, u):
                    if not (first(k) and u == 0):
                        act.wait_ge(slots_ready, s)
                    keep_lo(s + 1, 1 - u)
                act.wait_ge(bias_ready, s + 1)
                if not first(k):
                    act.wait_ge(scattered[u], 16 * G * k)
                act.copy(record[:, u, :, 0:H].bitcast(F32), bias_ps[:, 0:G * H].rearrange("p (t h) -> p t h", t=G)
                         ).then_inc(bias_kept, 1)

            act.wait_ge(table_ready, 1)
            keep_lo(0, 0)
            in_pairs(act, step, SI)

        @block.vector
        def _(dve):
            def hot(s, u):
                one_hot_lo(dve, hot_lo[:, u], c["iotab"][:], r["lo"], s * G)
                one_hot_hi(dve, hot_hi[:, u], c["iotab"], r["hi"], s * G).then_inc(hot_ready, 1)

            def step(k, u):
                s = 2 * k + u
                for q in range(2):
                    dve.wait_ge(same_ready, 2 * s + q + 1)
                    if not first(k):
                        dve.wait_ge(slots_ready, s - 1)
                    dve.tensor_tensor(before[:, u, 4 * q:4 * q + 4, :], same_ps[:, q], bcast(c["below"][:], 1, 4),
                                      ALU.mult).then_inc(before_ready, 1)
                dve.wait_ge(next_a_kept, s + 1)
                dve.tensor_tensor(next_r[:, u].rearrange("p t b -> p (t b)"), next_ps[:, 0:(G + 1) * BC],
                                  next_a[:, u].rearrange("p t b -> p (t b)"), ALU.subtract).then_inc(next_r_kept, 1)
                if not end(k, u):
                    if not (first(k) and u == 0):
                        dve.wait_ge(slots_ready, s)
                    hot(s + 1, 1 - u)
                if not first(k):
                    dve.wait_ge(scattered[u], 16 * G * k)
                dve.tensor_copy(record[:, u, :, H:H + 3], r["meta"][:, ds(s * G, G), :]).then_inc(meta_kept, 1)
                dve.wait_ge(slots_ready, s + 1)
                dve.tensor_tensor(picked[:], slot_ps[:, 0:G * BC].rearrange("p (t b) -> p t b", t=G), hot_hi[:, u],
                                  ALU.mult).then_inc(picked_ready, 1)
                dve.wait_ge(picked_ready, s + 1)
                dve.tensor_reduce(slotf[:], picked[:], AX.X, ALU.add).then_inc(slotf_ready, 1)
                dve.wait_ge(slotf_ready, s + 1)
                dve.tensor_copy(slot[:], slotf[:]).then_inc(slot_ready, 1)
                dve.wait_ge(slot_ready, s + 1)
                dve.tensor_scalar(within[:], slot[:], P - 1, 3, ALU.bitwise_and, ALU.logical_shift_left)
                dve.tensor_scalar(tile8[:], slot[:], 7, G - 1, ALU.logical_shift_right, ALU.bitwise_and)
                dve.tensor_scalar(group[:], slot[:], 10, 10, ALU.logical_shift_right, ALU.logical_shift_left
                                  ).then_inc(bits_ready, 1)
                dve.wait_ge(bits_ready, s + 1)
                dve.tensor_tensor(within[:], within[:], tile8[:], ALU.bitwise_or).then_inc(joined, 1)
                dve.wait_ge(joined, s + 1)
                dve.tensor_tensor(row[:, u, :], within[:], group[:], ALU.bitwise_or).then_inc(rows_ready, 1)

            hot(0, 0)
            dve.memset(record[:], 0).then_inc(table_ready, 1)
            dve.tensor_copy(next_a[:, 1, G, :], r["start_a"][:])
            dve.tensor_copy(next_r[:, 1, G, :], r["start_r"][:]).then_inc(table_ready, 1)
            in_pairs(dve, step, SI)


def buckets(nc, c, engine, s):
    _, values = nc.values_load_multi_w_load_instructions(
        c["bucket_of"][0:1, ds(s * G, G)], engines=[engine], min_val=0, max_val=B - 1,
        skip_runtime_bounds_check_because="count() bounds them by a min with B - 1")
    return values


def attend(nc, c, q3, acc, kv_dram, rec_dram, piece_dram, ends_dram):
    GH = G * H
    with ExitStack() as ctx:
        sb, psum, sem = allocators(nc, ctx, "attend")
        rec = sb("rec", [P, 2, G, RW], I32)
        kv = sb("kv", [P, 2, G, 2 * D], F32)
        keyf = sb("keyf", [P, 2, G, H], F32)
        row_b = sb("row_b", [P, 2, G], BF16)
        key_t = sb("key_t", [GH, 2, P], F32)
        reset = sb("reset", [GH, P + 1], F32)
        begun = sb("begun", [GH, 1], F32)
        carried = sb("carried", [GH, P], F32)
        keep = sb("keep", [P, G], F32)
        row_f = sb("row_f", [P, G], F32)
        off2 = sb("off2", [P, 2, 4, P], BF16)
        hot_t = sb("hot_t", [P, 2, G, P], BF16)
        hot = sb("hot", [P, 2, G, P], F32)
        prod = sb("prod", [P, 2, 4, D], F32)
        score = sb("score", [P, 2, G, H], F32)
        run_max = sb("run_max", [GH, P], F32)
        seg_max = sb("seg_max", [GH, 2, P], F32)
        wv = sb("wv", [P, 2, G, W], F32)
        piece = sb("piece", [1, 2, G, W], F32)
        ends = sb("ends", [GH, 2, 4], F32)
        neg_row = sb("neg_row", [P, 1], F32)
        key_ps = psum("key_ps", [P, 512], F32)
        seg_ps = psum("seg_ps", [P, 512], F32)
        lo_ps = psum("lo_ps", [P, 2, 4, P], F32)
        q_ps = psum("q_ps", [P, 2, 4, P], F32)
        sum_ps = psum("sum_ps", [P, 2, 512], F32)
        opened, turns_opened, load_opened = map(sem, ("opened", "turns_opened", "load_opened"))
        rec_in = [sem(f"rec_in{u}") for u in range(2)]
        kv_in = [sem(f"kv_in{u}") for u in range(2)]
        ends_out = [sem(f"ends_out{u}") for u in range(2)]
        pieces_out = [sem(f"pieces_out{u}") for u in range(2)]
        cleared, keys_ready, keys_turned, keys_kept, same_ready, reset_ready, shifted, begun_ready = map(
            sem, ("cleared", "keys_ready", "keys_turned", "keys_kept", "same_ready", "reset_ready", "shifted", "begun_ready"))
        carried_ready, carried_turned, keep_ready, row_ready, hot_ready, lo_turned, squared, hot_t_ready = map(
            sem, ("carried_ready", "carried_turned", "keep_ready", "row_ready", "hot_ready", "lo_turned", "squared", "hot_t_ready"))
        q_ready, prod_ready, dot_ready, score_ready, scores_turned, run_ready, max_ready, max_turned, rel_ready = map(
            sem, ("q_ready", "prod_ready", "dot_ready", "score_ready", "scores_turned", "run_ready", "max_ready", "max_turned", "rel_ready"))
        exp_ready, weighted, sums_ready, summed, piece_kept, ends_kept = map(
            sem, ("exp_ready", "weighted", "sums_ready", "summed", "piece_kept", "ends_kept"))
        block = ctx.enter_context(nc.Block())
        first = lambda k: isinstance(k, int) and k == 0
        start = lambda k, u: first(k) and u == 0

        @block.sync
        def _(sp):
            def step(k, u):
                s = 2 * k + u
                if not first(k):
                    sp.wait_ge(score_ready, s - 1)
                    sp.sem_inc(load_opened, 1)
                    sp.wait_ge(kv_in[u], 16 * G * k)
                    sp.sem_inc(load_opened, 1)
                sp.dma_start(rec[:, u], rec_dram[ds(s * (G * P), G * P), :].rearrange("(p t) w -> p t w", t=G)
                             ).then_inc(rec_in[u], 16)

            in_pairs(sp, step, ST)

        @block.gpsimd
        def _(pool):
            def step(k, u):
                s = 2 * k + u
                if not first(k):
                    pool.wait_ge(weighted, s - 1)
                pool.wait_ge(rec_in[u], 16 * (k + 1))
                pool.sem_inc(opened, 1)
                for t in range(G):
                    pool.indirect_dma_start(kv[:, u, t, :], None, kv_dram[:, :],
                                            bass.IndirectOffsetOnAxis(ap=rec[:, u, t, H + 2:H + 3], axis=0)
                                            ).then_inc(kv_in[u], 16)

            in_pairs(pool, step, ST)

        @block.tensor
        def _(pe):
            def sums(s, u):
                pe.wait_ge(weighted, s + 1)
                pe.wait_ge(hot_ready, s + 1)
                for t in range(G):
                    if t % 2 == 0 and not (isinstance(s, int) and s == 0 and t < 4):
                        pe.wait_ge(piece_kept, (G // 2) * s + t // 2 - 1)
                    o = sum_ps[:, t // 2 % 2, (t % 2) * W:(t % 2 + 1) * W]
                    mm = pe.matmul(o, hot[:, u, t, :], wv[:, u, t, :], start=True, stop=True)
                    if t % 2:
                        mm.then_inc(sums_ready, 1)

            def step(k, u):
                s = 2 * k + u
                pe.wait_ge(keys_ready, s + 1)
                if not start(k, u):
                    pe.wait_ge(keep_ready, s)
                pe.sem_inc(turns_opened, 1)
                pe.transpose(key_ps[0:GH, 0:P], keyf[:, u].rearrange("p t h -> p (t h)"), c["ident"][:]).then_inc(keys_turned, 1)
                for q in range(2):
                    if not start(k, u):
                        pe.wait_ge(squared, 2 * s - 1 + q)
                    for t in range(4):
                        mm = pe.matmul(lo_ps[:, q, t, :], row_b[:, u, 4 * q + t:4 * q + t + 1].broadcast_to([P, P]),
                                       c["identb"][:], start=True, stop=True)
                    mm.then_inc(lo_turned, 1)
                pe.wait_ge(keys_kept, s + 1)
                pe.sem_inc(turns_opened, 1)
                pe.matmul(key_ps[0:GH, P:P + 1], c["shift"][:], key_t[:, u, P - 1:P], start=True, stop=False)
                pe.matmul(key_ps[0:GH, P:P + 1], c["wrap"][:], key_t[:, 1 - u, P - 1:P], start=False, stop=True).then_inc(shifted, 1)
                pe.wait_ge(carried_ready, s + 1)
                pe.sem_inc(turns_opened, 1)
                pe.transpose(key_ps[:, 192:192 + GH], carried[:], c["ident"][0:GH, 0:GH]).then_inc(carried_turned, 1)
                if not start(k, u):
                    sums(s - 1, 1 - u)
                bucket = buckets(nc, c, mybir.EngineType.PE, s)
                for q in range(2):
                    pe.wait_ge(hot_t_ready, 2 * s + q + 1)
                    if not start(k, u):
                        pe.wait_ge(prod_ready, 2 * s - 1 + q)
                    for t in range(4):
                        for part in range(3):
                            mm = pe.matmul(q_ps[:, q, t, :], hot_t[:, u, 4 * q + t, :], q3[:, ds(bucket[4 * q + t], 1), part, :],
                                           start=(part == 0), stop=(part == 2))
                    mm.then_inc(q_ready, 1)
                pe.wait_ge(score_ready, s + 1)
                if not start(k, u):
                    pe.wait_ge(rel_ready, s)
                pe.sem_inc(turns_opened, 1)
                pe.transpose(seg_ps[0:GH, 0:P], score[:, u].rearrange("p t h -> p (t h)"), c["ident"][:]).then_inc(scores_turned, 1)
                pe.wait_ge(max_ready, s + 1)
                pe.sem_inc(turns_opened, 1)
                pe.transpose(seg_ps[:, 192:192 + GH], seg_max[:, u, :], c["ident"][0:GH, 0:GH]).then_inc(max_turned, 1)

            pe.wait_ge(cleared, 1)
            in_pairs(pe, step, ST)
            sums(ST - 1, 1)

        @block.scalar
        def _(act):
            def pieces(k, s, u):
                if not (isinstance(k, int) and k < 1):
                    act.wait_ge(pieces_out[u], 16 * k + 1)
                for t in range(0, G, 2):
                    act.wait_ge(summed, G * s + t + 2)
                    act.copy(piece[:, u, t:t + 2, :], sum_ps[0:1, t // 2 % 2, 0:2 * W].rearrange("a (t w) -> a t w", t=2)
                             ).then_inc(piece_kept, 1)
                act.wait_ge(piece_kept, (G // 2) * (s + 1))
                act.dma_start(piece_dram[ds(s * G, G), :].rearrange("(a t) w -> a t w", a=1), piece[:, u]
                              ).then_inc(pieces_out[u], 16)

            def step(k, u):
                s = 2 * k + u
                for q in range(2):
                    act.wait_ge(lo_turned, 2 * s + q + 1)
                    act.activation(off2[:, q], lo_ps[:, q], ACT.Square, bias=neg_row[:, 0:1]).then_inc(squared, 1)
                for q in range(2):
                    act.wait_ge(squared, 2 * s + q + 1)
                    if not first(k):
                        act.wait_ge(q_ready, 2 * s - 3 + q)
                    act.activation(hot_t[:, u, 4 * q:4 * q + 4, :], off2[:, q], ACT.Relu, bias=1.0, scale=-1.0).then_inc(hot_t_ready, 1)
                if not start(k, u):
                    pieces(k - 1 if u == 0 else k, s - 1, 1 - u)
                act.wait_ge(max_ready, s + 1)
                if not first(k):
                    act.wait_ge(ends_out[u], 16 * k)
                act.copy(ends[:, u, 0:2], seg_max[:, u, 0:P:P - 1])
                act.copy(ends[:, u, 2:4], key_t[:, u, 0:P:P - 1]).then_inc(ends_kept, 1)
                act.wait_ge(rel_ready, s + 1)
                if not first(k):
                    act.wait_ge(sums_ready, (G // 2) * (s - 1))
                act.activation(wv[:, u, :, 0:H], score[:, u], ACT.Exp).then_inc(exp_ready, 1)
                act.wait_ge(ends_kept, s + 1)
                act.dma_start(ends_dram[ds(s * G, G), :, :].rearrange("t h w -> (t h) w"), ends[:, u, :]).then_inc(ends_out[u], 16)

            act.wait_ge(cleared, 1)
            for u in range(2):
                act.sem_inc(pieces_out[u], 1)
            in_pairs(act, step, ST)
            pieces(ST // 2 - 1, ST - 1, 1)
            for u in range(2):
                act.wait_ge(pieces_out[u], 16 * (ST // 2) + 1)
                act.wait_ge(ends_out[u], 16 * (ST // 2))

        @block.vector
        def _(dve):
            def weigh(s, u):
                dve.wait_ge(exp_ready, s + 1)
                dve.tensor_tensor(wv[:, u, :, H:].rearrange("p t (d h) -> p t d h", h=H),
                                  kv[:, u, :, D:].rearrange("p t (d h) -> p t d h", h=H),
                                  bcast(wv[:, u, :, 0:H], 2, DH), ALU.mult).then_inc(weighted, 1)

            def add(bucket, s, tiles):
                for t in tiles:
                    if t % 2 == 0:
                        dve.wait_ge(sums_ready, (G // 2) * s + t // 2 + 1)
                    if not (isinstance(s, int) and s == 0 and t == 0):
                        dve.wait_ge(summed, G * s + t)
                    a = acc[:, ds(bucket[t], 1), :].rearrange("p b w -> p (b w)")
                    dve.tensor_tensor(a, sum_ps[:, t // 2 % 2, (t % 2) * W:(t % 2 + 1) * W], a, ALU.add).then_inc(summed, 1)

            def step(k, u):
                s = 2 * k + u
                dve.wait_ge(rec_in[u], 16 * (k + 1))
                dve.tensor_copy(keyf[:, u], rec[:, u, :, H:H + 1].broadcast_to([P, G, H]))
                dve.tensor_copy(row_b[:, u], rec[:, u, :, H + 1]).then_inc(keys_ready, 1)
                if not start(k, u):
                    weigh(s - 1, 1 - u)
                dve.wait_ge(keys_turned, s + 1)
                if not first(k):
                    dve.wait_ge(ends_kept, s - 1)
                dve.tensor_copy(key_t[:, u, :], key_ps[0:GH, 0:P]).then_inc(keys_kept, 1)
                dve.wait_ge(keys_kept, s + 1)
                dve.tensor_tensor(reset[:, 1:P], key_t[:, u, 1:P], key_t[:, u, 0:P - 1], ALU.is_equal).then_inc(same_ready, 1)
                dve.wait_ge(same_ready, s + 1)
                dve.tensor_scalar(reset[:, 1:P], reset[:, 1:P], 1.0, BIG, ALU.subtract, ALU.mult).then_inc(reset_ready, 1)
                dve.wait_ge(shifted, s + 1)
                dve.tensor_tensor(begun[:], key_ps[0:GH, P:P + 1], key_t[:, u, 0:1], ALU.is_equal).then_inc(begun_ready, 1)
                dve.wait_ge(begun_ready, s + 1)
                dve.tensor_scalar(carried[:], key_t[:, u, :], key_t[:, u, 0:1], begun[:, 0:1], ALU.is_equal, ALU.mult
                                  ).then_inc(carried_ready, 1)
                if not start(k, u):
                    bucket = buckets(nc, c, mybir.EngineType.DVE, s - 1)
                    add(bucket, s - 1, range(0, 4))
                dve.wait_ge(carried_turned, s + 1)
                dve.tensor_scalar(keep[:], key_ps[:, 192:192 + GH:H], -1.0, 1.0, ALU.mult, ALU.add).then_inc(keep_ready, 1)
                dve.wait_ge(keep_ready, s + 1)
                dve.tensor_tensor(row_f[:], rec[:, u, :, H + 1], keep[:], ALU.mult).then_inc(row_ready, 1)
                dve.wait_ge(row_ready, s + 1)
                for t in range(G):
                    ins = dve.tensor_scalar(hot[:, u, t, :], c["iota"][:], row_f[:, t:t + 1], None, ALU.is_equal)
                ins.then_inc(hot_ready, 1)
                if not start(k, u):
                    add(bucket, s - 1, range(4, G))
                dve.wait_ge(kv_in[u], 16 * G * (k + 1))
                for q in range(2):
                    dve.wait_ge(q_ready, 2 * s + q + 1)
                    dve.tensor_tensor(prod[:, q], q_ps[:, q], kv[:, u, 4 * q:4 * q + 4, 0:D], ALU.mult).then_inc(prod_ready, 1)
                for q in range(2):
                    dve.wait_ge(prod_ready, 2 * s + q + 1)
                    dve.tensor_reduce(score[:, u, 4 * q:4 * q + 4, :], prod[:, q].rearrange("p t (h d) -> p t h d", h=H),
                                      AX.X, ALU.add).then_inc(dot_ready, 1)
                dve.wait_ge(dot_ready, 2 * s + 2)
                dve.tensor_tensor(score[:, u], score[:, u], rec[:, u, :, 0:H].bitcast(F32), ALU.add).then_inc(score_ready, 1)
                dve.wait_ge(scores_turned, s + 1)
                dve.wait_ge(reset_ready, s + 1)
                dve.tensor_tensor_scan(run_max[:], reset[:, 0:P], seg_ps[0:GH, 0:P], -BIG, ALU.add, ALU.max).then_inc(run_ready, 1)
                dve.wait_ge(run_ready, s + 1)
                dve.tensor_tensor_scan(seg_max[:, u, ::-1], reset[:, P:0:-1], run_max[:, ::-1], -BIG, ALU.add, ALU.max
                                       ).then_inc(max_ready, 1)
                dve.wait_ge(max_turned, s + 1)
                dve.tensor_tensor(score[:, u], score[:, u], seg_ps[:, 192:192 + GH].rearrange("p (t h) -> p t h", t=G), ALU.subtract
                                  ).then_inc(rel_ready, 1)

            dve.tensor_scalar(neg_row[:], c["rown"][:], -1.0, None, ALU.mult)
            dve.memset(reset[:], -BIG)
            dve.memset(key_t[:, 1, :], -5.0)
            dve.memset(acc[:], 0.0).then_inc(cleared, 1)
            dve.wait_ge(cleared, 1)
            in_pairs(dve, step, ST)
            weigh(ST - 1, 1)
            add(buckets(nc, c, mybir.EngineType.DVE, ST - 1), ST - 1, range(G))


def merge(nc, c, piece_dram, ends_dram, merge_dram):
    TP = MT * P
    with ExitStack() as ctx:
        sb, psum, sem = allocators(nc, ctx, "merge")
        ends = sb("ends", [H, T, 4], F32)
        top = sb("top", [H, 2 * T], F32)
        key = sb("key", [H, 2 * T], F32)
        reset = sb("reset", [H, 2 * T + 1], F32)
        run_max = sb("run_max", [H, 2 * T], F32)
        seg_max = sb("seg_max", [H, 2 * T], F32)
        scale = sb("scale", [H, 2 * T], F32)
        carry = sb("carry", [H, T + 1], F32)
        whole = sb("whole", [H, T], F32)
        begins = sb("begins", [H, T], F32)
        rows = sb("row_table", [H, 4, TP], F32)
        spare = sb("spare", [H, T], F32)
        last_row = sb("last_row", [H, T], F32)
        cols = sb("cols", [P, 4, MT, H], F32)
        index = sb("index", [P, MT], I32)
        piece = sb("piece", [P, MT, W], F32)
        part = sb("part", [P, MT, MW], F32)
        same = sb("same", [P, MT, TP], F32)
        total = sb("total", [P, MT, MW], F32)
        col_ps = psum("col_ps", [P, 512], F32)
        key_ps = psum("key_ps", [P, 2, 512], F32)
        total_ps = psum("total_ps", [P, 3, 512], F32)
        ends_in, piece_in, cleared, done, exp_ready, rows_ready, cols_ready, keys_ready, part_ready, total_ready, total_kept, scattered = map(
            sem, ("ends_in", "piece_in", "cleared", "done", "exp_ready", "rows_ready", "cols_ready", "keys_ready",
                  "part_ready", "total_ready", "total_kept", "scattered"))
        rel_ready = sem("rel_ready")
        block = ctx.enter_context(nc.Block())
        full = T // P
        rest = T - full * P

        @block.sync
        def _(sp):
            sp.dma_start(ends[:], ends_dram.rearrange("t h w -> h t w")).then_inc(ends_in, 16)
            sp.wait_ge(cleared, 2)
            sp.dma_start(piece[:, 0:full, :], piece_dram[0:full * P, :].rearrange("(j p) w -> p j w", p=P)).then_inc(piece_in, 16)
            if rest:
                sp.dma_start(piece[0:rest, full:MT, :], piece_dram[full * P:T, :].rearrange("(j p) w -> p j w", j=1)
                             ).then_inc(piece_in, 16)

        @block.gpsimd
        def _(pool):
            pool.iota(spare[:], [[1, T]], base=TRASH, channel_multiplier=0, allow_small_or_imprecise_dtypes=True)
            pool.iota(rows[:, 2, :], [[1, TP]], base=TRASH, channel_multiplier=0,
                      allow_small_or_imprecise_dtypes=True).then_inc(cleared, 1)
            pool.wait_ge(total_kept, MT)
            for j in range(MT):
                pool.indirect_dma_start(merge_dram[:, :], bass.IndirectOffsetOnAxis(ap=index[:, j:j + 1], axis=0),
                                        total[:, j, :], None).then_inc(scattered, 16)
            pool.wait_ge(scattered, 16 * MT)

        @block.scalar
        def _(act):
            act.wait_ge(rel_ready, 1)
            act.activation(scale[:], scale[:], ACT.Exp).then_inc(exp_ready, 1)

        @block.tensor
        def _(pe):
            pe.wait_ge(rows_ready, 1)
            for k in range(2):
                mm = pe.matmul(key_ps[:, k, 0:TP // 2], c["ones"][0:1, :], rows[0:1, 3, k * (TP // 2):(k + 1) * (TP // 2)],
                               start=True, stop=True)
            mm.then_inc(keys_ready, 1)
            for m in range(4):
                for j in range(MT):
                    mm = pe.transpose(col_ps[:, (m * MT + j) * H:(m * MT + j + 1) * H], rows[:, m, j * P:(j + 1) * P],
                                      c["ident"][0:H, 0:H])
            mm.then_inc(cols_ready, 1)
            pe.wait_ge(part_ready, 1)
            for j in range(MT):
                o = total_ps[:, j // 3, (j % 3) * MW:(j % 3 + 1) * MW]
                for i in range(MT):
                    mm = pe.matmul(o, same[:, i, j * P:(j + 1) * P], part[:, i, :], start=(i == 0), stop=(i == MT - 1))
            mm.then_inc(total_ready, 1)

        @block.vector
        def _(dve):
            n = [0]

            def then(ins):
                n[0] += 1
                ins.then_inc(done, 1)
                dve.wait_ge(done, n[0])

            dve.wait_ge(cleared, 1)
            dve.memset(rows[:, 0:2, :], 0.0)
            dve.memset(rows[:, 3, :], -7.0)
            dve.memset(carry[:], 0.0)
            dve.memset(reset[:], -BIG)
            then(dve.memset(piece[:], 0.0))
            dve.sem_inc(cleared, 1)
            dve.wait_ge(ends_in, 16)
            dve.tensor_copy(top[:].rearrange("h (t e) -> h t e", e=2), ends[:, :, 0:2])
            then(dve.tensor_copy(key[:].rearrange("h (t e) -> h t e", e=2), ends[:, :, 2:4]))
            then(dve.tensor_tensor(reset[:, 1:2 * T], key[:, 1:], key[:, 0:2 * T - 1], ALU.is_equal))
            then(dve.tensor_scalar(reset[:, 1:2 * T], reset[:, 1:2 * T], 1.0, BIG, ALU.subtract, ALU.mult))
            then(dve.tensor_tensor_scan(run_max[:], reset[:, 0:2 * T], top[:], -BIG, ALU.add, ALU.max))
            then(dve.tensor_tensor_scan(seg_max[:, ::-1], reset[:, 2 * T:0:-1], run_max[:, ::-1], -BIG, ALU.add, ALU.max))
            dve.tensor_tensor(scale[:], top[:], seg_max[:], ALU.subtract).then_inc(rel_ready, 1)
            first, last = key[:, 0::2], key[:, 1::2]
            dve.tensor_tensor(carry[:, 1:T], key[:, 2::2], key[:, 1:2 * T - 1:2], ALU.is_equal)
            then(dve.tensor_tensor(whole[:], first, last, ALU.is_equal))
            then(dve.tensor_tensor(begins[:], whole[:], carry[:, 0:T], ALU.mult))
            then(dve.tensor_scalar(begins[:], begins[:], -1.0, 1.0, ALU.mult, ALU.add))
            dve.wait_ge(exp_ready, 1)
            dve.tensor_tensor(rows[:, 0, 0:T], scale[:, 0::2], carry[:, 0:T], ALU.mult)
            then(dve.tensor_scalar(rows[:, 1, 1:T], scale[:, 1:2 * T - 1:2], 1.0, None, ALU.subtract))
            then(dve.tensor_tensor(rows[:, 1, 1:T], rows[:, 1, 1:T], begins[:, 0:T - 1], ALU.mult))
            then(dve.tensor_tensor(rows[:, 1, 1:T], rows[:, 1, 1:T], carry[:, 1:T], ALU.mult))
            then(dve.tensor_tensor(last_row[:], whole[:], carry[:, 1:T + 1], ALU.mult))
            then(dve.tensor_scalar(last_row[:], last_row[:], -1.0, 1.0, ALU.mult, ALU.add))
            then(dve.tensor_tensor(last_row[:], last_row[:], carry[:, 0:T], ALU.mult))
            then(dve.scalar_tensor_tensor(last_row[:], first, 0.0, last_row[:], ALU.is_ge, ALU.mult))
            then(dve.scalar_tensor_tensor(whole[:], first, 1.0, spare[:], ALU.add, ALU.subtract))
            then(dve.tensor_tensor(whole[:], whole[:], last_row[:], ALU.mult))
            then(dve.tensor_tensor(rows[:, 2, 0:T], whole[:], spare[:], ALU.add))
            then(dve.tensor_copy(rows[:, 3, 0:T], first))
            dve.sem_inc(rows_ready, 1)
            dve.wait_ge(cols_ready, 1)
            then(dve.tensor_copy(cols[:].rearrange("p m j h -> p (m j h)"), col_ps[:, 0:4 * MT * H]))
            dve.tensor_copy(index[:], cols[:, 2, :, 0])
            dve.wait_ge(keys_ready, 1)
            for i in range(MT):
                dve.tensor_scalar(same[:, i, :].rearrange("p (k t) -> p k t", k=2), key_ps[:, :, 0:TP // 2],
                                  cols[:, 3, i, 0:1], None, ALU.is_equal)
            dve.wait_ge(piece_in, 16 + (16 if rest else 0))
            dve.tensor_copy(part[:, :, 0:H], cols[:, 1])
            dve.tensor_tensor(part[:, :, H:].rearrange("p j (d h) -> p j d h", h=H),
                              piece[:].rearrange("p j (d h) -> p j d h", h=H),
                              bcast(cols[:, 0], 2, W // H), ALU.mult).then_inc(part_ready, 1)
            dve.wait_ge(total_ready, 1)
            for j in range(MT):
                dve.tensor_copy(total[:, j, :], total_ps[:, j // 3, (j % 3) * MW:(j % 3 + 1) * MW]).then_inc(total_kept, 1)


def finish(nc, c, acc, x, merge_dram, out):
    S = B // FB
    first = lambda k: isinstance(k, int) and k == 0
    start = lambda k, u: first(k) and u == 0
    end = lambda k, u: isinstance(k, int) and k == S // 2 - 1 and u == 1
    with ExitStack() as ctx:
        sb, psum, sem = allocators(nc, ctx, "finish")
        x_rows = sb("x_rows", [P, 2, FB, D], F32)
        add = sb("add", [P, 2, FB, MW], F32)
        factor = sb("factor", [P, FB, H], F32)
        both = sb("both", [P, FB, W], F32)
        share = sb("share", [P, FB, H], F32)
        mixed = sb("mixed", [P, FB, D], F32)
        mixed_t = sb("mixed_t", [P, FB, P], F32)
        res = sb("res", [P, FB, D], F32)
        stats = sb("stats", [P, FB, 6], F32)
        moments = sb("moments", [P, FB, 2], F32)
        dev = sb("dev", [P, FB], F32)
        scale = sb("scale", [P, FB], F32)
        eps = sb("eps", [P, 1], F32)
        y = sb("y", [P, 2, FB, D], F32)
        turn_ps = psum("turn_ps", [P, 8, P], F32)
        out_ps = psum("out_ps", [P, 8, D], F32)
        rows_in = [sem(f"rows_in{u}") for u in range(2)]
        y_out = [sem(f"y_out{u}") for u in range(2)]
        load_opened, stats_opened = sem("load_opened"), sem("stats_opened")
        x_zeroed, factor_ready, scaled, both_ready, share_ready, inverse_ready, mixed_ready = map(
            sem, ("x_zeroed", "factor_ready", "scaled", "both_ready", "share_ready", "inverse_ready", "mixed_ready"))
        turned, turn_kept, projected, res_ready, stats_ready, moments_ready, dev_ready, scale_ready, y_ready = map(
            sem, ("turned", "turn_kept", "projected", "res_ready", "stats_ready", "moments_ready", "dev_ready", "scale_ready", "y_ready"))
        block = ctx.enter_context(nc.Block())

        @block.sync
        def _(sp):
            sp.wait_ge(x_zeroed, 1)

            def step(k, u):
                s = 2 * k + u
                if not first(k):
                    sp.wait_ge(res_ready, s - 1)
                    sp.sem_inc(load_opened, 1)
                for p, rows, j in bucket_rows(x, s, end(k, u)):
                    sp.dma_start(x_rows[p, u, j, :], rows).then_inc(rows_in[u], 16)
                sp.dma_start(add[:, u, :, :],
                             bass.AP(merge_dram.tensor, s * (FB * BN * MW), [[MW, P], [BN * MW, FB], [1, MW]])
                             ).then_inc(rows_in[u], 16)

            in_pairs(sp, step, S)

        @block.tensor
        def _(pe):
            def step(k, u):
                s = 2 * k + u
                pe.wait_ge(mixed_ready, s + 1)
                if not start(k, u):
                    pe.wait_ge(turn_kept, s)
                for j in range(FB):
                    mm = pe.transpose(turn_ps[:, j, :], mixed[:, j, :], c["ident"][:])
                mm.then_inc(turned, 1)
                pe.wait_ge(turn_kept, s + 1)
                if not start(k, u):
                    pe.wait_ge(res_ready, s)
                for j in range(FB):
                    pe.matmul(out_ps[:, j, :], mixed_t[:, j, :], c["w_out"][:], start=True, stop=False)
                    mm = pe.matmul(out_ps[:, j, :], c["ones"][0:1, :], c["b_out"][:], start=False, stop=True)
                mm.then_inc(projected, 1)

            in_pairs(pe, step, S)

        @block.scalar
        def _(act):
            def step(k, u):
                s = 2 * k + u
                act.wait_ge(turned, s + 1)
                if not start(k, u):
                    act.wait_ge(projected, s)
                act.copy(mixed_t[:], turn_ps[:, 0:FB, :]).then_inc(turn_kept, 1)
                act.wait_ge(moments_ready, FB * (s + 1))
                act.activation(dev[:], moments[:, :, 1], ACT.Sqrt, bias=eps[:, 0:1]).then_inc(dev_ready, 1)
                act.wait_ge(y_ready, s + 1)
                for p, rows, j in bucket_rows(out, s, end(k, u)):
                    act.dma_start(rows, y[p, u, j, :]).then_inc(y_out[u], 16)

            in_pairs(act, step, S)
            act.wait_ge(y_out[0], 16 * S)
            act.wait_ge(y_out[1], 16 * S + 16)

        @block.vector
        def _(dve):
            by_head = lambda ap: ap.rearrange("p j (d h) -> p j d h", h=H)

            def step(k, u):
                s = 2 * k + u
                dve.wait_ge(rows_in[u], 48 * (k + 1) + (16 if end(k, u) else 0))
                dve.tensor_scalar(factor[:], add[:, u, :, 0:H], 1.0, None, ALU.add).then_inc(factor_ready, 1)
                dve.wait_ge(factor_ready, s + 1)
                dve.tensor_tensor(by_head(both[:]), by_head(acc[:, ds(s * FB, FB), :]), bcast(factor[:], 2, W // H),
                                  ALU.mult).then_inc(scaled, 1)
                dve.wait_ge(scaled, s + 1)
                dve.tensor_tensor(both[:], both[:], add[:, u, :, H:], ALU.add).then_inc(both_ready, 1)
                dve.wait_ge(both_ready, s + 1)
                dve.tensor_scalar(share[:], both[:, :, 0:H], 1e-10, None, ALU.add).then_inc(share_ready, 1)
                dve.wait_ge(share_ready, s + 1)
                dve.reciprocal(share[:], share[:]).then_inc(inverse_ready, 1)
                dve.wait_ge(inverse_ready, s + 1)
                if not start(k, u):
                    dve.wait_ge(turned, s)
                dve.tensor_tensor(by_head(mixed[:]), by_head(both[:, :, H:]), bcast(share[:], 2, DH), ALU.mult
                                  ).then_inc(mixed_ready, 1)
                dve.wait_ge(projected, s + 1)
                dve.tensor_tensor(res[:], out_ps[:, 0:FB, :], x_rows[:, u], ALU.add).then_inc(res_ready, 1)
                dve.wait_ge(res_ready, s + 1)
                for j in range(FB):
                    dve.bn_stats(stats[:, j, :], res[:, j, :]).then_inc(stats_ready, 1)
                if not start(k, u):
                    dve.wait_ge(dev_ready, s)
                dve.wait_ge(stats_ready, FB * s + FB)
                dve.sem_inc(stats_opened, 1)
                for j in range(FB):
                    dve.bn_aggr(moments[:, j, :], stats[:, j, :]).then_inc(moments_ready, 1)
                dve.wait_ge(dev_ready, s + 1)
                dve.reciprocal(scale[:], dev[:]).then_inc(scale_ready, 1)
                dve.wait_ge(scale_ready, s + 1)
                if not first(k):
                    dve.wait_ge(y_out[u], 32 * k)
                for j in range(FB):
                    ins = dve.tensor_scalar(y[:, u, j, :], res[:, j, :], moments[:, j, 0:1], scale[:, j:j + 1],
                                            ALU.subtract, ALU.mult)
                ins.then_inc(y_ready, 1)

            dve.memset(eps[:], EPS)
            dve.memset(x_rows[:], 0.0).then_inc(x_zeroed, 1)
            in_pairs(dve, step, S)


_INS = ["x", "src", "dst", "edge_attr_128"] + [f"L0_gnn_{m}_{p}" for m in ("q", "k", "v", "out", "eb") for p in "wb"]


def kernel(**inputs):
    import numpy as np
    import concourse.bacc as bacc
    from concourse.bass_utils import run_bass_kernel_spmd

    nc = bacc.Bacc("TRN2", target_bir_lowering=False, num_devices=1)
    arrays = {f"in_{name}": np.ascontiguousarray(inputs[name]) for name in _INS}
    args = [nc.dram_tensor(name, a.shape, mybir.dt.from_np(a.dtype), kind="ExternalInput").ap() for name, a in arrays.items()]
    out = nc.dram_tensor("out", (N, D), F32, kind="ExternalOutput").ap()
    build(nc, *args, out)
    return run_bass_kernel_spmd(nc, [arrays], core_ids=[0]).results[0]["out"]
```

```python
from contextlib import ExitStack

import concourse.bass as bass
import concourse.mybir as mybir

P = 128
F32, BF16, I32 = mybir.dt.float32, mybir.dt.bfloat16, mybir.dt.int32
ALU = mybir.AluOpType
ACT = mybir.ActivationFunctionType
AX = mybir.AxisListType
ds = bass.ds

N, D = 6250, 128
E = 106250
H = 8
DH = D // H
EPS = 1e-5
BN = P - 1
B = -(-N // BN)
BC = B + 2
G = 8
EC = E // P
REST = E - EC * P
SI = -(-(EC + 1) // (2 * G)) * 2
CI = SI * G
T = -(-((E + B * (P - 1)) // P) // (2 * G)) * (2 * G)
ST = T // G
ROWS = T * P + G * P
RW = 16
W = H + D
MT = -(-T // P)
MW = H + W
TRASH = B * P + P
BIG = 1.0e30
GH = G * H
FB = 5
assert B % (2 * FB) == 0 and 2 * P * (CI - EC) < ROWS - T * P and SI * G >= EC + 1


def bcast(ap, dim, count):
    shape = list(ap.shape)
    return ap.unsqueeze(dim).broadcast_to(shape[:dim] + [count] + shape[dim:])


def build(nc, x, src, dst, edge, q_w, q_b, k_w, k_b, v_w, v_b, out_w, out_b, eb_w, eb_b, out):
    kv_dram = nc.dram_tensor("kv_rows", [N, 2 * D], F32, kind="Internal").ap()
    rec_dram = nc.dram_tensor("sorted_records", [ROWS, RW], I32, kind="Internal").ap()
    piece_dram = nc.dram_tensor("pieces", [T, W], F32, kind="Internal").ap()
    ends_dram = nc.dram_tensor("segment_ends", [T, H, 4], F32, kind="Internal").ap()
    merge_dram = nc.dram_tensor("merge_rows", [TRASH + MT * P, MW], F32, kind="Internal").ap()

    with ExitStack() as keep:
        sb = lambda name, shape, dt: keep.enter_context(nc.sbuf_tensor(name, shape, dt))
        c = {
            "ident": sb("ident", [P, P], F32), "identb": sb("identb", [P, P], BF16),
            "iota": sb("iota", [P, P], F32), "iota_g": sb("iota_g", [P, P, G], BF16),
            "rown": sb("rown", [P, 1], F32), "ones": sb("ones", [P, P], F32),
            "below": sb("below", [P, P], BF16), "belowf": sb("belowf", [P, P], F32),
            "shift": sb("shift", [G * H, G * H], F32), "wrap": sb("wrap", [G * H, G * H], F32),
            "w_kvq": sb("w_kvq", [P, 3 * D], F32), "b_kvq": sb("b_kvq", [1, 3 * D], F32),
            "w_out": sb("w_out", [P, D], F32), "b_out": sb("b_out", [1, D], F32),
            "w_eb": sb("w_eb", [P, G, G * H], F32), "b_eb": sb("b_eb", [1, G * H], F32),
            "bucket_of": sb("bucket_of", [1, T], I32),
        }
        acc = sb("acc", [P, 2, B, W], F32)
        with ExitStack() as queries:
            q3 = queries.enter_context(nc.sbuf_tensor("q3", [P, B, 3, D], BF16))
            with ExitStack() as ranks:
                rsb = lambda name, shape, dt: ranks.enter_context(nc.sbuf_tensor(name, shape, dt))
                r = {
                    "meta": rsb("meta", [P, CI, 3], I32),
                    "lo": rsb("lo", [P, CI], BF16), "hi": rsb("hi", [P, CI], BF16),
                    "start_a": rsb("start_a", [P, BC], BF16), "start_r": rsb("start_r", [P, BC], BF16),
                }
                constants(nc, c, x, q_w, q_b, k_w, k_b, v_w, v_b, out_w, out_b, eb_w, eb_b)
                fill(nc, rec_dram, merge_dram)
                project(nc, c, q3, x, kv_dram)
                count(nc, c, r, src, dst)
                rank(nc, c, r, edge, rec_dram)
            attend(nc, c, q3, acc, kv_dram, rec_dram, piece_dram, ends_dram)
        merge(nc, c, piece_dram, ends_dram, merge_dram)
        finish(nc, c, acc, x, merge_dram, out)


def allocators(nc, ctx, stage):
    return (lambda name, shape, dt: ctx.enter_context(nc.sbuf_tensor(f"{stage}_{name}", shape, dt)),
            lambda name, shape, dt: ctx.enter_context(nc.psum_tensor(f"{stage}_{name}", shape, dt)),
            lambda name: ctx.enter_context(nc.semaphore(f"{stage}_{name}")))


def constants(nc, c, x, q_w, q_b, k_w, k_b, v_w, v_b, out_w, out_b, eb_w, eb_b):
    with ExitStack() as ctx:
        sb, psum, sem = allocators(nc, ctx, "constants")
        w_raw = sb("w_raw", [P, 5, D], F32)
        b_raw = sb("b_raw", [1, 3 * D + H], F32)
        w_ps = psum("w_ps", [P, 8, P], F32)
        w_in = sem("w_in")
        filled = sem("filled")
        const_done = sem("const_done")
        w_turned = sem("w_turned")
        w_eb_zeroed = sem("w_eb_zeroed")
        block = ctx.enter_context(nc.Block())
        @block.sync
        def _(sp):
            for k, w in enumerate((k_w, v_w, q_w, out_w)):
                sp.dma_start(w_raw[:, k, :], w).then_inc(w_in, 16)
            sp.dma_start(w_raw[0:H, 4, :], eb_w).then_inc(w_in, 16)
            sp.dma_start(b_raw[0:1, 0:D], k_b.rearrange("(a n) -> a n", a=1)).then_inc(w_in, 16)
            sp.dma_start(b_raw[0:1, D:2 * D], v_b.rearrange("(a n) -> a n", a=1)).then_inc(w_in, 16)
            sp.dma_start(b_raw[0:1, 2 * D:3 * D], q_b.rearrange("(a n) -> a n", a=1)).then_inc(w_in, 16)
            sp.dma_start(c["b_out"][:], out_b.rearrange("(a n) -> a n", a=1)).then_inc(w_in, 16)
            sp.dma_start(b_raw[0:1, 3 * D:], eb_b.rearrange("(a n) -> a n", a=1)).then_inc(w_in, 16)
            sp.wait_ge(w_in, 16 * 10)

        @block.gpsimd
        def _(pool):
            pool.memset(c["ident"][:], 0.0).then_inc(filled, 1)
            pool.memset(c["ones"][:], 1.0).then_inc(filled, 1)
            pool.memset(c["shift"][:], 0.0).then_inc(filled, 1)
            pool.memset(c["wrap"][:], 0.0).then_inc(filled, 1)
            pool.iota(c["iota"][:], [[1, P]], base=0, channel_multiplier=0,
                      allow_small_or_imprecise_dtypes=True).then_inc(const_done, 1)
            pool.iota(c["iota_g"][:], [[1, P], [0, G]], base=0, channel_multiplier=0,
                      allow_small_or_imprecise_dtypes=True).then_inc(const_done, 1)
            pool.iota(c["rown"][:], [[0, 1]], base=0, channel_multiplier=1,
                      allow_small_or_imprecise_dtypes=True).then_inc(const_done, 1)
            pool.wait_ge(filled, 4)
            pool.affine_select(out=c["ident"][:], in_=c["ident"][:], compare_op=ALU.not_equal, fill=1.0,
                               base=0, pattern=[[-1, P]], channel_multiplier=1).then_inc(const_done, 1)
            pool.affine_select(out=c["belowf"][:], in_=c["ones"][:], compare_op=ALU.is_ge, fill=0.0,
                               base=-1, pattern=[[1, P]], channel_multiplier=-1).then_inc(const_done, 1)
            pool.affine_select(out=c["shift"][:], in_=c["shift"][:], compare_op=ALU.not_equal, fill=1.0,
                               base=H, pattern=[[-1, G * H]], channel_multiplier=1).then_inc(const_done, 1)
            pool.affine_select(out=c["wrap"][:], in_=c["wrap"][:], compare_op=ALU.not_equal, fill=1.0,
                               base=H - G * H, pattern=[[-1, G * H]], channel_multiplier=1).then_inc(const_done, 1)

        @block.tensor
        def _(pe):
            pe.wait_ge(w_in, 16 * 10)
            pe.wait_ge(const_done, 7)
            for k in range(4):
                pe.transpose(w_ps[:, k, :], w_raw[:, k, :], c["ident"][:])
            pe.transpose(w_ps[:, 4, 0:H], w_raw[0:H, 4, :], c["ident"][0:H, 0:H]).then_inc(w_turned, 1)

        @block.vector
        def _(dve):
            dve.wait_ge(const_done, 7)
            dve.tensor_copy(c["identb"][:], c["ident"][:])
            dve.tensor_copy(c["below"][:], c["belowf"][:])
            dve.memset(c["w_eb"][:], 0.0).then_inc(w_eb_zeroed, 1)
            dve.wait_ge(w_in, 16 * 10)
            heads_in = lambda ap: ap.rearrange("p (h d) -> p d h", h=H)
            heads_out = lambda ap: ap.rearrange("p (d h) -> p d h", h=H)
            dve.tensor_copy(c["b_kvq"][:, 0:D], b_raw[:, 0:D])
            dve.tensor_copy(heads_out(c["b_kvq"][:, D:2 * D]), heads_in(b_raw[:, D:2 * D]))
            dve.tensor_copy(c["b_eb"][:].rearrange("a (t h) -> a t h", t=G), bcast(b_raw[:, 3 * D:], 1, G))
            dve.tensor_scalar(c["b_kvq"][:, 2 * D:], b_raw[:, 2 * D:3 * D], DH ** -0.5, None, ALU.mult)
            dve.wait_ge(w_turned, 1)
            dve.tensor_copy(c["w_kvq"][:, 0:D], w_ps[:, 0, :])
            dve.tensor_copy(heads_out(c["w_kvq"][:, D:2 * D]), heads_in(w_ps[:, 1, :]))
            dve.tensor_scalar(c["w_kvq"][:, 2 * D:], w_ps[:, 2, :], DH ** -0.5, None, ALU.mult)
            dve.wait_ge(w_eb_zeroed, 1)
            for t in range(G):
                dve.tensor_copy(c["w_eb"][:, t, t * H:(t + 1) * H], w_ps[:, 4, 0:H])

    with ExitStack() as ctx:
        sb, psum, sem = allocators(nc, ctx, "constants2")
        w_perm = sb("w_perm", [P, D], F32)
        w_rows = sb("w_rows", [P, D], F32)
        wo_ps = psum("wo_ps", [P, D], F32)
        wo_in = sem("wo_in")
        wo_perm = sem("wo_perm")
        wo_turned = sem("wo_turned")
        block = ctx.enter_context(nc.Block())
        @block.sync
        def _(sp):
            sp.dma_start(w_rows[:], out_w).then_inc(wo_in, 16)

        @block.vector
        def _(dve):
            dve.wait_ge(wo_in, 16)
            dve.tensor_copy(w_perm[:].rearrange("p (d h) -> p d h", h=H),
                            w_rows[:].rearrange("p (h d) -> p d h", h=H)).then_inc(wo_perm, 1)
            dve.wait_ge(wo_turned, 1)
            dve.tensor_copy(c["w_out"][:], wo_ps[:])

        @block.tensor
        def _(pe):
            pe.wait_ge(wo_perm, 1)
            pe.transpose(wo_ps[:], w_perm[:], c["ident"][:]).then_inc(wo_turned, 1)


def fill(nc, rec_dram, merge_dram):
    per = ROWS // P // G
    mper = B * P // P // 2
    assert ROWS == P * per * G and B % 2 == 0
    with ExitStack() as ctx:
        sb, psum, sem = allocators(nc, ctx, "fill")
        blank = sb("blank", [P, per, RW], I32)
        zero = sb("zero", [P, mper, MW], F32)
        zeroed = sem("zeroed")
        blank_ready = sem("blank_ready")
        blanks_out = sem("blanks_out")
        zeros_out = sem("zeros_out")
        block = ctx.enter_context(nc.Block())
        @block.vector
        def _(dve):
            dve.memset(blank[:], 0).then_inc(zeroed, 1)
            dve.wait_ge(zeroed, 1)
            dve.memset(blank[:, :, H], -1).then_inc(blank_ready, 1)
            dve.memset(blank[:, :, H + 1], 200).then_inc(blank_ready, 1)
            dve.memset(zero[:], 0.0).then_inc(blank_ready, 1)

        @block.sync
        def _(sp):
            sp.wait_ge(blank_ready, 3)
            for k in range(G):
                sp.dma_start(rec_dram[k * P * per:(k + 1) * P * per, :].rearrange("(p r) w -> p r w", p=P),
                             blank[:]).then_inc(blanks_out, 16)
            for k in range(2):
                sp.dma_start(merge_dram[k * P * mper:(k + 1) * P * mper, :].rearrange("(p r) w -> p r w", p=P),
                             zero[:]).then_inc(zeros_out, 16)
            sp.wait_ge(blanks_out, 16 * G)
            sp.wait_ge(zeros_out, 32)


def bucket_rows(dram, k, tail):
    whole = FB - 1 if tail else FB
    by_row = dram[ds(k * (FB * BN), whole * BN), :].rearrange("(j p) d -> p j d", p=BN)
    parts = [(slice(1, 65), by_row[0:64], slice(0, whole)), (slice(65, P), by_row[64:BN], slice(0, whole))]
    if tail:
        at = (B - 1) * BN
        parts.append((slice(1, 1 + N - at), dram[at:N, :].rearrange("(j p) d -> p j d", j=1), slice(FB - 1, FB)))
    return parts


def in_pairs(eng, step, steps, head=1):
    for k in range(head):
        step(k, 0)
        step(k, 1)
    with eng.Fori(head, steps // 2 - 1) as k:
        step(k, 0)
        step(k, 1)
    step(steps // 2 - 1, 0)
    step(steps // 2 - 1, 1)


def project(nc, c, q3, x, kv_dram):
    S = B // FB
    first = lambda k: isinstance(k, int) and k == 0
    end = lambda k, u: isinstance(k, int) and k == S // 2 - 1 and u == 1
    with ExitStack() as ctx:
        sb, psum, sem = allocators(nc, ctx, "project")
        x_rows = sb("x_rows", [P, 2, FB, D], F32)
        x_t = sb("x_t", [P, FB, P], F32)
        kv_out = sb("kv_out", [P, 2, FB, 2 * D], F32)
        q_left = sb("q_left", [P, FB, D], F32)
        turn_ps = psum("turn_ps", [P, 8, P], F32)
        kv_ps = psum("kv_ps", [P, 6, 2 * D], F32)
        q_ps = psum("q_ps", [P, 8, D], F32)
        x_in = [sem(f"x_in{u}") for u in range(2)]
        kv_stored = [sem(f"kv_stored{u}") for u in range(2)]
        x_zeroed, x_turned, x_kept, kv_ready, q_ready, kv_kept, q_part0, q_rest, q_part1, q_part2 = map(
            sem, ("x_zeroed", "x_turned", "x_kept", "kv_ready", "q_ready", "kv_kept", "q_part0", "q_rest", "q_part1", "q_part2"))
        block = ctx.enter_context(nc.Block())
        @block.sync
        def _(sp):
            sp.wait_ge(x_zeroed, 1)

            def step(k, u):
                if not first(k):
                    sp.wait_ge(x_turned, 2 * k + u - 1)
                for p, rows, j in bucket_rows(x, 2 * k + u, end(k, u)):
                    sp.dma_start(x_rows[p, u, j, :], rows).then_inc(x_in[u], 16)

            in_pairs(sp, step, S)

        @block.tensor
        def _(pe):
            def step(k, u):
                s = 2 * k + u
                pe.wait_ge(x_in[u], 32 * (k + 1) + (16 if end(k, u) else 0))
                if not (first(k) and u == 0):
                    pe.wait_ge(x_kept, s)
                for j in range(FB):
                    mm = pe.transpose(turn_ps[:, j, :], x_rows[:, u, j, :], c["ident"][:])
                mm.then_inc(x_turned, 1)
                pe.wait_ge(x_kept, s + 1)
                if not (first(k) and u == 0):
                    pe.wait_ge(q_rest, s)
                for j in range(FB):
                    pe.matmul(q_ps[:, j, :], x_t[:, j, :], c["w_kvq"][:, 2 * D:], start=True, stop=False)
                    mm = pe.matmul(q_ps[:, j, :], c["ones"][0:1, :], c["b_kvq"][:, 2 * D:], start=False, stop=True)
                mm.then_inc(q_ready, 1)
                if not (first(k) and u == 0):
                    pe.wait_ge(kv_kept, s)
                for j in range(FB):
                    pe.matmul(kv_ps[:, j, :], x_t[:, j, :], c["w_kvq"][:, 0:2 * D], start=True, stop=False)
                    mm = pe.matmul(kv_ps[:, j, :], c["ones"][0:1, :], c["b_kvq"][:, 0:2 * D], start=False, stop=True)
                mm.then_inc(kv_ready, 1)

            in_pairs(pe, step, S)

        @block.scalar
        def _(act):
            def step(k, u):
                s = 2 * k + u
                act.wait_ge(x_turned, s + 1)
                if not (first(k) and u == 0):
                    act.wait_ge(kv_ready, s)
                act.copy(x_t[:], turn_ps[:, 0:FB, :]).then_inc(x_kept, 1)
                act.wait_ge(q_ready, s + 1)
                act.copy(q3[:, ds(s * FB, FB), 0, :], q_ps[:, 0:FB, :]).then_inc(q_part0, 1)
                act.wait_ge(kv_ready, s + 1)
                if not first(k):
                    act.wait_ge(kv_stored[u], k * 32)
                act.copy(kv_out[:, u], kv_ps[:, 0:FB, :]).then_inc(kv_kept, 1)
                act.wait_ge(kv_kept, s + 1)
                for p, rows, j in bucket_rows(kv_dram, s, end(k, u)):
                    act.dma_start(rows, kv_out[p, u, j, :]).then_inc(kv_stored[u], 16)

            in_pairs(act, step, S)
            act.wait_ge(kv_stored[0], 16 * S)
            act.wait_ge(kv_stored[1], 16 * S + 16)

        @block.vector
        def _(dve):
            def step(k, u):
                s = 2 * k + u
                part = lambda m: q3[:, ds(s * FB, FB), m, :]
                dve.wait_ge(q_part0, s + 1)
                if not (first(k) and u == 0):
                    dve.wait_ge(q_part2, s)
                dve.tensor_tensor(q_left[:], q_ps[:, 0:FB, :], part(0), ALU.subtract).then_inc(q_rest, 1)
                dve.wait_ge(q_rest, s + 1)
                dve.tensor_copy(part(1), q_left[:]).then_inc(q_part1, 1)
                dve.wait_ge(q_part1, s + 1)
                dve.tensor_tensor(part(2), q_left[:], part(1), ALU.subtract).then_inc(q_part2, 1)

            dve.memset(x_rows[:], 0.0).then_inc(x_zeroed, 1)
            in_pairs(dve, step, S)


def one_hots(dve, c, r, hot_lo, hot_hi, s, hot_ready):
    at = ds(s * G, G)
    dve.tensor_tensor(hot_lo, c["iota_g"][:], bcast(r["lo"][:, at], 1, P), ALU.is_equal)
    dve.tensor_tensor(hot_hi, c["iota_g"][:, 0:BC, :], bcast(r["hi"][:, at], 1, BC), ALU.is_equal).then_inc(hot_ready, 1)


def count(nc, c, r, src, dst):
    with ExitStack() as ctx:
        sb, psum, sem = allocators(nc, ctx, "count")
        src_c = sb("src_c", [P, CI], I32)
        dst_c = sb("dst_c", [P, CI], I32)
        srcf = sb("srcf", [P, CI], F32)
        hif = sb("hif", [P, CI], F32)
        hii = sb("hii", [P, CI], I32)
        off = sb("off", [P, CI], F32)
        low = sb("low", [P, CI], F32)
        hot_lo = sb("hot_lo", [P, 2, P, G], BF16)
        hot_hi = sb("hot_hi", [P, 2, BC, G], BF16)
        cnt = sb("cnt", [P, BC], F32)
        toti = sb("toti", [P, BC], I32)
        tiles = sb("tiles", [P, B], F32)
        last = sb("last", [P, B], F32)
        first = sb("first", [P, BC], F32)
        onesb = sb("onesb", [P, B], F32)
        lastc = sb("lastc", [P, 1], F32)
        iota_t = sb("iota_t", [P, T], F32)
        ended = sb("ended", [P, T], F32)
        zerob = sb("zerob", [P, P], BF16)
        cnt_ps = psum("cnt_ps", [P, 512], F32)
        tot_ps = psum("tot_ps", [P, 512], F32)
        turn_ps = psum("turn_ps", [P, 512], F32)
        bkt_ps = psum("bkt_ps", [P, 2, 512], F32)
        idx_in = sem("idx_in")
        blank_src = sem("blank_src")
        rest_in = sem("rest_in")
        split = sem("split")
        hot_ready = sem("hot_ready")
        hot_used = sem("hot_used")
        counted = sem("counted")
        step_done = sem("step_done")
        summed = sem("summed")
        aux = sem("aux")
        block = ctx.enter_context(nc.Block())
        half = T // 2

        @block.sync
        def _(sp):
            sp.dma_start(src_c[:, 0:EC], src[0:EC * P].rearrange("(p j) -> p j", p=P)).then_inc(idx_in, 16)
            sp.dma_start(dst_c[:, 0:EC], dst[0:EC * P].rearrange("(p j) -> p j", p=P)).then_inc(idx_in, 16)
            sp.wait_ge(blank_src, 2)
            sp.dma_start(src_c[0:REST, EC:EC + 1], src[EC * P:E].rearrange("(p j) -> p j", j=1)).then_inc(rest_in, 16)
            sp.dma_start(dst_c[0:REST, EC:EC + 1], dst[EC * P:E].rearrange("(p j) -> p j", j=1)).then_inc(rest_in, 16)

        @block.gpsimd
        def _(pool):
            pool.iota(src_c[:, EC:CI], [[0, CI - EC]], base=B * BN, channel_multiplier=1).then_inc(blank_src, 1)
            pool.memset(dst_c[:, EC:CI], 0).then_inc(blank_src, 1)
            pool.iota(iota_t[:], [[1, T]], base=0, channel_multiplier=0,
                      allow_small_or_imprecise_dtypes=True).then_inc(aux, 1)
            pool.memset(onesb[:], 1.0).then_inc(aux, 1)
            pool.memset(zerob[:], 0.0).then_inc(aux, 1)
            pool.iota(first[:, B:BC], [[P * (CI - EC), BC - B]], base=T * P, channel_multiplier=CI - EC,
                      allow_small_or_imprecise_dtypes=True).then_inc(aux, 1)

        @block.vector
        def _(dve):
            n = [0]

            def then(ins):
                n[0] += 1
                ins.then_inc(split, 1)
                dve.wait_ge(split, n[0])

            dve.wait_ge(idx_in, 32)
            dve.wait_ge(rest_in, 32)
            then(dve.tensor_copy(srcf[:], src_c[:]))
            then(dve.tensor_scalar(hii[:], srcf[:], 1.0 / BN, 0.5 / BN - 0.5, ALU.mult, ALU.add))
            then(dve.tensor_copy(hif[:], hii[:]))
            then(dve.scalar_tensor_tensor(off[:], hif[:], -float(BN), srcf[:], ALU.mult, ALU.add))
            dve.tensor_scalar(low[:], off[:], 0.0, None, ALU.is_lt)
            then(dve.tensor_scalar(off[:], off[:], float(BN), None, ALU.is_ge))
            then(dve.tensor_tensor(off[:], off[:], low[:], ALU.subtract))
            then(dve.tensor_tensor(hif[:], hif[:], off[:], ALU.add))
            dve.tensor_copy(r["hi"][:], hif[:])
            then(dve.scalar_tensor_tensor(low[:], hif[:], -float(BN), srcf[:], ALU.mult, ALU.add))
            then(dve.tensor_scalar(low[:], low[:], 1.0, None, ALU.add))
            dve.tensor_copy(r["lo"][:], low[:])
            dve.tensor_copy(r["meta"][:, :, 0], src_c[:])
            dve.tensor_copy(r["meta"][:, :, 1], low[:])
            then(dve.tensor_copy(r["meta"][:, :, 2], dst_c[:]))

            def hot(k, u):
                one_hots(dve, c, r, hot_lo[:, u], hot_hi[:, u], 2 * k + u, hot_ready)

            hot(0, 0)
            hot(0, 1)
            with dve.Fori(1, SI // 2) as k:
                for u in range(2):
                    dve.wait_ge(hot_used, 2 * k + u - 1)
                    hot(k, u)
            dve.wait_ge(counted, 1)
            then(dve.tensor_copy(cnt[:], cnt_ps[:, 0:BC]))
            dve.wait_ge(summed, 1)
            dve.wait_ge(aux, 4)
            then(dve.tensor_scalar(toti[:], tot_ps[:, 0:BC], float(P - 1), None, ALU.add))
            then(dve.tensor_scalar(toti[:], toti[:], 7, None, ALU.logical_shift_right))
            then(dve.tensor_copy(tiles[:], toti[:, 0:B]))
            then(dve.tensor_tensor_scan(last[:], onesb[:], tiles[:], 0.0, ALU.mult, ALU.add))
            then(dve.tensor_tensor(tiles[:], last[:], tiles[:], ALU.subtract))
            then(dve.scalar_tensor_tensor(first[:, 0:B], tiles[:], float(P), tot_ps[:, 256:256 + B], ALU.mult, ALU.add))
            then(dve.tensor_copy(r["start_a"][:], first[:]))
            then(dve.tensor_tensor(r["start_r"][:], first[:], r["start_a"][:], ALU.subtract))
            dve.wait_ge(summed, 2)
            then(dve.tensor_copy(lastc[0:B, :], turn_ps[0:B, 0:1]))
            then(dve.tensor_scalar(ended[0:B, :], iota_t[0:B, :], lastc[0:B, 0:1], None, ALU.is_ge))
            dve.sem_inc(step_done, 1)
            dve.wait_ge(summed, 3)
            then(dve.tensor_scalar(c["bucket_of"][:].rearrange("a (k t) -> a k t", k=2), bkt_ps[0:1, :, 0:half],
                                   float(B - 1), None, ALU.min))

        @block.tensor
        def _(pe):
            pe.wait_ge(aux, 4)
            pe.matmul(cnt_ps[:, 0:BC], zerob[:], zerob[:, 0:BC], start=True, stop=False)
            with pe.Fori(0, SI // 2) as k:
                for u in range(2):
                    pe.wait_ge(hot_ready, 2 * k + u + 1)
                    for t in range(G):
                        mm = pe.matmul(cnt_ps[:, 0:BC], hot_lo[:, u, :, t], hot_hi[:, u, :, t], start=False, stop=False)
                    mm.then_inc(hot_used, 1)
            pe.matmul(cnt_ps[:, 0:BC], zerob[:], zerob[:, 0:BC], start=False, stop=True).then_inc(counted, 1)
            pe.wait_ge(split, COUNT_COPIED)
            pe.matmul(tot_ps[:, 0:BC], c["ones"][:], cnt[:], start=True, stop=True)
            pe.matmul(tot_ps[:, 256:256 + BC], c["belowf"][:], cnt[:], start=True, stop=True).then_inc(summed, 1)
            pe.wait_ge(split, LAST_TILE)
            pe.transpose(turn_ps[0:B, 0:P], last[:], c["ident"][:]).then_inc(summed, 1)
            pe.wait_ge(step_done, 1)
            for k in range(2):
                mm = pe.matmul(bkt_ps[0:1, k, 0:half], c["ones"][0:B, 0:1], ended[0:B, k * half:(k + 1) * half],
                               start=True, stop=True)
            mm.then_inc(summed, 1)


COUNT_COPIED = 11
LAST_TILE = COUNT_COPIED + 4


def rank(nc, c, r, edge, rec_dram):
    with ExitStack() as ctx:
        sb, psum, sem = allocators(nc, ctx, "rank")
        edges = sb("edges", [P, 2, G, D], F32)
        edges_t = sb("edges_t", [P, 2, G // 2, P], F32)
        hot_lo = sb("hot_lo", [P, 2, P, G], BF16)
        hot_hi = sb("hot_hi", [P, 2, BC, G], BF16)
        hot_lo_t = sb("hot_lo_t", [P, 2, G, P], BF16)
        before = sb("before", [P, 2, G, P], BF16)
        next_a = sb("next_a", [P, 2, G + 1, BC], BF16)
        next_r = sb("next_r", [P, 2, G + 1, BC], BF16)
        bias_t = sb("bias_t", [GH, P], F32)
        picked = sb("picked", [P, G, BC], F32)
        slotf = sb("slotf", [P, G], F32)
        slot = sb("slot", [P, G], I32)
        within = sb("within", [P, G], I32)
        tile8 = sb("tile8", [P, G], I32)
        group = sb("group", [P, G], I32)
        row = sb("row", [P, 2, G], I32)
        record = sb("record", [P, 2, G, RW], I32)
        turn_ps = psum("turn_ps", [P, G, P], BF16)
        edge_ps = psum("edge_ps", [P, 2, 4, P], F32)
        next_ps = psum("next_ps", [P, 512], F32)
        same_ps = psum("same_ps", [P, 2, 4, P], F32)
        slot_ps = psum("slot_ps", [P, 512], F32)
        bias_ps = psum("bias_ps", [P, 512], F32)
        opened = sem("opened")
        edges_in = [sem(f"edges_in{u}") for u in range(2)]
        scattered = [sem(f"scattered{u}") for u in range(2)]
        bias_opened, bias_t_kept, bias_turned = map(sem, ("bias_opened", "bias_t_kept", "bias_turned"))
        edges_turned, edges_kept, bias_ready, bias_kept = map(sem, ("edges_turned", "edges_kept", "bias_ready", "bias_kept"))
        hot_ready, lo_turned, lo_kept, same_ready, before_ready = map(
            sem, ("hot_ready", "lo_turned", "lo_kept", "same_ready", "before_ready"))
        next_ready, next_a_kept, next_r_kept, slots_ready = map(
            sem, ("next_ready", "next_a_kept", "next_r_kept", "slots_ready"))
        picked_ready, slotf_ready, slot_ready, bits_ready, joined, rows_ready, meta_kept, table_ready = map(
            sem, ("picked_ready", "slotf_ready", "slot_ready", "bits_ready", "joined", "rows_ready", "meta_kept", "table_ready"))
        block = ctx.enter_context(nc.Block())
        LAST = SI - 1
        tail = EC - LAST * G
        assert 0 < tail < G

        first = lambda k: isinstance(k, int) and k == 0
        end = lambda k, u: isinstance(k, int) and k == SI // 2 - 1 and u == 1

        @block.sync
        def _(sp):
            by_col = edge[0:EC * P, :].rearrange("(p j) d -> p j d", p=P)

            def step(k, u):
                if not first(k):
                    sp.wait_ge(edges_turned, 2 * (2 * (k - 1) + u) + 2)
                if end(k, u):
                    sp.dma_start(edges[:, u, 0:tail, :], by_col[:, LAST * G:EC, :]).then_inc(edges_in[u], 16)
                    sp.dma_start(edges[0:REST, u, tail, :], edge[EC * P:E, :]).then_inc(edges_in[u], 16)
                else:
                    sp.dma_start(edges[:, u, :, :], by_col[:, ds((2 * k + u) * G, G), :]).then_inc(edges_in[u], 16)

            in_pairs(sp, step, SI)

        @block.gpsimd
        def _(pool):
            def step(k, u):
                s = 2 * k + u
                pool.wait_ge(rows_ready, s + 1)
                pool.wait_ge(meta_kept, s + 1)
                pool.wait_ge(bias_kept, s + 1)
                pool.sem_inc(opened, 1)
                for t in range(G):
                    pool.indirect_dma_start(rec_dram[:, :], bass.IndirectOffsetOnAxis(ap=row[:, u, t:t + 1], axis=0),
                                            record[:, u, t, :], None).then_inc(scattered[u], 16)

            in_pairs(pool, step, SI)
            for u in range(2):
                pool.wait_ge(scattered[u], 16 * G * (SI // 2))

        @block.tensor
        def _(pe):
            def turn_lo(s, u):
                pe.wait_ge(hot_ready, s + 1)
                if not (isinstance(s, int) and s == 0):
                    pe.wait_ge(lo_kept, s)
                for t in range(G):
                    mm = pe.transpose(turn_ps[:, t, :], hot_lo[:, u, :, t], c["identb"][:])
                mm.then_inc(lo_turned, 1)

            def step(k, u):
                s = 2 * k + u
                if first(k) and u == 0:
                    pe.wait_ge(table_ready, 2)
                else:
                    pe.wait_ge(next_r_kept, s)
                base = lambda part: bcast(part[:, 1 - u, G, :], 1, G + 1)
                table = next_ps[:, 0:(G + 1) * BC].rearrange("p (t b) -> p t b", t=G + 1)
                pe.matmul(table, c["identb"][:], base(next_a), start=True, stop=False)
                pe.matmul(table, c["identb"][:], base(next_r), start=False, stop=False)
                for t in range(G):
                    mm = pe.matmul(table[:, t + 1:, :], hot_lo[:, u, :, t], bcast(hot_hi[:, u, :, t], 1, G - t),
                                   start=False, stop=(t == G - 1))
                mm.then_inc(next_ready, 1)
                pe.wait_ge(lo_kept, s + 1)
                for q in range(2):
                    if not (first(k) and u == 0):
                        pe.wait_ge(before_ready, 2 * s - 1 + q)
                    for t in range(4):
                        mm = pe.matmul(same_ps[:, q, t, :], hot_lo_t[:, u, 4 * q + t, :], hot_lo_t[:, u, 4 * q + t, :],
                                       start=True, stop=True)
                    mm.then_inc(same_ready, 1)
                pe.wait_ge(edges_in[u], 16 * (k + 1) + (16 if end(k, u) else 0))
                for q in range(2):
                    if not (first(k) and u == 0):
                        pe.wait_ge(edges_kept, 2 * s - 1 + q)
                    for t in range(4):
                        mm = pe.transpose(edge_ps[:, q, t, :], edges[:, u, 4 * q + t, :], c["ident"][:])
                    mm.then_inc(edges_turned, 1)
                if not end(k, u):
                    turn_lo(s + 1, 1 - u)
                if not (first(k) and u == 0):
                    pe.wait_ge(bias_kept, s)
                pe.sem_inc(bias_opened, 1)
                o = bias_ps[0:GH, 0:P]
                pe.matmul(o, c["b_eb"][:], c["ones"][0:1, :], start=True, stop=False)
                for t in range(G):
                    if t % 4 == 0:
                        pe.wait_ge(edges_kept, 2 * s + t // 4 + 1)
                        pe.sem_inc(bias_opened, 1)
                    mm = pe.matmul(o, c["w_eb"][:, t, :], edges_t[:, t // 4, t % 4, :], start=False, stop=(t == G - 1))
                mm.then_inc(bias_ready, 1)
                pe.wait_ge(next_r_kept, s + 1)
                if not (first(k) and u == 0):
                    pe.wait_ge(picked_ready, s)
                for t in range(G):
                    if t % 4 == 0:
                        pe.wait_ge(before_ready, 2 * s + t // 4 + 1)
                    o = slot_ps[:, t * BC:(t + 1) * BC]
                    pe.matmul(o, hot_lo_t[:, u, t, :], next_a[:, u, t, :], start=True, stop=False)
                    pe.matmul(o, hot_lo_t[:, u, t, :], next_r[:, u, t, :], start=False, stop=False)
                    mm = pe.matmul(o, before[:, u, t, :], hot_hi[:, u, :, t], start=False, stop=True)
                mm.then_inc(slots_ready, 1)
                pe.wait_ge(bias_t_kept, s + 1)
                pe.sem_inc(bias_opened, 1)
                pe.transpose(bias_ps[:, 192:192 + GH], bias_t[:], c["ident"][0:GH, 0:GH]).then_inc(bias_turned, 1)

            turn_lo(0, 0)
            in_pairs(pe, step, SI)

        @block.scalar
        def _(act):
            def keep_lo(s, u):
                act.wait_ge(lo_turned, s + 1)
                act.copy(hot_lo_t[:, u], turn_ps[:]).then_inc(lo_kept, 1)

            def step(k, u):
                s = 2 * k + u
                act.wait_ge(next_ready, s + 1)
                if not first(k):
                    act.wait_ge(slots_ready, s - 1)
                act.copy(next_a[:, u].rearrange("p t b -> p (t b)"), next_ps[:, 0:(G + 1) * BC]).then_inc(next_a_kept, 1)
                for q in range(2):
                    act.wait_ge(edges_turned, 2 * s + q + 1)
                    if not (first(k) and u == 0):
                        act.wait_ge(bias_ready, s)
                    act.copy(edges_t[:, q], edge_ps[:, q]).then_inc(edges_kept, 1)
                act.wait_ge(bias_ready, s + 1)
                if not (first(k) and u == 0):
                    act.wait_ge(bias_turned, s)
                act.copy(bias_t[:], bias_ps[0:GH, 0:P]).then_inc(bias_t_kept, 1)
                if not end(k, u):
                    if not (first(k) and u == 0):
                        act.wait_ge(slots_ready, s)
                    keep_lo(s + 1, 1 - u)
                act.wait_ge(bias_turned, s + 1)
                if not first(k):
                    act.wait_ge(scattered[u], 16 * G * k)
                act.copy(record[:, u, :, 0:H].bitcast(F32), bias_ps[:, 192:192 + GH].rearrange("p (t h) -> p t h", t=G)
                         ).then_inc(bias_kept, 1)

            act.wait_ge(table_ready, 1)
            keep_lo(0, 0)
            in_pairs(act, step, SI)

        @block.vector
        def _(dve):
            def front(k, u):
                s = 2 * k + u
                for q in range(2):
                    dve.wait_ge(same_ready, 2 * s + q + 1)
                    dve.tensor_tensor(before[:, u, 4 * q:4 * q + 4, :], same_ps[:, q], bcast(c["below"][:], 1, 4),
                                      ALU.mult).then_inc(before_ready, 1)
                dve.wait_ge(next_a_kept, s + 1)
                dve.tensor_tensor(next_r[:, u].rearrange("p t b -> p (t b)"), next_ps[:, 0:(G + 1) * BC],
                                  next_a[:, u].rearrange("p t b -> p (t b)"), ALU.subtract).then_inc(next_r_kept, 1)

            def back(k, s, u, hots):
                dve.wait_ge(slots_ready, s + 1)
                dve.tensor_tensor(picked[:], slot_ps[:, 0:G * BC].rearrange("p (t b) -> p t b", t=G),
                                  hot_hi[:, u].rearrange("p b t -> p t b"), ALU.mult).then_inc(picked_ready, 1)
                dve.wait_ge(picked_ready, s + 1)
                dve.tensor_reduce(slotf[:], picked[:], AX.X, ALU.add).then_inc(slotf_ready, 1)
                if not (isinstance(k, int) and k == 0):
                    dve.wait_ge(scattered[u], 16 * G * k)
                dve.tensor_copy(record[:, u, :, H:H + 3], r["meta"][:, ds(s * G, G), :]).then_inc(meta_kept, 1)
                dve.wait_ge(slotf_ready, s + 1)
                dve.tensor_copy(slot[:], slotf[:]).then_inc(slot_ready, 1)
                if hots:
                    one_hots(dve, c, r, hot_lo[:, u], hot_hi[:, u], s + 2, hot_ready)
                dve.wait_ge(slot_ready, s + 1)
                dve.tensor_scalar(within[:], slot[:], P - 1, 3, ALU.bitwise_and, ALU.logical_shift_left)
                dve.tensor_scalar(tile8[:], slot[:], 7, G - 1, ALU.logical_shift_right, ALU.bitwise_and)
                dve.tensor_scalar(group[:], slot[:], 10, 10, ALU.logical_shift_right, ALU.logical_shift_left
                                  ).then_inc(bits_ready, 1)
                dve.wait_ge(bits_ready, s + 1)
                dve.tensor_tensor(within[:], within[:], tile8[:], ALU.bitwise_or).then_inc(joined, 1)
                dve.wait_ge(joined, s + 1)
                dve.tensor_tensor(row[:, u, :], within[:], group[:], ALU.bitwise_or).then_inc(rows_ready, 1)

            def step(k, u):
                s = 2 * k + u
                if not (first(k) and u == 0):
                    back(k - 1 if u == 0 else k, s - 1, 1 - u, not end(k, u))
                front(k, u)

            for s in range(2):
                one_hots(dve, c, r, hot_lo[:, s], hot_hi[:, s], s, hot_ready)
            dve.memset(record[:], 0).then_inc(table_ready, 1)
            dve.tensor_copy(next_a[:, 1, G, :], r["start_a"][:])
            dve.tensor_copy(next_r[:, 1, G, :], r["start_r"][:]).then_inc(table_ready, 1)
            in_pairs(dve, step, SI, head=2)
            back(SI // 2 - 1, SI - 1, 1, False)


def buckets(nc, c, engine, s, lo, hi):
    _, values = nc.values_load_multi_w_load_instructions(
        c["bucket_of"][0:1, ds(s * G + lo, hi - lo)], engines=[engine], min_val=0, max_val=B - 1,
        skip_runtime_bounds_check_because="count() bounds them by a min with B - 1")
    return values


def in_fours(eng, step, steps):
    whole = (steps - 4) // 4
    for k in range(2):
        for v in range(4):
            step(k, v)
    with eng.Fori(2, whole) as k:
        for v in range(4):
            step(k, v)
    for s in range(4 * whole, steps):
        step(s // 4, s % 4)


def attend(nc, c, q3, acc, kv_dram, rec_dram, piece_dram, ends_dram):
    ahead = lambda k, v: (k, v + 1) if v < 3 else (k + 1, 0)
    behind = lambda k, v: (k, v - 1) if v > 0 else (k - 1, 3)
    fixed = lambda k: isinstance(k, int)
    start = lambda k, v: fixed(k) and 4 * k + v == 0
    early = lambda k, v: fixed(k) and 4 * k + v < 2
    last = lambda k, v: fixed(k) and 4 * k + v == ST - 1
    used = lambda k, v: 2 * k + v // 2
    banks = [range(0, 3), range(3, 6), range(6, G)]
    NB = len(banks)
    with ExitStack() as ctx:
        sb, psum, sem = allocators(nc, ctx, "attend")
        rec = sb("rec", [P, 4, G, RW], I32)
        kv = sb("kv", [P, 4, G, 2 * D], F32)
        keyf = sb("keyf", [P, 2, G, H], F32)
        row_b = sb("row_b", [P, 2, G], BF16)
        key_t = sb("key_t", [GH, 2, P], F32)
        reset = sb("reset", [GH, 2, P + 1], F32)
        begun = sb("begun", [GH, 1], F32)
        carried = sb("carried", [GH, P], F32)
        keep = sb("keep", [P, G], F32)
        row_k = sb("row_k", [P, G], BF16)
        off2 = sb("off2", [P, 2, 4, P], BF16)
        hot_t = sb("hot_t", [P, 2, G, P], BF16)
        hot_b = sb("hot_b", [P, P, G], BF16)
        hot = sb("hot", [P, 2, G, P], F32)
        prod = sb("prod", [P, 2, 4, D], F32)
        score = sb("score", [P, 2, G, H], F32)
        run_max = sb("run_max", [GH, P], F32)
        seg_max = sb("seg_max", [GH, 2, P], F32)
        wv = sb("wv", [P, 2, G, W], F32)
        piece = sb("piece", [1, 2, G, W], F32)
        ends = sb("ends", [GH, 2, 4], F32)
        neg_row = sb("neg_row", [P, 1], F32)
        key_ps = psum("key_ps", [P, 512], F32)
        seg_ps = psum("seg_ps", [P, 512], F32)
        lo_ps = psum("lo_ps", [P, 4, P], F32)
        q_ps = psum("q_ps", [P, 2, 4, P], F32)
        sum_ps = psum("sum_ps", [P, NB, 512], F32)
        opened, turns_opened, load_opened = map(sem, ("opened", "turns_opened", "load_opened"))
        rec_in = [sem(f"rec_in{v}") for v in range(4)]
        kv_in = [sem(f"kv_in{v}") for v in range(4)]
        ends_out = [sem(f"ends_out{u}") for u in range(2)]
        pieces_out = [sem(f"pieces_out{u}") for u in range(2)]
        cleared, keys_ready, keys_turned, keys_kept, same_ready, reset_ready, shifted, begun_ready = map(
            sem, ("cleared", "keys_ready", "keys_turned", "keys_kept", "same_ready", "reset_ready", "shifted", "begun_ready"))
        carried_ready, carried_turned, keep_ready, row_ready, hot_b_ready, hot_ready, lo_turned, squared, hot_t_ready = map(
            sem, ("carried_ready", "carried_turned", "keep_ready", "row_ready", "hot_b_ready", "hot_ready", "lo_turned",
                  "squared", "hot_t_ready"))
        q_ready, prod_ready, dot_ready, score_ready, scores_turned, run_ready, max_ready, max_turned, rel_ready = map(
            sem, ("q_ready", "prod_ready", "dot_ready", "score_ready", "scores_turned", "run_ready", "max_ready", "max_turned", "rel_ready"))
        exp_ready, weighted, sums_ready, summed, piece_kept, ends_kept = map(
            sem, ("exp_ready", "weighted", "sums_ready", "summed", "piece_kept", "ends_kept"))
        block = ctx.enter_context(nc.Block())

        @block.sync
        def _(sp):
            def load(k, v):
                sp.dma_start(rec[:, v], rec_dram[ds((4 * k + v) * (G * P), G * P), :].rearrange("(p t) w -> p t w", t=G)
                             ).then_inc(rec_in[v], 16)

            def store_pieces(k, v):
                s, u = 4 * k + v, v % 2
                sp.wait_ge(piece_kept, NB * (s + 1))
                sp.dma_start(piece_dram[ds(s * G, G), :].rearrange("(a t) w -> a t w", a=1), piece[:, u]
                             ).then_inc(pieces_out[u], 16)

            def step(k, v):
                s, u = 4 * k + v, v % 2
                if not (fixed(k) and s + 4 >= ST):
                    sp.wait_ge(score_ready, s + 1)
                    sp.sem_inc(load_opened, 1)
                    sp.wait_ge(kv_in[v], 16 * G * (k + 1))
                    sp.sem_inc(load_opened, 1)
                    load(k + 1, v)
                sp.wait_ge(ends_kept, s + 1)
                sp.dma_start(ends_dram[ds(s * G, G), :, :].rearrange("t h w -> (t h) w"), ends[:, u, :]).then_inc(ends_out[u], 16)
                if not start(k, v):
                    store_pieces(*behind(k, v))

            for v in range(4):
                load(0, v)
            in_fours(sp, step, ST)
            store_pieces((ST - 1) // 4, (ST - 1) % 4)
            for u in range(2):
                sp.wait_ge(pieces_out[u], 16 * (ST // 2))
                sp.wait_ge(ends_out[u], 16 * (ST // 2))

        @block.gpsimd
        def _(pool):
            def step(k, v):
                s = 4 * k + v
                if not (fixed(k) and k == 0):
                    pool.wait_ge(weighted, s - 3)
                pool.wait_ge(rec_in[v], 16 * (k + 1))
                pool.sem_inc(opened, 1)
                for t in range(G):
                    pool.indirect_dma_start(kv[:, v, t, :], None, kv_dram[:, :],
                                            bass.IndirectOffsetOnAxis(ap=rec[:, v, t, H + 2:H + 3], axis=0)
                                            ).then_inc(kv_in[v], 16)

            in_fours(pool, step, ST)

        @block.tensor
        def _(pe):
            def turn_keys(k, v):
                s, u = 4 * k + v, v % 2
                pe.wait_ge(keys_ready, s + 1)
                if not start(k, v):
                    pe.wait_ge(keep_ready, s)
                pe.sem_inc(turns_opened, 1)
                pe.transpose(key_ps[0:GH, 0:P], keyf[:, u].rearrange("p t h -> p (t h)"), c["ident"][:]).then_inc(keys_turned, 1)
                spread_rows(k, v, 0)

            def shift_keys(k, v):
                s, u = 4 * k + v, v % 2
                pe.wait_ge(keys_kept, s + 1)
                pe.sem_inc(turns_opened, 1)
                pe.matmul(key_ps[0:GH, P:P + 1], c["shift"][:], key_t[:, u, P - 1:P], start=True, stop=False)
                pe.matmul(key_ps[0:GH, P:P + 1], c["wrap"][:], key_t[:, 1 - u, P - 1:P], start=False, stop=True).then_inc(shifted, 1)

            def spread_rows(k, v, q):
                s, u = 4 * k + v, v % 2
                if not (start(k, v) and q == 0):
                    pe.wait_ge(squared, 2 * s + q)
                for t in range(4):
                    mm = pe.matmul(lo_ps[:, t, :], row_b[:, u, 4 * q + t:4 * q + t + 1].broadcast_to([P, P]),
                                   c["identb"][:], start=True, stop=True)
                mm.then_inc(lo_turned, 1)

            def turn_carried(k, v):
                pe.wait_ge(carried_ready, 4 * k + v + 1)
                pe.sem_inc(turns_opened, 1)
                pe.transpose(key_ps[:, 192:192 + GH], carried[:], c["ident"][0:GH, 0:GH]).then_inc(carried_turned, 1)

            def sums(k, v, bank):
                s, u = 4 * k + v, v % 2
                if bank == 0:
                    pe.wait_ge(hot_ready, s + 1)
                    if not start(k, v):
                        pe.wait_ge(piece_kept, NB * s)
                    pe.wait_ge(weighted, s + 1)
                for i, t in enumerate(banks[bank]):
                    mm = pe.matmul(sum_ps[:, bank, i * W:(i + 1) * W], hot[:, u, t, :], wv[:, u, t, :], start=True, stop=True)
                mm.then_inc(sums_ready, 1)

            def q_rows(k, v, bucket, q):
                s, u = 4 * k + v, v % 2
                pe.wait_ge(hot_t_ready, 2 * s + q + 1)
                if not start(k, v):
                    pe.wait_ge(prod_ready, 2 * s - 1 + q)
                for t in range(4):
                    for part in range(3):
                        mm = pe.matmul(q_ps[:, q, t, :], hot_t[:, u, 4 * q + t, :], q3[:, ds(bucket[4 * q + t], 1), part, :],
                                       start=(part == 0), stop=(part == 2))
                mm.then_inc(q_ready, 1)

            def step(k, v):
                s, u = 4 * k + v, v % 2
                if not last(k, v):
                    spread_rows(*ahead(k, v), 1)
                    turn_carried(*ahead(k, v))
                if not start(k, v):
                    sums(*behind(k, v), 0)
                    sums(*behind(k, v), 1)
                if not last(k, v):
                    bucket = buckets(nc, c, mybir.EngineType.PE, s + 1, 0, G)
                pe.wait_ge(score_ready, s + 1)
                if not start(k, v):
                    pe.wait_ge(rel_ready, s)
                pe.sem_inc(turns_opened, 1)
                pe.transpose(seg_ps[0:GH, 0:P], score[:, u].rearrange("p t h -> p (t h)"), c["ident"][:]).then_inc(scores_turned, 1)
                if not start(k, v):
                    sums(*behind(k, v), 2)
                if not last(k, v):
                    q_rows(*ahead(k, v), bucket, 0)
                pe.wait_ge(max_ready, s + 1)
                pe.sem_inc(turns_opened, 1)
                pe.transpose(seg_ps[:, 192:192 + GH], seg_max[:, u, :], c["ident"][0:GH, 0:GH]).then_inc(max_turned, 1)
                if not (last(k, v) or last(*ahead(k, v))):
                    turn_keys(*ahead(*ahead(k, v)))
                    shift_keys(*ahead(*ahead(k, v)))
                if not last(k, v):
                    q_rows(*ahead(k, v), bucket, 1)

            pe.wait_ge(cleared, 1)
            turn_keys(0, 0)
            shift_keys(0, 0)
            spread_rows(0, 0, 1)
            turn_carried(0, 0)
            turn_keys(0, 1)
            shift_keys(0, 1)
            bucket = buckets(nc, c, mybir.EngineType.PE, 0, 0, G)
            q_rows(0, 0, bucket, 0)
            q_rows(0, 0, bucket, 1)
            in_fours(pe, step, ST)
            for bank in range(NB):
                sums((ST - 1) // 4, (ST - 1) % 4, bank)

        @block.scalar
        def _(act):
            def keys(k, v):
                s, u = 4 * k + v, v % 2
                act.wait_ge(rec_in[v], 16 * (k + 1))
                if not early(k, v):
                    act.wait_ge(lo_turned, 2 * s - 2)
                act.copy(keyf[:, u], rec[:, v, :, H:H + 1].broadcast_to([P, G, H]))
                act.copy(row_b[:, u], rec[:, v, :, H + 1]).then_inc(keys_ready, 1)

            def keep_keys(k, v):
                act.wait_ge(keys_turned, 4 * k + v + 1)
                if not early(k, v):
                    act.wait_ge(ends_kept, 4 * k + v - 1)
                act.copy(key_t[:, v % 2, :], key_ps[0:GH, 0:P]).then_inc(keys_kept, 1)

            def one_hot_t(k, v):
                s, u = 4 * k + v, v % 2
                for q in range(2):
                    act.wait_ge(lo_turned, 2 * s + q + 1)
                    if not start(k, v):
                        act.wait_ge(hot_t_ready, 2 * s - 1 + q)
                    act.activation(off2[:, q], lo_ps[:], ACT.Square, bias=neg_row[:, 0:1]).then_inc(squared, 1)
                for q in range(2):
                    act.wait_ge(squared, 2 * s + q + 1)
                    if not early(k, v):
                        act.wait_ge(q_ready, 2 * s - 3 + q)
                    act.activation(hot_t[:, u, 4 * q:4 * q + 4, :], off2[:, q], ACT.Relu, bias=1.0, scale=-1.0).then_inc(hot_t_ready, 1)

            def widen_hot(k, v):
                s, u = 4 * k + v, v % 2
                act.wait_ge(hot_b_ready, s + 1)
                if not early(k, v):
                    act.wait_ge(sums_ready, NB * (s - 1))
                act.copy(hot[:, u], hot_b[:].rearrange("p n t -> p t n")).then_inc(hot_ready, 1)

            def pieces(k, v, b):
                s, u, tiles = 4 * k + v, v % 2, banks[b]
                if b == 0 and not early(k, v):
                    act.wait_ge(pieces_out[u], 16 * used(k, v))
                act.wait_ge(summed, G * s + tiles[-1] + 1)
                act.copy(piece[:, u, tiles[0]:tiles[-1] + 1, :],
                         sum_ps[0:1, b, 0:len(tiles) * W].rearrange("a (t w) -> a t w", w=W)).then_inc(piece_kept, 1)

            def step(k, v):
                s, u = 4 * k + v, v % 2
                more = not (last(k, v) or last(*ahead(k, v)))
                if more:
                    keys(*ahead(*ahead(k, v)))
                if not last(k, v):
                    one_hot_t(*ahead(k, v))
                if not last(k, v):
                    widen_hot(*ahead(k, v))
                act.wait_ge(max_ready, s + 1)
                if not early(k, v):
                    act.wait_ge(ends_out[u], 16 * used(k, v))
                act.copy(ends[:, u, 0:2], seg_max[:, u, 0:P:P - 1])
                act.copy(ends[:, u, 2:4], key_t[:, u, 0:P:P - 1]).then_inc(ends_kept, 1)
                act.wait_ge(rel_ready, s + 1)
                if not early(k, v):
                    act.wait_ge(sums_ready, NB * (s - 1))
                act.activation(wv[:, u, :, 0:H], score[:, u], ACT.Exp).then_inc(exp_ready, 1)
                if more:
                    keep_keys(*ahead(*ahead(k, v)))
                if not start(k, v):
                    for b in range(NB):
                        pieces(*behind(k, v), b)

            act.wait_ge(cleared, 1)
            keys(0, 0)
            keys(0, 1)
            keep_keys(0, 0)
            one_hot_t(0, 0)
            widen_hot(0, 0)
            keep_keys(0, 1)
            in_fours(act, step, ST)
            for b in range(NB):
                pieces((ST - 1) // 4, (ST - 1) % 4, b)

        @block.vector
        def _(dve):
            def weigh(k, v):
                u = v % 2
                dve.wait_ge(exp_ready, 4 * k + v + 1)
                dve.tensor_tensor(wv[:, u, :, H:].rearrange("p t (d h) -> p t d h", h=H),
                                  kv[:, v, :, D:].rearrange("p t (d h) -> p t d h", h=H),
                                  bcast(wv[:, u, :, 0:H], 2, DH), ALU.mult).then_inc(weighted, 1)

            def add(bucket, k, v, t):
                s, b, i = 4 * k + v, t // 3, t % 3
                if i == 0:
                    dve.wait_ge(sums_ready, NB * s + b + 1)
                if not (start(k, v) and t < 2):
                    dve.wait_ge(summed, G * s + t - 1)
                a = acc[:, t % 2, ds(bucket[t % 4], 1), :].rearrange("p b w -> p (b w)")
                dve.tensor_tensor(a, sum_ps[:, b, i * W:(i + 1) * W], a, ALU.add).then_inc(summed, 1)

            def segments(k, v):
                s, u = 4 * k + v, v % 2
                dve.wait_ge(keys_kept, s + 1)
                dve.tensor_tensor(reset[:, u, 1:P], key_t[:, u, 1:P], key_t[:, u, 0:P - 1], ALU.is_equal).then_inc(same_ready, 1)
                dve.wait_ge(shifted, s + 1)
                dve.tensor_tensor(begun[:], key_ps[0:GH, P:P + 1], key_t[:, u, 0:1], ALU.is_equal).then_inc(begun_ready, 1)
                dve.wait_ge(same_ready, s + 1)
                dve.tensor_scalar(reset[:, u, 1:P], reset[:, u, 1:P], 1.0, BIG, ALU.subtract, ALU.mult).then_inc(reset_ready, 1)
                dve.wait_ge(begun_ready, s + 1)
                dve.tensor_scalar(carried[:], key_t[:, u, :], key_t[:, u, 0:1], begun[:, 0:1], ALU.is_equal, ALU.mult
                                  ).then_inc(carried_ready, 1)

            def keep_rows(k, v):
                dve.wait_ge(carried_turned, 4 * k + v + 1)
                dve.tensor_scalar(keep[:], key_ps[:, 192:192 + GH:H], -1.0, 1.0, ALU.mult, ALU.add).then_inc(keep_ready, 1)

            def clear_carried(k, v):
                dve.wait_ge(keep_ready, 4 * k + v + 1)
                dve.tensor_tensor(row_k[:], rec[:, v, :, H + 1], keep[:], ALU.mult).then_inc(row_ready, 1)

            def one_hot(k, v):
                s = 4 * k + v
                dve.wait_ge(row_ready, s + 1)
                if not start(k, v):
                    dve.wait_ge(hot_ready, s)
                dve.tensor_tensor(hot_b[:], c["iota_g"][:], bcast(row_k[:], 1, P), ALU.is_equal).then_inc(hot_b_ready, 1)

            def step(k, v):
                s, u = 4 * k + v, v % 2
                more, begin = not last(k, v), start(k, v)
                if more:
                    segments(*ahead(k, v))
                if not begin:
                    bk, bv = behind(k, v)
                    weigh(bk, bv)
                if not (fixed(k) and 4 * k + v == 0):
                    low = buckets(nc, c, mybir.EngineType.DVE, s - 1, 0, 4)
                dve.wait_ge(kv_in[v], 16 * G * (k + 1))
                for q in range(2):
                    dve.wait_ge(q_ready, 2 * s + q + 1)
                    dve.tensor_tensor(prod[:, q], q_ps[:, q], kv[:, v, 4 * q:4 * q + 4, 0:D], ALU.mult).then_inc(prod_ready, 1)
                for q in range(2):
                    dve.wait_ge(prod_ready, 2 * s + q + 1)
                    dve.tensor_reduce(score[:, u, 4 * q:4 * q + 4, :], prod[:, q].rearrange("p t (h d) -> p t h d", h=H),
                                      AX.X, ALU.add).then_inc(dot_ready, 1)
                if more:
                    keep_rows(*ahead(k, v))
                dve.wait_ge(dot_ready, 2 * s + 2)
                dve.tensor_tensor(score[:, u], score[:, u], rec[:, v, :, 0:H].bitcast(F32), ALU.add).then_inc(score_ready, 1)
                if more:
                    clear_carried(*ahead(k, v))
                if not begin:
                    high = buckets(nc, c, mybir.EngineType.DVE, s - 1, 4, G)
                if more:
                    one_hot(*ahead(k, v))
                if not begin:
                    add(low, bk, bv, 0)
                    add(low, bk, bv, 1)
                dve.wait_ge(scores_turned, s + 1)
                dve.tensor_tensor_scan(run_max[:], reset[:, u, 0:P], seg_ps[0:GH, 0:P], -BIG, ALU.add, ALU.max).then_inc(run_ready, 1)
                if not begin:
                    add(low, bk, bv, 2)
                dve.wait_ge(run_ready, s + 1)
                if not early(k, v):
                    dve.wait_ge(ends_kept, s - 1)
                dve.tensor_tensor_scan(seg_max[:, u, ::-1], reset[:, u, P:0:-1], run_max[:, ::-1], -BIG, ALU.add, ALU.max
                                       ).then_inc(max_ready, 1)
                if not begin:
                    add(low, bk, bv, 3)
                    add(high, bk, bv, 4)
                    add(high, bk, bv, 5)
                dve.wait_ge(max_turned, s + 1)
                dve.tensor_tensor(score[:, u], score[:, u], seg_ps[:, 192:192 + GH].rearrange("p (t h) -> p t h", t=G), ALU.subtract
                                  ).then_inc(rel_ready, 1)
                if not begin:
                    add(high, bk, bv, 6)
                    add(high, bk, bv, 7)

            dve.tensor_scalar(neg_row[:], c["rown"][:], -1.0, None, ALU.mult)
            dve.memset(reset[:], -BIG)
            dve.memset(key_t[:, 1, :], -5.0)
            dve.memset(acc[:], 0.0).then_inc(cleared, 1)
            dve.wait_ge(cleared, 1)
            segments(0, 0)
            keep_rows(0, 0)
            clear_carried(0, 0)
            one_hot(0, 0)
            in_fours(dve, step, ST)
            k, v = (ST - 1) // 4, (ST - 1) % 4
            weigh(k, v)
            for half in range(2):
                bucket = buckets(nc, c, mybir.EngineType.DVE, ST - 1, 4 * half, 4 * half + 4)
                for t in range(4 * half, 4 * half + 4):
                    add(bucket, k, v, t)


def merge(nc, c, piece_dram, ends_dram, merge_dram):
    TP = MT * P
    with ExitStack() as ctx:
        sb, psum, sem = allocators(nc, ctx, "merge")
        ends = sb("ends", [H, T, 4], F32)
        top = sb("top", [H, 2 * T], F32)
        key = sb("key", [H, 2 * T], F32)
        reset = sb("reset", [H, 2 * T + 1], F32)
        run_max = sb("run_max", [H, 2 * T], F32)
        seg_max = sb("seg_max", [H, 2 * T], F32)
        scale = sb("scale", [H, 2 * T], F32)
        carry = sb("carry", [H, T + 1], F32)
        whole = sb("whole", [H, T], F32)
        begins = sb("begins", [H, T], F32)
        rows = sb("row_table", [H, 4, TP], F32)
        spare = sb("spare", [H, T], F32)
        last_row = sb("last_row", [H, T], F32)
        cols = sb("cols", [P, 4, MT, H], F32)
        index = sb("index", [P, MT], I32)
        piece = sb("piece", [P, MT, W], F32)
        part = sb("part", [P, MT, MW], F32)
        same = sb("same", [P, MT, TP], F32)
        total = sb("total", [P, MT, MW], F32)
        col_ps = psum("col_ps", [P, 512], F32)
        key_ps = psum("key_ps", [P, 2, 512], F32)
        total_ps = psum("total_ps", [P, 3, 512], F32)
        ends_in, piece_in, cleared, done, exp_ready, rows_ready, cols_ready, keys_ready, part_ready, total_ready, total_kept, scattered = map(
            sem, ("ends_in", "piece_in", "cleared", "done", "exp_ready", "rows_ready", "cols_ready", "keys_ready",
                  "part_ready", "total_ready", "total_kept", "scattered"))
        rel_ready = sem("rel_ready")
        block = ctx.enter_context(nc.Block())
        full = T // P
        rest = T - full * P

        @block.sync
        def _(sp):
            sp.dma_start(ends[:], ends_dram.rearrange("t h w -> h t w")).then_inc(ends_in, 16)
            sp.wait_ge(cleared, 2)
            sp.dma_start(piece[:, 0:full, :], piece_dram[0:full * P, :].rearrange("(j p) w -> p j w", p=P)).then_inc(piece_in, 16)
            if rest:
                sp.dma_start(piece[0:rest, full:MT, :], piece_dram[full * P:T, :].rearrange("(j p) w -> p j w", j=1)
                             ).then_inc(piece_in, 16)

        @block.gpsimd
        def _(pool):
            pool.iota(spare[:], [[1, T]], base=TRASH, channel_multiplier=0, allow_small_or_imprecise_dtypes=True)
            pool.iota(rows[:, 2, :], [[1, TP]], base=TRASH, channel_multiplier=0,
                      allow_small_or_imprecise_dtypes=True).then_inc(cleared, 1)
            pool.wait_ge(total_kept, MT)
            for j in range(MT):
                pool.indirect_dma_start(merge_dram[:, :], bass.IndirectOffsetOnAxis(ap=index[:, j:j + 1], axis=0),
                                        total[:, j, :], None).then_inc(scattered, 16)
            pool.wait_ge(scattered, 16 * MT)

        @block.scalar
        def _(act):
            act.wait_ge(rel_ready, 1)
            act.activation(scale[:], scale[:], ACT.Exp).then_inc(exp_ready, 1)

        @block.tensor
        def _(pe):
            pe.wait_ge(rows_ready, 1)
            for k in range(2):
                mm = pe.matmul(key_ps[:, k, 0:TP // 2], c["ones"][0:1, :], rows[0:1, 3, k * (TP // 2):(k + 1) * (TP // 2)],
                               start=True, stop=True)
            mm.then_inc(keys_ready, 1)
            for m in range(4):
                for j in range(MT):
                    mm = pe.transpose(col_ps[:, (m * MT + j) * H:(m * MT + j + 1) * H], rows[:, m, j * P:(j + 1) * P],
                                      c["ident"][0:H, 0:H])
            mm.then_inc(cols_ready, 1)
            pe.wait_ge(part_ready, 1)
            for j in range(MT):
                o = total_ps[:, j // 3, (j % 3) * MW:(j % 3 + 1) * MW]
                for i in range(MT):
                    mm = pe.matmul(o, same[:, i, j * P:(j + 1) * P], part[:, i, :], start=(i == 0), stop=(i == MT - 1))
            mm.then_inc(total_ready, 1)

        @block.vector
        def _(dve):
            n = [0]

            def then(ins):
                n[0] += 1
                ins.then_inc(done, 1)
                dve.wait_ge(done, n[0])

            dve.wait_ge(cleared, 1)
            dve.memset(rows[:, 0:2, :], 0.0)
            dve.memset(rows[:, 3, :], -7.0)
            dve.memset(carry[:], 0.0)
            dve.memset(reset[:], -BIG)
            then(dve.memset(piece[:], 0.0))
            dve.sem_inc(cleared, 1)
            dve.wait_ge(ends_in, 16)
            dve.tensor_copy(top[:].rearrange("h (t e) -> h t e", e=2), ends[:, :, 0:2])
            then(dve.tensor_copy(key[:].rearrange("h (t e) -> h t e", e=2), ends[:, :, 2:4]))
            then(dve.tensor_tensor(reset[:, 1:2 * T], key[:, 1:], key[:, 0:2 * T - 1], ALU.is_equal))
            then(dve.tensor_scalar(reset[:, 1:2 * T], reset[:, 1:2 * T], 1.0, BIG, ALU.subtract, ALU.mult))
            then(dve.tensor_tensor_scan(run_max[:], reset[:, 0:2 * T], top[:], -BIG, ALU.add, ALU.max))
            then(dve.tensor_tensor_scan(seg_max[:, ::-1], reset[:, 2 * T:0:-1], run_max[:, ::-1], -BIG, ALU.add, ALU.max))
            dve.tensor_tensor(scale[:], top[:], seg_max[:], ALU.subtract).then_inc(rel_ready, 1)
            first, last = key[:, 0::2], key[:, 1::2]
            dve.tensor_tensor(carry[:, 1:T], key[:, 2::2], key[:, 1:2 * T - 1:2], ALU.is_equal)
            then(dve.tensor_tensor(whole[:], first, last, ALU.is_equal))
            then(dve.tensor_tensor(begins[:], whole[:], carry[:, 0:T], ALU.mult))
            then(dve.tensor_scalar(begins[:], begins[:], -1.0, 1.0, ALU.mult, ALU.add))
            dve.wait_ge(exp_ready, 1)
            dve.tensor_tensor(rows[:, 0, 0:T], scale[:, 0::2], carry[:, 0:T], ALU.mult)
            then(dve.tensor_scalar(rows[:, 1, 1:T], scale[:, 1:2 * T - 1:2], 1.0, None, ALU.subtract))
            then(dve.tensor_tensor(rows[:, 1, 1:T], rows[:, 1, 1:T], begins[:, 0:T - 1], ALU.mult))
            then(dve.tensor_tensor(rows[:, 1, 1:T], rows[:, 1, 1:T], carry[:, 1:T], ALU.mult))
            then(dve.tensor_tensor(last_row[:], whole[:], carry[:, 1:T + 1], ALU.mult))
            then(dve.tensor_scalar(last_row[:], last_row[:], -1.0, 1.0, ALU.mult, ALU.add))
            then(dve.tensor_tensor(last_row[:], last_row[:], carry[:, 0:T], ALU.mult))
            then(dve.scalar_tensor_tensor(last_row[:], first, 0.0, last_row[:], ALU.is_ge, ALU.mult))
            then(dve.scalar_tensor_tensor(whole[:], first, 1.0, spare[:], ALU.add, ALU.subtract))
            then(dve.tensor_tensor(whole[:], whole[:], last_row[:], ALU.mult))
            then(dve.tensor_tensor(rows[:, 2, 0:T], whole[:], spare[:], ALU.add))
            then(dve.tensor_copy(rows[:, 3, 0:T], first))
            dve.sem_inc(rows_ready, 1)
            dve.wait_ge(cols_ready, 1)
            then(dve.tensor_copy(cols[:].rearrange("p m j h -> p (m j h)"), col_ps[:, 0:4 * MT * H]))
            dve.tensor_copy(index[:], cols[:, 2, :, 0])
            dve.wait_ge(keys_ready, 1)
            for i in range(MT):
                dve.tensor_scalar(same[:, i, :].rearrange("p (k t) -> p k t", k=2), key_ps[:, :, 0:TP // 2],
                                  cols[:, 3, i, 0:1], None, ALU.is_equal)
            dve.wait_ge(piece_in, 16 + (16 if rest else 0))
            dve.tensor_copy(part[:, :, 0:H], cols[:, 1])
            dve.tensor_tensor(part[:, :, H:].rearrange("p j (d h) -> p j d h", h=H),
                              piece[:].rearrange("p j (d h) -> p j d h", h=H),
                              bcast(cols[:, 0], 2, W // H), ALU.mult).then_inc(part_ready, 1)
            dve.wait_ge(total_ready, 1)
            for j in range(MT):
                dve.tensor_copy(total[:, j, :], total_ps[:, j // 3, (j % 3) * MW:(j % 3 + 1) * MW]).then_inc(total_kept, 1)


def finish(nc, c, acc, x, merge_dram, out):
    S = B // FB
    first = lambda k: isinstance(k, int) and k == 0
    start = lambda k, u: first(k) and u == 0
    end = lambda k, u: isinstance(k, int) and k == S // 2 - 1 and u == 1
    with ExitStack() as ctx:
        sb, psum, sem = allocators(nc, ctx, "finish")
        x_rows = sb("x_rows", [P, 2, FB, D], F32)
        add = sb("add", [P, 2, FB, MW], F32)
        factor = sb("factor", [P, FB, H], F32)
        both = sb("both", [P, FB, W], F32)
        share = sb("share", [P, FB, H], F32)
        mixed = sb("mixed", [P, FB, D], F32)
        mixed_t = sb("mixed_t", [P, FB, P], F32)
        res = sb("res", [P, FB, D], F32)
        stats = sb("stats", [P, FB, 6], F32)
        moments = sb("moments", [P, FB, 2], F32)
        dev = sb("dev", [P, FB], F32)
        scale = sb("scale", [P, FB], F32)
        eps = sb("eps", [P, 1], F32)
        y = sb("y", [P, 2, FB, D], F32)
        turn_ps = psum("turn_ps", [P, 8, P], F32)
        out_ps = psum("out_ps", [P, 8, D], F32)
        rows_in = [sem(f"rows_in{u}") for u in range(2)]
        y_out = [sem(f"y_out{u}") for u in range(2)]
        load_opened, stats_opened, halves_joined = map(sem, ("load_opened", "stats_opened", "halves_joined"))
        x_zeroed, factor_ready, scaled, both_ready, share_ready, inverse_ready, mixed_ready = map(
            sem, ("x_zeroed", "factor_ready", "scaled", "both_ready", "share_ready", "inverse_ready", "mixed_ready"))
        turned, turn_kept, projected, res_ready, stats_ready, moments_ready, dev_ready, scale_ready, y_ready = map(
            sem, ("turned", "turn_kept", "projected", "res_ready", "stats_ready", "moments_ready", "dev_ready", "scale_ready", "y_ready"))
        block = ctx.enter_context(nc.Block())

        @block.sync
        def _(sp):
            sp.wait_ge(x_zeroed, 1)

            def step(k, u):
                s = 2 * k + u
                if not first(k):
                    sp.wait_ge(res_ready, s - 1)
                    sp.sem_inc(load_opened, 1)
                for p, rows, j in bucket_rows(x, s, end(k, u)):
                    sp.dma_start(x_rows[p, u, j, :], rows).then_inc(rows_in[u], 16)
                sp.dma_start(add[:, u, :, :],
                             bass.AP(merge_dram.tensor, s * (FB * BN * MW), [[MW, P], [BN * MW, FB], [1, MW]])
                             ).then_inc(rows_in[u], 16)

            in_pairs(sp, step, S)

        @block.tensor
        def _(pe):
            def step(k, u):
                s = 2 * k + u
                pe.wait_ge(mixed_ready, s + 1)
                if not start(k, u):
                    pe.wait_ge(turn_kept, s)
                for j in range(FB):
                    mm = pe.transpose(turn_ps[:, j, :], mixed[:, j, :], c["ident"][:])
                mm.then_inc(turned, 1)
                pe.wait_ge(turn_kept, s + 1)
                if not start(k, u):
                    pe.wait_ge(res_ready, s)
                for j in range(FB):
                    pe.matmul(out_ps[:, j, :], mixed_t[:, j, :], c["w_out"][:], start=True, stop=False)
                    mm = pe.matmul(out_ps[:, j, :], c["ones"][0:1, :], c["b_out"][:], start=False, stop=True)
                mm.then_inc(projected, 1)

            in_pairs(pe, step, S)

        @block.scalar
        def _(act):
            def step(k, u):
                s = 2 * k + u
                act.wait_ge(turned, s + 1)
                if not start(k, u):
                    act.wait_ge(projected, s)
                act.copy(mixed_t[:], turn_ps[:, 0:FB, :]).then_inc(turn_kept, 1)
                act.wait_ge(moments_ready, FB * (s + 1))
                act.activation(dev[:], moments[:, :, 1], ACT.Sqrt, bias=eps[:, 0:1]).then_inc(dev_ready, 1)
                act.wait_ge(y_ready, s + 1)
                for p, rows, j in bucket_rows(out, s, end(k, u)):
                    act.dma_start(rows, y[p, u, j, :]).then_inc(y_out[u], 16)

            in_pairs(act, step, S)
            act.wait_ge(y_out[0], 16 * S)
            act.wait_ge(y_out[1], 16 * S + 16)

        @block.vector
        def _(dve):
            by_head = lambda ap: ap.rearrange("p j (d h) -> p j d h", h=H)

            def step(k, u):
                s = 2 * k + u
                dve.wait_ge(rows_in[u], 48 * (k + 1) + (16 if end(k, u) else 0))
                dve.tensor_scalar(factor[:], add[:, u, :, 0:H], 1.0, None, ALU.add).then_inc(factor_ready, 1)
                dve.wait_ge(factor_ready, s + 1)
                dve.tensor_tensor(both[:], acc[:, 0, ds(s * FB, FB), :], acc[:, 1, ds(s * FB, FB), :], ALU.add).then_inc(halves_joined, 1)
                dve.wait_ge(halves_joined, s + 1)
                dve.tensor_tensor(by_head(both[:]), by_head(both[:]), bcast(factor[:], 2, W // H), ALU.mult).then_inc(scaled, 1)
                dve.wait_ge(scaled, s + 1)
                dve.tensor_tensor(both[:], both[:], add[:, u, :, H:], ALU.add).then_inc(both_ready, 1)
                dve.wait_ge(both_ready, s + 1)
                dve.tensor_scalar(share[:], both[:, :, 0:H], 1e-10, None, ALU.add).then_inc(share_ready, 1)
                dve.wait_ge(share_ready, s + 1)
                dve.reciprocal(share[:], share[:]).then_inc(inverse_ready, 1)
                dve.wait_ge(inverse_ready, s + 1)
                if not start(k, u):
                    dve.wait_ge(turned, s)
                dve.tensor_tensor(by_head(mixed[:]), by_head(both[:, :, H:]), bcast(share[:], 2, DH), ALU.mult
                                  ).then_inc(mixed_ready, 1)
                dve.wait_ge(projected, s + 1)
                dve.tensor_tensor(res[:], out_ps[:, 0:FB, :], x_rows[:, u], ALU.add).then_inc(res_ready, 1)
                dve.wait_ge(res_ready, s + 1)
                for j in range(FB):
                    dve.bn_stats(stats[:, j, :], res[:, j, :]).then_inc(stats_ready, 1)
                if not start(k, u):
                    dve.wait_ge(dev_ready, s)
                dve.wait_ge(stats_ready, FB * s + FB)
                dve.sem_inc(stats_opened, 1)
                for j in range(FB):
                    dve.bn_aggr(moments[:, j, :], stats[:, j, :]).then_inc(moments_ready, 1)
                dve.wait_ge(dev_ready, s + 1)
                dve.reciprocal(scale[:], dev[:]).then_inc(scale_ready, 1)
                dve.wait_ge(scale_ready, s + 1)
                if not first(k):
                    dve.wait_ge(y_out[u], 32 * k)
                for j in range(FB):
                    ins = dve.tensor_scalar(y[:, u, j, :], res[:, j, :], moments[:, j, 0:1], scale[:, j:j + 1],
                                            ALU.subtract, ALU.mult)
                ins.then_inc(y_ready, 1)

            dve.memset(eps[:], EPS)
            dve.memset(x_rows[:], 0.0).then_inc(x_zeroed, 1)
            in_pairs(dve, step, S)


_INS = ["x", "src", "dst", "edge_attr_128"] + [f"L0_gnn_{m}_{p}" for m in ("q", "k", "v", "out", "eb") for p in "wb"]


def kernel(**inputs):
    import numpy as np
    import concourse.bacc as bacc
    from concourse.bass_utils import run_bass_kernel_spmd

    nc = bacc.Bacc("TRN2", target_bir_lowering=False, num_devices=1)
    arrays = {f"in_{name}": np.ascontiguousarray(inputs[name]) for name in _INS}
    args = [nc.dram_tensor(name, a.shape, mybir.dt.from_np(a.dtype), kind="ExternalInput").ap() for name, a in arrays.items()]
    out = nc.dram_tensor("out", (N, D), F32, kind="ExternalOutput").ap()
    build(nc, *args, out)
    return run_bass_kernel_spmd(nc, [arrays], core_ids=[0]).results[0]["out"]
```

```python
from contextlib import ExitStack

import concourse.bass as bass
import concourse.mybir as mybir

P = 128
F32, BF16, I32 = mybir.dt.float32, mybir.dt.bfloat16, mybir.dt.int32
ALU = mybir.AluOpType
ACT = mybir.ActivationFunctionType
AX = mybir.AxisListType
ds = bass.ds

N, D = 6250, 128
E = 106250
H = 8
DH = D // H
EPS = 1e-5
BN = P - 1
B = -(-N // BN)
BC = B + 2
G = 8
EC = E // P
REST = E - EC * P
SI = -(-(EC + 1) // (2 * G)) * 2
CI = SI * G
T = -(-((E + B * (P - 1)) // P) // (2 * G)) * (2 * G)
ST = T // G
ROWS = T * P + G * P
RW = 16
W = H + D
MT = -(-T // P)
MW = H + W
TRASH = B * P + P
BIG = 1.0e30
GH = G * H
FB = 5
assert B % (2 * FB) == 0 and 2 * P * (CI - EC) < ROWS - T * P and SI * G >= EC + 1


def bcast(ap, dim, count):
    shape = list(ap.shape)
    return ap.unsqueeze(dim).broadcast_to(shape[:dim] + [count] + shape[dim:])


def build(nc, x, src, dst, edge, q_w, q_b, k_w, k_b, v_w, v_b, out_w, out_b, eb_w, eb_b, out):
    kv_dram = nc.dram_tensor("kv_rows", [N, 2 * D], F32, kind="Internal").ap()
    rec_dram = nc.dram_tensor("sorted_records", [ROWS, RW], I32, kind="Internal").ap()
    piece_dram = nc.dram_tensor("pieces", [T, W], F32, kind="Internal").ap()
    ends_dram = nc.dram_tensor("segment_ends", [H, T, 4], F32, kind="Internal").ap()
    merge_dram = nc.dram_tensor("merge_rows", [TRASH + MT * P, MW], F32, kind="Internal").ap()

    with ExitStack() as keep:
        sb = lambda name, shape, dt: keep.enter_context(nc.sbuf_tensor(name, shape, dt))
        c = {
            "ident": sb("ident", [P, P], F32), "identb": sb("identb", [P, P], BF16),
            "iota": sb("iota", [P, P], F32), "iota_g": sb("iota_g", [P, P, G], BF16),
            "rown": sb("rown", [P, 1], F32), "ones": sb("ones", [P, P], F32),
            "below": sb("below", [P, P], BF16), "belowf": sb("belowf", [P, P], F32),
            "shift": sb("shift", [G * H, G * H], F32), "wrap": sb("wrap", [G * H, G * H], F32),
            "w_kvq": sb("w_kvq", [P, 3 * D], F32), "b_kvq": sb("b_kvq", [1, 3 * D], F32),
            "b_rows": sb("b_rows", [P, 4 * D], F32),
            "w_out": sb("w_out", [P, D], F32), "b_out": sb("b_out", [1, D], F32),
            "w_eb": sb("w_eb", [P, G, G * H], F32), "b_eb": sb("b_eb", [1, G * H], F32),
            "carrier": keep.enter_context(nc.semaphore("carrier")),
            "bucket_of": sb("bucket_of", [1, T], I32),
        }
        acc = sb("acc", [P, 2, B, W], F32)
        with ExitStack() as queries:
            q3 = queries.enter_context(nc.sbuf_tensor("q3", [P, B, 3, D], BF16))
            with ExitStack() as ranks:
                rsb = lambda name, shape, dt: ranks.enter_context(nc.sbuf_tensor(name, shape, dt))
                r = {
                    "meta": rsb("meta", [P, CI, 3], I32),
                    "lo": rsb("lo", [P, CI], BF16), "hi": rsb("hi", [P, CI], BF16),
                    "start_a": rsb("start_a", [P, BC], BF16), "start_r": rsb("start_r", [P, BC], BF16),
                }
                constants(nc, c, r, acc, src, dst, q_w, q_b, k_w, k_b, v_w, v_b, out_w, out_b, eb_w, eb_b)
                cnt = rsb("cnt", [P, BC], F32)
                prepare(nc, c, r, q3, cnt, x, kv_dram, rec_dram, merge_dram)
                tables(nc, c, r, cnt)
                rank(nc, c, r, edge, rec_dram)
            attend(nc, c, q3, acc, kv_dram, rec_dram, piece_dram, ends_dram)
        x_rows = sb("x_rows", [P, B, D], F32)
        merge(nc, c, acc, x, x_rows, piece_dram, ends_dram, merge_dram)
        finish(nc, c, acc, x_rows, merge_dram, out)


def allocators(nc, ctx, stage):
    return (lambda name, shape, dt: ctx.enter_context(nc.sbuf_tensor(f"{stage}_{name}", shape, dt)),
            lambda name, shape, dt: ctx.enter_context(nc.psum_tensor(f"{stage}_{name}", shape, dt)),
            lambda name: ctx.enter_context(nc.semaphore(f"{stage}_{name}")))


def constants(nc, c, r, acc, src, dst, q_w, q_b, k_w, k_b, v_w, v_b, out_w, out_b, eb_w, eb_b):
    with ExitStack() as ctx:
        sb, psum, sem = allocators(nc, ctx, "constants")
        src_c = sb("src_c", [P, CI], I32)
        dst_c = sb("dst_c", [P, CI], I32)
        srcf = sb("srcf", [P, CI], F32)
        hif = sb("hif", [P, CI], F32)
        hii = sb("hii", [P, CI], I32)
        off = sb("off", [P, CI], F32)
        low = sb("low", [P, CI], F32)
        w_raw = sb("w_raw", [P, 5, D], F32)
        b_raw = sb("b_raw", [1, 3 * D + H], F32)
        w_ps = psum("w_ps", [P, 8, P], F32)
        w_in = sem("w_in")
        idx_in, blank_src, rest_in, split = map(sem, ("idx_in", "blank_src", "rest_in", "split"))
        filled = sem("filled")
        const_done = sem("const_done")
        w_turned = sem("w_turned")
        w_eb_zeroed = sem("w_eb_zeroed")
        block = ctx.enter_context(nc.Block())
        @block.sync
        def _(sp):
            sp.dma_start(src_c[:, 0:EC], src[0:EC * P].rearrange("(p j) -> p j", p=P)).then_inc(idx_in, 16)
            sp.dma_start(dst_c[:, 0:EC], dst[0:EC * P].rearrange("(p j) -> p j", p=P)).then_inc(idx_in, 16)
            sp.wait_ge(blank_src, 2)
            sp.dma_start(src_c[0:REST, EC:EC + 1], src[EC * P:E].rearrange("(p j) -> p j", j=1)).then_inc(rest_in, 16)
            sp.dma_start(dst_c[0:REST, EC:EC + 1], dst[EC * P:E].rearrange("(p j) -> p j", j=1)).then_inc(rest_in, 16)
            for k, w in enumerate((k_w, v_w, q_w, out_w)):
                sp.dma_start(w_raw[:, k, :], w).then_inc(w_in, 16)
            sp.dma_start(w_raw[0:H, 4, :], eb_w).then_inc(w_in, 16)
            sp.dma_start(b_raw[0:1, 0:D], k_b.rearrange("(a n) -> a n", a=1)).then_inc(w_in, 16)
            sp.dma_start(b_raw[0:1, D:2 * D], v_b.rearrange("(a n) -> a n", a=1)).then_inc(w_in, 16)
            sp.dma_start(b_raw[0:1, 2 * D:3 * D], q_b.rearrange("(a n) -> a n", a=1)).then_inc(w_in, 16)
            sp.dma_start(c["b_out"][:], out_b.rearrange("(a n) -> a n", a=1)).then_inc(w_in, 16)
            sp.dma_start(b_raw[0:1, 3 * D:], eb_b.rearrange("(a n) -> a n", a=1)).then_inc(w_in, 16)
            sp.wait_ge(w_in, 16 * 10)

        @block.gpsimd
        def _(pool):
            pool.iota(src_c[:, EC:CI], [[0, CI - EC]], base=B * BN, channel_multiplier=1).then_inc(blank_src, 1)
            pool.memset(dst_c[:, EC:CI], 0).then_inc(blank_src, 1)
            pool.memset(c["ident"][:], 0.0).then_inc(filled, 1)
            pool.memset(c["ones"][:], 1.0).then_inc(filled, 1)
            pool.memset(c["shift"][:], 0.0).then_inc(filled, 1)
            pool.memset(c["wrap"][:], 0.0).then_inc(filled, 1)
            pool.iota(c["iota"][:], [[1, P]], base=0, channel_multiplier=0,
                      allow_small_or_imprecise_dtypes=True).then_inc(const_done, 1)
            pool.iota(c["iota_g"][:], [[1, P], [0, G]], base=0, channel_multiplier=0,
                      allow_small_or_imprecise_dtypes=True).then_inc(const_done, 1)
            pool.iota(c["rown"][:], [[0, 1]], base=0, channel_multiplier=1,
                      allow_small_or_imprecise_dtypes=True).then_inc(const_done, 1)
            pool.wait_ge(filled, 4)
            pool.affine_select(out=c["ident"][:], in_=c["ident"][:], compare_op=ALU.not_equal, fill=1.0,
                               base=0, pattern=[[-1, P]], channel_multiplier=1).then_inc(const_done, 1)
            pool.affine_select(out=c["belowf"][:], in_=c["ones"][:], compare_op=ALU.is_ge, fill=0.0,
                               base=-1, pattern=[[1, P]], channel_multiplier=-1).then_inc(const_done, 1)
            pool.affine_select(out=c["shift"][:], in_=c["shift"][:], compare_op=ALU.not_equal, fill=1.0,
                               base=H, pattern=[[-1, G * H]], channel_multiplier=1).then_inc(const_done, 1)
            pool.affine_select(out=c["wrap"][:], in_=c["wrap"][:], compare_op=ALU.not_equal, fill=1.0,
                               base=H - G * H, pattern=[[-1, G * H]], channel_multiplier=1).then_inc(const_done, 1)
            pool.memset(acc[:], 0.0)

        @block.tensor
        def _(pe):
            pe.wait_ge(w_in, 16 * 10)
            pe.wait_ge(const_done, 7)
            for k in range(4):
                pe.transpose(w_ps[:, k, :], w_raw[:, k, :], c["ident"][:])
            pe.transpose(w_ps[:, 4, 0:H], w_raw[0:H, 4, :], c["ident"][0:H, 0:H]).then_inc(w_turned, 1)

        @block.vector
        def _(dve):
            n = [0]

            def then(ins):
                n[0] += 1
                ins.then_inc(split, 1)
                dve.wait_ge(split, n[0])

            dve.wait_ge(idx_in, 32)
            dve.wait_ge(rest_in, 32)
            then(dve.tensor_copy(srcf[:], src_c[:]))
            then(dve.tensor_scalar(hii[:], srcf[:], 1.0 / BN, 0.5 / BN - 0.5, ALU.mult, ALU.add))
            then(dve.tensor_copy(hif[:], hii[:]))
            then(dve.scalar_tensor_tensor(off[:], hif[:], -float(BN), srcf[:], ALU.mult, ALU.add))
            dve.tensor_scalar(low[:], off[:], 0.0, None, ALU.is_lt)
            then(dve.tensor_scalar(off[:], off[:], float(BN), None, ALU.is_ge))
            then(dve.tensor_tensor(off[:], off[:], low[:], ALU.subtract))
            then(dve.tensor_tensor(hif[:], hif[:], off[:], ALU.add))
            dve.tensor_copy(r["hi"][:], hif[:])
            then(dve.scalar_tensor_tensor(low[:], hif[:], -float(BN), srcf[:], ALU.mult, ALU.add))
            then(dve.tensor_scalar(low[:], low[:], 1.0, None, ALU.add))
            dve.tensor_copy(r["lo"][:], low[:])
            dve.tensor_copy(r["meta"][:, :, 0], src_c[:])
            dve.tensor_copy(r["meta"][:, :, 1], low[:])
            then(dve.tensor_copy(r["meta"][:, :, 2], dst_c[:]))

            dve.wait_ge(const_done, 7)
            dve.tensor_copy(c["identb"][:], c["ident"][:])
            dve.tensor_copy(c["below"][:], c["belowf"][:])
            dve.memset(c["w_eb"][:], 0.0).then_inc(w_eb_zeroed, 1)
            dve.wait_ge(w_in, 16 * 10)
            heads_in = lambda ap: ap.rearrange("p (h d) -> p d h", h=H)
            heads_out = lambda ap: ap.rearrange("p (d h) -> p d h", h=H)
            dve.tensor_copy(c["b_kvq"][:, 0:D], b_raw[:, 0:D])
            dve.tensor_copy(heads_out(c["b_kvq"][:, D:2 * D]), heads_in(b_raw[:, D:2 * D]))
            dve.tensor_copy(c["b_eb"][:].rearrange("a (t h) -> a t h", t=G), bcast(b_raw[:, 3 * D:], 1, G))
            dve.tensor_scalar(c["b_kvq"][:, 2 * D:], b_raw[:, 2 * D:3 * D], DH ** -0.5, None, ALU.mult)
            dve.wait_ge(w_turned, 1)
            dve.tensor_copy(c["w_kvq"][:, 0:D], w_ps[:, 0, :])
            dve.tensor_copy(heads_out(c["w_kvq"][:, D:2 * D]), heads_in(w_ps[:, 1, :]))
            dve.tensor_scalar(c["w_kvq"][:, 2 * D:], w_ps[:, 2, :], DH ** -0.5, None, ALU.mult)
            dve.wait_ge(w_eb_zeroed, 1)
            for t in range(G):
                dve.tensor_copy(c["w_eb"][:, t, t * H:(t + 1) * H], w_ps[:, 4, 0:H])

    with ExitStack() as ctx:
        sb, psum, sem = allocators(nc, ctx, "constants2")
        w_perm = sb("w_perm", [P, D], F32)
        w_rows = sb("w_rows", [P, D], F32)
        wo_ps = psum("wo_ps", [P, D], F32)
        wo_in = sem("wo_in")
        wo_perm = sem("wo_perm")
        wo_turned = sem("wo_turned")
        bias_ps = psum("bias_ps", [P, 512], F32)
        bias_spread = sem("bias_spread")
        block = ctx.enter_context(nc.Block())
        @block.sync
        def _(sp):
            sp.dma_start(w_rows[:], out_w).then_inc(wo_in, 16)

        @block.vector
        def _(dve):
            dve.wait_ge(wo_in, 16)
            dve.tensor_copy(w_perm[:].rearrange("p (d h) -> p d h", h=H),
                            w_rows[:].rearrange("p (h d) -> p d h", h=H)).then_inc(wo_perm, 1)
            dve.wait_ge(bias_spread, 1)
            dve.tensor_copy(c["b_rows"][:], bias_ps[:])
            dve.wait_ge(wo_turned, 1)
            dve.tensor_copy(c["w_out"][:], wo_ps[:])

        @block.tensor
        def _(pe):
            pe.matmul(bias_ps[:, 0:3 * D], c["ones"][0:1, :], c["b_kvq"][:], start=True, stop=True)
            pe.matmul(bias_ps[:, 3 * D:], c["ones"][0:1, :], c["b_out"][:], start=True, stop=True).then_inc(bias_spread, 1)
            pe.wait_ge(wo_perm, 1)
            pe.transpose(wo_ps[:], w_perm[:], c["ident"][:]).then_inc(wo_turned, 1)


def bucket_rows(dram, k, tail):
    whole = FB - 1 if tail else FB
    by_row = dram[ds(k * (FB * BN), whole * BN), :].rearrange("(j p) d -> p j d", p=BN)
    parts = [(slice(1, 65), by_row[0:64], slice(0, whole)), (slice(65, P), by_row[64:BN], slice(0, whole))]
    if tail:
        at = (B - 1) * BN
        parts.append((slice(1, 1 + N - at), dram[at:N, :].rearrange("(j p) d -> p j d", j=1), slice(FB - 1, FB)))
    return parts


def in_pairs(eng, step, steps, head=1):
    for k in range(head):
        step(k, 0)
        step(k, 1)
    with eng.Fori(head, steps // 2 - 1) as k:
        step(k, 0)
        step(k, 1)
    step(steps // 2 - 1, 0)
    step(steps // 2 - 1, 1)


def one_hots(dve, c, r, hot_lo, hot_hi, s, hot_ready):
    at = ds(s * G, G)
    dve.tensor_tensor(hot_lo, c["iota_g"][:], bcast(r["lo"][:, at], 1, P), ALU.is_equal)
    dve.tensor_tensor(hot_hi, c["iota_g"][:, 0:BC, :], bcast(r["hi"][:, at], 1, BC), ALU.is_equal).then_inc(hot_ready, 1)


def prepare(nc, c, r, q3, cnt, x, kv_dram, rec_dram, merge_dram):
    S = B // FB
    CS = SI // S
    left = SI - S * CS
    per = ROWS // P // G
    mper = B * P // P // 2
    assert ROWS == P * per * G and B % 2 == 0 and FB == 5 and CS == 10 and left % 2 == 0
    first = lambda k: isinstance(k, int) and k == 0
    start = lambda k, u: first(k) and u == 0
    end = lambda k, u: isinstance(k, int) and k == S // 2 - 1 and u == 1
    with ExitStack() as ctx:
        sb, psum, sem = allocators(nc, ctx, "prepare")
        blank = sb("blank", [P, per, RW], I32)
        zero = sb("zero", [P, mper, MW], F32)
        x_rows = sb("x_rows", [P, 2, FB, D], F32)
        x_t = sb("x_t", [P, FB, P], F32)
        kv_out = sb("kv_out", [P, 2, FB, 2 * D], F32)
        q_out = sb("q_out", [P, 2, FB, D], F32)
        q_left = sb("q_left", [P, FB, D], F32)
        zerob = sb("zerob", [P, P], BF16)
        hot_lo = sb("hot_lo", [P, 2, P, G], BF16)
        hot_hi = sb("hot_hi", [P, 2, BC, G], BF16)
        turn_ps = psum("turn_ps", [P, 8, P], F32)
        kv_ps = psum("kv_ps", [P, 6, 2 * D], F32)
        q_ps = psum("q_ps", [P, 8, D], F32)
        cnt_ps = psum("cnt_ps", [P, 512], F32)
        x_in = [sem(f"x_in{u}") for u in range(2)]
        kv_stored = [sem(f"kv_stored{u}") for u in range(2)]
        hot_ready, hot_used, counted = map(sem, ("hot_ready", "hot_used", "counted"))
        zeroed, blank_ready, blanks_out, zeros_out = map(sem, ("zeroed", "blank_ready", "blanks_out", "zeros_out"))
        x_zeroed, x_turned, x_kept, kv_ready, q_ready, kv_added, q_added = map(
            sem, ("x_zeroed", "x_turned", "x_kept", "kv_ready", "q_ready", "kv_added", "q_added"))
        q_part0, q_rest, q_part1, q_part2 = map(sem, ("q_part0", "q_rest", "q_part1", "q_part2"))
        block = ctx.enter_context(nc.Block())

        @block.sync
        def _(sp):
            sp.wait_ge(x_zeroed, 1)

            def step(k, u):
                if not first(k):
                    sp.wait_ge(x_turned, 2 * k + u - 1)
                for p, rows, j in bucket_rows(x, 2 * k + u, end(k, u)):
                    sp.dma_start(x_rows[p, u, j, :], rows).then_inc(x_in[u], 16)

            in_pairs(sp, step, S)

        @block.gpsimd
        def _(pool):
            pool.memset(x_rows[:], 0.0).then_inc(x_zeroed, 1)
            pool.memset(zerob[:], 0.0).then_inc(zeroed, 1)
            pool.memset(blank[:], 0).then_inc(zeroed, 1)
            pool.wait_ge(zeroed, 2)
            pool.memset(blank[:, :, H], -1).then_inc(blank_ready, 1)
            pool.memset(blank[:, :, H + 1], 200).then_inc(blank_ready, 1)
            pool.memset(zero[:], 0.0).then_inc(blank_ready, 1)
            pool.wait_ge(blank_ready, 3)
            for k in range(G):
                pool.dma_start(rec_dram[k * P * per:(k + 1) * P * per, :].rearrange("(p r) w -> p r w", p=P),
                               blank[:]).then_inc(blanks_out, 16)
            for k in range(2):
                pool.dma_start(merge_dram[k * P * mper:(k + 1) * P * mper, :].rearrange("(p r) w -> p r w", p=P),
                               zero[:]).then_inc(zeros_out, 16)

            def step(k, u):
                s = 2 * k + u
                part = lambda m: q3[:, ds(s * FB, FB), m, :]
                pool.wait_ge(q_added, s + 1)
                pool.tensor_copy(part(0), q_out[:, u]).then_inc(q_part0, 1)
                pool.wait_ge(q_part0, s + 1)
                if not start(k, u):
                    pool.wait_ge(q_part2, s)
                pool.sem_inc(c["carrier"], 1)
                pool.tensor_tensor(q_left[:], q_out[:, u], part(0), ALU.subtract).then_inc(q_rest, 1)
                pool.wait_ge(q_rest, s + 1)
                pool.tensor_copy(part(1), q_left[:]).then_inc(q_part1, 1)
                pool.wait_ge(q_part1, s + 1)
                pool.sem_inc(c["carrier"], 1)
                pool.tensor_tensor(part(2), q_left[:], part(1), ALU.subtract).then_inc(q_part2, 1)

            in_pairs(pool, step, S)
            pool.wait_ge(blanks_out, 16 * G)
            pool.wait_ge(zeros_out, 32)

        @block.tensor
        def _(pe):
            def count_step(i, u):
                pe.wait_ge(hot_ready, i + 1)
                for t in range(G):
                    mm = pe.matmul(cnt_ps[:, 0:BC], hot_lo[:, u, :, t], hot_hi[:, u, :, t], start=False, stop=False)
                mm.then_inc(hot_used, 1)

            def step(k, u):
                s = 2 * k + u
                pe.wait_ge(x_in[u], 32 * (k + 1) + (16 if end(k, u) else 0))
                if not start(k, u):
                    pe.wait_ge(x_kept, s)
                for j in range(FB):
                    mm = pe.transpose(turn_ps[:, j, :], x_rows[:, u, j, :], c["ident"][:])
                mm.then_inc(x_turned, 1)
                pe.wait_ge(x_kept, s + 1)
                parts = [[("q", 0), ("q", 1), ("q", 2)], [("q", 3), ("q", 4), ("kv", 0)], [("kv", 1), ("kv", 2)],
                         [("kv", 3), ("kv", 4)], []]
                for i, part in enumerate(parts):
                    for w in range(2):
                        count_step(s * CS + 2 * i + w, w)
                    for what, j in part:
                        if what == "q":
                            if j == 0 and not start(k, u):
                                pe.wait_ge(q_added, s)
                            mm = pe.matmul(q_ps[:, j, :], x_t[:, j, :], c["w_kvq"][:, 2 * D:], start=True, stop=True)
                            ready = q_ready
                        else:
                            if j == 0 and not start(k, u):
                                pe.wait_ge(kv_added, s)
                            mm = pe.matmul(kv_ps[:, j, :], x_t[:, j, :], c["w_kvq"][:, 0:2 * D], start=True, stop=True)
                            ready = kv_ready
                        if j == FB - 1:
                            mm.then_inc(ready, 1)

            pe.sem_inc(hot_used, 1)
            pe.wait_ge(zeroed, 1)
            pe.matmul(cnt_ps[:, 0:BC], zerob[:], zerob[:, 0:BC], start=True, stop=False)
            in_pairs(pe, step, S)
            for i in range(S * CS, SI):
                count_step(i, i % 2)
            pe.matmul(cnt_ps[:, 0:BC], zerob[:], zerob[:, 0:BC], start=False, stop=True).then_inc(counted, 1)

        @block.scalar
        def _(act):
            def store(k, u):
                act.wait_ge(kv_added, 2 * k + u + 1)
                for p, rows, j in bucket_rows(kv_dram, 2 * k + u, end(k, u)):
                    act.dma_start(rows, kv_out[p, u, j, :]).then_inc(kv_stored[u], 16)

            def step(k, u):
                s = 2 * k + u
                act.wait_ge(x_turned, s + 1)
                if not start(k, u):
                    act.wait_ge(kv_ready, s)
                act.copy(x_t[:], turn_ps[:, 0:FB, :]).then_inc(x_kept, 1)
                if not start(k, u):
                    store(k - 1 if u == 0 else k, 1 - u)

            in_pairs(act, step, S)
            store(S // 2 - 1, 1)
            act.wait_ge(kv_stored[0], 16 * S)
            act.wait_ge(kv_stored[1], 16 * S + 16)

        @block.vector
        def _(dve):
            def hots(i, w, new):
                if not new:
                    dve.wait_ge(hot_used, i)
                one_hots(dve, c, r, hot_lo[:, w], hot_hi[:, w], i, hot_ready)

            def add_q_bias(k, u):
                s = 2 * k + u
                dve.wait_ge(q_ready, s + 1)
                if not first(k):
                    dve.wait_ge(q_part1, s - 1)
                dve.tensor_tensor(q_out[:, u], q_ps[:, 0:FB, :], bcast(c["b_rows"][:, 2 * D:3 * D], 1, FB), ALU.add).then_inc(q_added, 1)

            def add_kv_bias(k, u):
                s = 2 * k + u
                dve.wait_ge(kv_ready, s + 1)
                if not first(k):
                    dve.wait_ge(kv_stored[u], k * 32)
                dve.tensor_tensor(kv_out[:, u], kv_ps[:, 0:FB, :], bcast(c["b_rows"][:, 0:2 * D], 1, FB), ALU.add).then_inc(kv_added, 1)

            def step(k, u):
                s = 2 * k + u
                if start(k, u):
                    for i in range(CS):
                        hots(i, i % 2, i < 2)
                else:
                    before = (k - 1 if u == 0 else k, 1 - u)
                    hot_pair(s, 0)
                    add_q_bias(*before)
                    hot_pair(s, 1)
                    add_kv_bias(*before)
                    for i in range(2, CS // 2):
                        hot_pair(s, i)

            def hot_pair(s, i):
                for w in range(2):
                    hots(s * CS + 2 * i + w, w, False)

            in_pairs(dve, step, S, head=2)
            for i in range(S * CS, SI):
                hots(i, i % 2, False)
            add_q_bias(S // 2 - 1, 1)
            add_kv_bias(S // 2 - 1, 1)
            dve.wait_ge(counted, 1)
            dve.tensor_copy(cnt[:], cnt_ps[:, 0:BC])


def tables(nc, c, r, cnt):
    with ExitStack() as ctx:
        sb, psum, sem = allocators(nc, ctx, "tables")
        toti = sb("toti", [P, BC], I32)
        tiles = sb("tiles", [P, B], F32)
        last = sb("last", [P, B], F32)
        first = sb("first", [P, BC], F32)
        onesb = sb("onesb", [P, B], F32)
        lastc = sb("lastc", [P, 1], F32)
        iota_t = sb("iota_t", [P, T], F32)
        ended = sb("ended", [P, T], F32)
        tot_ps = psum("tot_ps", [P, 512], F32)
        turn_ps = psum("turn_ps", [P, 512], F32)
        bkt_ps = psum("bkt_ps", [P, 2, 512], F32)
        done, step_done, summed, aux, last_known = map(sem, ("done", "step_done", "summed", "aux", "last_known"))
        block = ctx.enter_context(nc.Block())
        half = T // 2

        @block.gpsimd
        def _(pool):
            pool.memset(onesb[:], 1.0).then_inc(aux, 1)
            pool.iota(first[:, B:BC], [[P * (CI - EC), BC - B]], base=T * P, channel_multiplier=CI - EC,
                      allow_small_or_imprecise_dtypes=True).then_inc(aux, 1)
            pool.iota(iota_t[:], [[1, T]], base=0, channel_multiplier=0,
                      allow_small_or_imprecise_dtypes=True).then_inc(aux, 1)

        @block.vector
        def _(dve):
            n = [0]

            def then(ins):
                n[0] += 1
                ins.then_inc(done, 1)
                dve.wait_ge(done, n[0])

            dve.wait_ge(summed, 1)
            dve.wait_ge(aux, 3)
            then(dve.tensor_scalar(toti[:], tot_ps[:, 0:BC], float(P - 1), None, ALU.add))
            then(dve.tensor_scalar(toti[:], toti[:], 7, None, ALU.logical_shift_right))
            then(dve.tensor_copy(tiles[:], toti[:, 0:B]))
            then(dve.tensor_tensor_scan(last[:], onesb[:], tiles[:], 0.0, ALU.mult, ALU.add))
            dve.sem_inc(last_known, 1)
            then(dve.tensor_tensor(tiles[:], last[:], tiles[:], ALU.subtract))
            then(dve.scalar_tensor_tensor(first[:, 0:B], tiles[:], float(P), tot_ps[:, 256:256 + B], ALU.mult, ALU.add))
            then(dve.tensor_copy(r["start_a"][:], first[:]))
            then(dve.tensor_tensor(r["start_r"][:], first[:], r["start_a"][:], ALU.subtract))
            dve.wait_ge(summed, 2)
            then(dve.tensor_copy(lastc[0:B, :], turn_ps[0:B, 0:1]))
            then(dve.tensor_scalar(ended[0:B, :], iota_t[0:B, :], lastc[0:B, 0:1], None, ALU.is_ge))
            dve.sem_inc(step_done, 1)
            dve.wait_ge(summed, 3)
            then(dve.tensor_scalar(c["bucket_of"][:].rearrange("a (k t) -> a k t", k=2), bkt_ps[0:1, :, 0:half],
                                   float(B - 1), None, ALU.min))

        @block.tensor
        def _(pe):
            pe.matmul(tot_ps[:, 0:BC], c["ones"][:], cnt[:], start=True, stop=True)
            pe.matmul(tot_ps[:, 256:256 + BC], c["belowf"][:], cnt[:], start=True, stop=True).then_inc(summed, 1)
            pe.wait_ge(last_known, 1)
            pe.transpose(turn_ps[0:B, 0:P], last[:], c["ident"][:]).then_inc(summed, 1)
            pe.wait_ge(step_done, 1)
            for k in range(2):
                mm = pe.matmul(bkt_ps[0:1, k, 0:half], c["ones"][0:B, 0:1], ended[0:B, k * half:(k + 1) * half],
                               start=True, stop=True)
            mm.then_inc(summed, 1)


def rank(nc, c, r, edge, rec_dram):
    with ExitStack() as ctx:
        sb, psum, sem = allocators(nc, ctx, "rank")
        edges = sb("edges", [P, 2, G, D], F32)
        edges_t = sb("edges_t", [P, 2, G // 2, P], F32)
        hot_lo = sb("hot_lo", [P, 2, P, G], BF16)
        hot_hi = sb("hot_hi", [P, 2, BC, G], BF16)
        hot_lo_t = sb("hot_lo_t", [P, 2, G, P], BF16)
        before = sb("before", [P, 2, G, P], BF16)
        next_a = sb("next_a", [P, 2, G + 1, BC], BF16)
        next_r = sb("next_r", [P, 2, G + 1, BC], BF16)
        bias_t = sb("bias_t", [GH, P], F32)
        picked = sb("picked", [P, G, BC], F32)
        slotf = sb("slotf", [P, G], F32)
        slot = sb("slot", [P, G], I32)
        within = sb("within", [P, G], I32)
        tile8 = sb("tile8", [P, G], I32)
        group = sb("group", [P, G], I32)
        row = sb("row", [P, 2, G], I32)
        record = sb("record", [P, 2, G, RW], I32)
        turn_ps = psum("turn_ps", [P, G, P], BF16)
        edge_ps = psum("edge_ps", [P, 2, 4, P], F32)
        next_ps = psum("next_ps", [P, 512], F32)
        same_ps = psum("same_ps", [P, 2, 4, P], F32)
        slot_ps = psum("slot_ps", [P, 512], F32)
        bias_ps = psum("bias_ps", [P, 512], F32)
        edges_in = [sem(f"edges_in{u}") for u in range(2)]
        scattered = [sem(f"scattered{u}") for u in range(2)]
        bias_t_kept, bias_turned = sem("bias_t_kept"), sem("bias_turned")
        edges_turned, edges_kept, bias_ready, bias_kept = map(sem, ("edges_turned", "edges_kept", "bias_ready", "bias_kept"))
        hot_ready, lo_turned, lo_kept, same_ready, before_ready = map(
            sem, ("hot_ready", "lo_turned", "lo_kept", "same_ready", "before_ready"))
        next_ready, next_a_kept, next_r_kept, slots_ready = map(
            sem, ("next_ready", "next_a_kept", "next_r_kept", "slots_ready"))
        picked_ready, slotf_ready, slot_ready, bits_ready, joined, rows_ready, meta_kept, table_ready = map(
            sem, ("picked_ready", "slotf_ready", "slot_ready", "bits_ready", "joined", "rows_ready", "meta_kept", "table_ready"))
        block = ctx.enter_context(nc.Block())
        LAST = SI - 1
        tail = EC - LAST * G
        assert 0 < tail < G

        first = lambda k: isinstance(k, int) and k == 0
        end = lambda k, u: isinstance(k, int) and k == SI // 2 - 1 and u == 1

        @block.sync
        def _(sp):
            by_col = edge[0:EC * P, :].rearrange("(p j) d -> p j d", p=P)

            def step(k, u):
                if not first(k):
                    sp.wait_ge(edges_turned, 2 * (2 * (k - 1) + u) + 2)
                if end(k, u):
                    sp.dma_start(edges[:, u, 0:tail, :], by_col[:, LAST * G:EC, :]).then_inc(edges_in[u], 16)
                    sp.dma_start(edges[0:REST, u, tail, :], edge[EC * P:E, :]).then_inc(edges_in[u], 16)
                else:
                    sp.dma_start(edges[:, u, :, :], by_col[:, ds((2 * k + u) * G, G), :]).then_inc(edges_in[u], 16)

            in_pairs(sp, step, SI)

        @block.gpsimd
        def _(pool):
            def step(k, u):
                s = 2 * k + u
                pool.wait_ge(rows_ready, s + 1)
                pool.wait_ge(meta_kept, s + 1)
                pool.wait_ge(bias_kept, s + 1)
                pool.sem_inc(c["carrier"], 1)
                for t in range(G):
                    pool.indirect_dma_start(rec_dram[:, :], bass.IndirectOffsetOnAxis(ap=row[:, u, t:t + 1], axis=0),
                                            record[:, u, t, :], None).then_inc(scattered[u], 16)

            in_pairs(pool, step, SI)
            for u in range(2):
                pool.wait_ge(scattered[u], 16 * G * (SI // 2))

        @block.tensor
        def _(pe):
            def turn_lo(s, u):
                pe.wait_ge(hot_ready, s + 1)
                if not (isinstance(s, int) and s == 0):
                    pe.wait_ge(lo_kept, s)
                for t in range(G):
                    mm = pe.transpose(turn_ps[:, t, :], hot_lo[:, u, :, t], c["identb"][:])
                mm.then_inc(lo_turned, 1)

            def step(k, u):
                s = 2 * k + u
                if first(k) and u == 0:
                    pe.wait_ge(table_ready, 2)
                else:
                    pe.wait_ge(next_r_kept, s)
                base = lambda part: bcast(part[:, 1 - u, G, :], 1, G + 1)
                table = next_ps[:, 0:(G + 1) * BC].rearrange("p (t b) -> p t b", t=G + 1)
                pe.matmul(table, c["identb"][:], base(next_a), start=True, stop=False)
                pe.matmul(table, c["identb"][:], base(next_r), start=False, stop=False)
                for t in range(G):
                    mm = pe.matmul(table[:, t + 1:, :], hot_lo[:, u, :, t], bcast(hot_hi[:, u, :, t], 1, G - t),
                                   start=False, stop=(t == G - 1))
                mm.then_inc(next_ready, 1)
                pe.wait_ge(lo_kept, s + 1)
                for q in range(2):
                    if not (first(k) and u == 0):
                        pe.wait_ge(before_ready, 2 * s - 1 + q)
                    for t in range(4):
                        mm = pe.matmul(same_ps[:, q, t, :], hot_lo_t[:, u, 4 * q + t, :], hot_lo_t[:, u, 4 * q + t, :],
                                       start=True, stop=True)
                    mm.then_inc(same_ready, 1)
                pe.wait_ge(edges_in[u], 16 * (k + 1) + (16 if end(k, u) else 0))
                for q in range(2):
                    if not (first(k) and u == 0):
                        pe.wait_ge(edges_kept, 2 * s - 1 + q)
                    for t in range(4):
                        mm = pe.transpose(edge_ps[:, q, t, :], edges[:, u, 4 * q + t, :], c["ident"][:])
                    mm.then_inc(edges_turned, 1)
                if not end(k, u):
                    turn_lo(s + 1, 1 - u)
                if not (first(k) and u == 0):
                    pe.wait_ge(bias_kept, s)
                pe.sem_inc(c["carrier"], 1)
                o = bias_ps[0:GH, 0:P]
                pe.matmul(o, c["b_eb"][:], c["ones"][0:1, :], start=True, stop=False)
                for t in range(G):
                    if t % 4 == 0:
                        pe.wait_ge(edges_kept, 2 * s + t // 4 + 1)
                        pe.sem_inc(c["carrier"], 1)
                    mm = pe.matmul(o, c["w_eb"][:, t, :], edges_t[:, t // 4, t % 4, :], start=False, stop=(t == G - 1))
                mm.then_inc(bias_ready, 1)
                pe.wait_ge(next_r_kept, s + 1)
                if not (first(k) and u == 0):
                    pe.wait_ge(picked_ready, s)
                for t in range(G):
                    if t % 4 == 0:
                        pe.wait_ge(before_ready, 2 * s + t // 4 + 1)
                    o = slot_ps[:, t * BC:(t + 1) * BC]
                    pe.matmul(o, hot_lo_t[:, u, t, :], next_a[:, u, t, :], start=True, stop=False)
                    pe.matmul(o, hot_lo_t[:, u, t, :], next_r[:, u, t, :], start=False, stop=False)
                    mm = pe.matmul(o, before[:, u, t, :], hot_hi[:, u, :, t], start=False, stop=True)
                mm.then_inc(slots_ready, 1)
                pe.wait_ge(bias_t_kept, s + 1)
                pe.sem_inc(c["carrier"], 1)
                pe.transpose(bias_ps[:, 192:192 + GH], bias_t[:], c["ident"][0:GH, 0:GH]).then_inc(bias_turned, 1)

            turn_lo(0, 0)
            in_pairs(pe, step, SI)

        @block.scalar
        def _(act):
            def keep_lo(s, u):
                act.wait_ge(lo_turned, s + 1)
                act.copy(hot_lo_t[:, u], turn_ps[:]).then_inc(lo_kept, 1)

            def step(k, u):
                s = 2 * k + u
                act.wait_ge(next_ready, s + 1)
                if not first(k):
                    act.wait_ge(slots_ready, s - 1)
                act.copy(next_a[:, u].rearrange("p t b -> p (t b)"), next_ps[:, 0:(G + 1) * BC]).then_inc(next_a_kept, 1)
                for q in range(2):
                    act.wait_ge(edges_turned, 2 * s + q + 1)
                    if not (first(k) and u == 0):
                        act.wait_ge(bias_ready, s)
                    act.copy(edges_t[:, q], edge_ps[:, q]).then_inc(edges_kept, 1)
                act.wait_ge(bias_ready, s + 1)
                if not (first(k) and u == 0):
                    act.wait_ge(bias_turned, s)
                act.copy(bias_t[:], bias_ps[0:GH, 0:P]).then_inc(bias_t_kept, 1)
                if not end(k, u):
                    if not (first(k) and u == 0):
                        act.wait_ge(slots_ready, s)
                    keep_lo(s + 1, 1 - u)
                act.wait_ge(bias_turned, s + 1)
                if not first(k):
                    act.wait_ge(scattered[u], 16 * G * k)
                act.copy(record[:, u, :, 0:H].bitcast(F32), bias_ps[:, 192:192 + GH].rearrange("p (t h) -> p t h", t=G)
                         ).then_inc(bias_kept, 1)

            act.wait_ge(table_ready, 1)
            keep_lo(0, 0)
            in_pairs(act, step, SI)

        @block.vector
        def _(dve):
            def front(k, u):
                s = 2 * k + u
                for q in range(2):
                    dve.wait_ge(same_ready, 2 * s + q + 1)
                    dve.tensor_tensor(before[:, u, 4 * q:4 * q + 4, :], same_ps[:, q], bcast(c["below"][:], 1, 4),
                                      ALU.mult).then_inc(before_ready, 1)
                dve.wait_ge(next_a_kept, s + 1)
                dve.tensor_tensor(next_r[:, u].rearrange("p t b -> p (t b)"), next_ps[:, 0:(G + 1) * BC],
                                  next_a[:, u].rearrange("p t b -> p (t b)"), ALU.subtract).then_inc(next_r_kept, 1)

            def back(k, s, u, hots):
                dve.wait_ge(slots_ready, s + 1)
                dve.tensor_tensor(picked[:], slot_ps[:, 0:G * BC].rearrange("p (t b) -> p t b", t=G),
                                  hot_hi[:, u].rearrange("p b t -> p t b"), ALU.mult).then_inc(picked_ready, 1)
                dve.wait_ge(picked_ready, s + 1)
                dve.tensor_reduce(slotf[:], picked[:], AX.X, ALU.add).then_inc(slotf_ready, 1)
                if not (isinstance(k, int) and k == 0):
                    dve.wait_ge(scattered[u], 16 * G * k)
                dve.tensor_copy(record[:, u, :, H:H + 3], r["meta"][:, ds(s * G, G), :]).then_inc(meta_kept, 1)
                dve.wait_ge(slotf_ready, s + 1)
                dve.tensor_copy(slot[:], slotf[:]).then_inc(slot_ready, 1)
                if hots:
                    one_hots(dve, c, r, hot_lo[:, u], hot_hi[:, u], s + 2, hot_ready)
                dve.wait_ge(slot_ready, s + 1)
                dve.tensor_scalar(within[:], slot[:], P - 1, 3, ALU.bitwise_and, ALU.logical_shift_left)
                dve.tensor_scalar(tile8[:], slot[:], 7, G - 1, ALU.logical_shift_right, ALU.bitwise_and)
                dve.tensor_scalar(group[:], slot[:], 10, 10, ALU.logical_shift_right, ALU.logical_shift_left
                                  ).then_inc(bits_ready, 1)
                dve.wait_ge(bits_ready, s + 1)
                dve.tensor_tensor(within[:], within[:], tile8[:], ALU.bitwise_or).then_inc(joined, 1)
                dve.wait_ge(joined, s + 1)
                dve.tensor_tensor(row[:, u, :], within[:], group[:], ALU.bitwise_or).then_inc(rows_ready, 1)

            def step(k, u):
                s = 2 * k + u
                if not (first(k) and u == 0):
                    back(k - 1 if u == 0 else k, s - 1, 1 - u, not end(k, u))
                front(k, u)

            for s in range(2):
                one_hots(dve, c, r, hot_lo[:, s], hot_hi[:, s], s, hot_ready)
            dve.memset(record[:], 0).then_inc(table_ready, 1)
            dve.tensor_copy(next_a[:, 1, G, :], r["start_a"][:])
            dve.tensor_copy(next_r[:, 1, G, :], r["start_r"][:]).then_inc(table_ready, 1)
            in_pairs(dve, step, SI, head=2)
            back(SI // 2 - 1, SI - 1, 1, False)


def buckets(nc, c, engine, s, lo, hi):
    _, values = nc.values_load_multi_w_load_instructions(
        c["bucket_of"][0:1, ds(s * G + lo, hi - lo)], engines=[engine], min_val=0, max_val=B - 1,
        skip_runtime_bounds_check_because="count() bounds them by a min with B - 1")
    return values


def in_fours(eng, step, steps):
    whole = (steps - 4) // 4
    for k in range(2):
        for v in range(4):
            step(k, v)
    with eng.Fori(2, whole) as k:
        for v in range(4):
            step(k, v)
    for s in range(4 * whole, steps):
        step(s // 4, s % 4)


def attend(nc, c, q3, acc, kv_dram, rec_dram, piece_dram, ends_dram):
    ahead = lambda k, v: (k, v + 1) if v < 3 else (k + 1, 0)
    behind = lambda k, v: (k, v - 1) if v > 0 else (k - 1, 3)
    fixed = lambda k: isinstance(k, int)
    start = lambda k, v: fixed(k) and 4 * k + v == 0
    early = lambda k, v: fixed(k) and 4 * k + v < 2
    last = lambda k, v: fixed(k) and 4 * k + v == ST - 1
    used = lambda k, v: 2 * k + v // 2
    banks = [range(0, 3), range(3, 6), range(6, G)]
    NB = len(banks)
    with ExitStack() as ctx:
        sb, psum, sem = allocators(nc, ctx, "attend")
        rec = sb("rec", [P, 4, G, RW], I32)
        kv = sb("kv", [P, 4, G, 2 * D], F32)
        keyf = sb("keyf", [P, 2, G, H], F32)
        row_b = sb("row_b", [P, 2, G], BF16)
        key_t = sb("key_t", [GH, 2, P], F32)
        reset = sb("reset", [GH, 2, P + 1], F32)
        begun = sb("begun", [GH, 1], F32)
        carried = sb("carried", [GH, P], F32)
        keep = sb("keep", [P, G], F32)
        row_k = sb("row_k", [P, G], BF16)
        off2 = sb("off2", [P, 2, 4, P], BF16)
        hot_t = sb("hot_t", [P, 2, G, P], BF16)
        hot_b = sb("hot_b", [P, P, G], BF16)
        hot = sb("hot", [P, 2, G, P], F32)
        prod = sb("prod", [P, 2, 4, D], F32)
        score = sb("score", [P, 2, G, H], F32)
        run_max = sb("run_max", [GH, P], F32)
        seg_max = sb("seg_max", [GH, 2, P], F32)
        wv = sb("wv", [P, 2, G, W], F32)
        piece = sb("piece", [1, 2, G, W], F32)
        ends = sb("ends", [GH, 2, 4], F32)
        neg_row = sb("neg_row", [P, 1], F32)
        key_ps = psum("key_ps", [P, 512], F32)
        seg_ps = psum("seg_ps", [P, 512], F32)
        lo_ps = psum("lo_ps", [P, 4, P], F32)
        q_ps = psum("q_ps", [P, 2, 4, P], F32)
        sum_ps = psum("sum_ps", [P, NB, 512], F32)
        rec_in = [sem(f"rec_in{v}") for v in range(4)]
        kv_in = [sem(f"kv_in{v}") for v in range(4)]
        ends_out = [sem(f"ends_out{u}") for u in range(2)]
        pieces_out = [sem(f"pieces_out{u}") for u in range(2)]
        cleared, keys_ready, keys_turned, keys_kept, same_ready, reset_ready, shifted, begun_ready = map(
            sem, ("cleared", "keys_ready", "keys_turned", "keys_kept", "same_ready", "reset_ready", "shifted", "begun_ready"))
        carried_ready, carried_turned, keep_ready, row_ready, hot_b_ready, hot_ready, lo_turned, squared, hot_t_ready = map(
            sem, ("carried_ready", "carried_turned", "keep_ready", "row_ready", "hot_b_ready", "hot_ready", "lo_turned",
                  "squared", "hot_t_ready"))
        q_ready, prod_ready, dot_ready, score_ready, scores_turned, run_ready, max_ready, max_turned, rel_ready = map(
            sem, ("q_ready", "prod_ready", "dot_ready", "score_ready", "scores_turned", "run_ready", "max_ready", "max_turned", "rel_ready"))
        exp_ready, weighted, sums_ready, summed, piece_kept, ends_kept = map(
            sem, ("exp_ready", "weighted", "sums_ready", "summed", "piece_kept", "ends_kept"))
        block = ctx.enter_context(nc.Block())

        @block.sync
        def _(sp):
            def load(k, v):
                sp.dma_start(rec[:, v], rec_dram[ds((4 * k + v) * (G * P), G * P), :].rearrange("(p t) w -> p t w", t=G)
                             ).then_inc(rec_in[v], 16)

            def store_pieces(k, v):
                s, u = 4 * k + v, v % 2
                sp.wait_ge(piece_kept, NB * (s + 1))
                sp.dma_start(piece_dram[ds(s * G, G), :].rearrange("(a t) w -> a t w", a=1), piece[:, u]
                             ).then_inc(pieces_out[u], 16)

            def step(k, v):
                s, u = 4 * k + v, v % 2
                if not (fixed(k) and s + 4 >= ST):
                    sp.wait_ge(score_ready, s + 1)
                    sp.sem_inc(c["carrier"], 1)
                    sp.wait_ge(kv_in[v], 16 * G * (k + 1))
                    sp.sem_inc(c["carrier"], 1)
                    load(k + 1, v)
                sp.wait_ge(ends_kept, s + 1)
                sp.dma_start(ends_dram[:, ds(s * G, G), :].rearrange("h t w -> t h w"), ends[:, u, :]).then_inc(ends_out[u], 16)
                if not start(k, v):
                    store_pieces(*behind(k, v))

            for v in range(4):
                load(0, v)
            in_fours(sp, step, ST)
            store_pieces((ST - 1) // 4, (ST - 1) % 4)
            for u in range(2):
                sp.wait_ge(pieces_out[u], 16 * (ST // 2))
                sp.wait_ge(ends_out[u], 16 * (ST // 2))

        @block.gpsimd
        def _(pool):
            def step(k, v):
                s = 4 * k + v
                if not (fixed(k) and k == 0):
                    pool.wait_ge(weighted, s - 3)
                pool.wait_ge(rec_in[v], 16 * (k + 1))
                pool.sem_inc(c["carrier"], 1)
                for t in range(G):
                    pool.indirect_dma_start(kv[:, v, t, :], None, kv_dram[:, :],
                                            bass.IndirectOffsetOnAxis(ap=rec[:, v, t, H + 2:H + 3], axis=0)
                                            ).then_inc(kv_in[v], 16)

            in_fours(pool, step, ST)

        @block.tensor
        def _(pe):
            def turn_keys(k, v):
                s, u = 4 * k + v, v % 2
                pe.wait_ge(keys_ready, s + 1)
                if not start(k, v):
                    pe.wait_ge(keep_ready, s)
                pe.sem_inc(c["carrier"], 1)
                pe.transpose(key_ps[0:GH, 0:P], keyf[:, u].rearrange("p t h -> p (t h)"), c["ident"][:]).then_inc(keys_turned, 1)
                spread_rows(k, v, 0)

            def shift_keys(k, v):
                s, u = 4 * k + v, v % 2
                pe.wait_ge(keys_kept, s + 1)
                pe.sem_inc(c["carrier"], 1)
                pe.matmul(key_ps[0:GH, P:P + 1], c["shift"][:], key_t[:, u, P - 1:P], start=True, stop=False)
                pe.matmul(key_ps[0:GH, P:P + 1], c["wrap"][:], key_t[:, 1 - u, P - 1:P], start=False, stop=True).then_inc(shifted, 1)

            def spread_rows(k, v, q):
                s, u = 4 * k + v, v % 2
                if not (start(k, v) and q == 0):
                    pe.wait_ge(squared, 2 * s + q)
                for t in range(4):
                    mm = pe.matmul(lo_ps[:, t, :], row_b[:, u, 4 * q + t:4 * q + t + 1].broadcast_to([P, P]),
                                   c["identb"][:], start=True, stop=True)
                mm.then_inc(lo_turned, 1)

            def turn_carried(k, v):
                pe.wait_ge(carried_ready, 4 * k + v + 1)
                pe.sem_inc(c["carrier"], 1)
                pe.transpose(key_ps[:, 192:192 + GH], carried[:], c["ident"][0:GH, 0:GH]).then_inc(carried_turned, 1)

            def sums(k, v, bank):
                s, u = 4 * k + v, v % 2
                if bank == 0:
                    pe.wait_ge(hot_ready, s + 1)
                    if not start(k, v):
                        pe.wait_ge(piece_kept, NB * s)
                    pe.wait_ge(weighted, s + 1)
                for i, t in enumerate(banks[bank]):
                    mm = pe.matmul(sum_ps[:, bank, i * W:(i + 1) * W], hot[:, u, t, :], wv[:, u, t, :], start=True, stop=True)
                mm.then_inc(sums_ready, 1)

            def q_rows(k, v, bucket, q):
                s, u = 4 * k + v, v % 2
                pe.wait_ge(hot_t_ready, 2 * s + q + 1)
                if not start(k, v):
                    pe.wait_ge(prod_ready, 2 * s - 1 + q)
                for t in range(4):
                    for part in range(3):
                        mm = pe.matmul(q_ps[:, q, t, :], hot_t[:, u, 4 * q + t, :], q3[:, ds(bucket[4 * q + t], 1), part, :],
                                       start=(part == 0), stop=(part == 2))
                mm.then_inc(q_ready, 1)

            def step(k, v):
                s, u = 4 * k + v, v % 2
                if not last(k, v):
                    spread_rows(*ahead(k, v), 1)
                    turn_carried(*ahead(k, v))
                if not start(k, v):
                    sums(*behind(k, v), 0)
                    sums(*behind(k, v), 1)
                if not last(k, v):
                    bucket = buckets(nc, c, mybir.EngineType.PE, s + 1, 0, G)
                pe.wait_ge(score_ready, s + 1)
                if not start(k, v):
                    pe.wait_ge(rel_ready, s)
                pe.sem_inc(c["carrier"], 1)
                pe.transpose(seg_ps[0:GH, 0:P], score[:, u].rearrange("p t h -> p (t h)"), c["ident"][:]).then_inc(scores_turned, 1)
                if not start(k, v):
                    sums(*behind(k, v), 2)
                if not last(k, v):
                    q_rows(*ahead(k, v), bucket, 0)
                pe.wait_ge(max_ready, s + 1)
                pe.sem_inc(c["carrier"], 1)
                pe.transpose(seg_ps[:, 192:192 + GH], seg_max[:, u, :], c["ident"][0:GH, 0:GH]).then_inc(max_turned, 1)
                if not (last(k, v) or last(*ahead(k, v))):
                    turn_keys(*ahead(*ahead(k, v)))
                    shift_keys(*ahead(*ahead(k, v)))
                if not last(k, v):
                    q_rows(*ahead(k, v), bucket, 1)

            pe.wait_ge(cleared, 1)
            turn_keys(0, 0)
            shift_keys(0, 0)
            spread_rows(0, 0, 1)
            turn_carried(0, 0)
            turn_keys(0, 1)
            shift_keys(0, 1)
            bucket = buckets(nc, c, mybir.EngineType.PE, 0, 0, G)
            q_rows(0, 0, bucket, 0)
            q_rows(0, 0, bucket, 1)
            in_fours(pe, step, ST)
            for bank in range(NB):
                sums((ST - 1) // 4, (ST - 1) % 4, bank)

        @block.scalar
        def _(act):
            def keys(k, v):
                s, u = 4 * k + v, v % 2
                act.wait_ge(rec_in[v], 16 * (k + 1))
                if not early(k, v):
                    act.wait_ge(lo_turned, 2 * s - 2)
                act.copy(keyf[:, u], rec[:, v, :, H:H + 1].broadcast_to([P, G, H]))
                act.copy(row_b[:, u], rec[:, v, :, H + 1]).then_inc(keys_ready, 1)

            def keep_keys(k, v):
                act.wait_ge(keys_turned, 4 * k + v + 1)
                if not early(k, v):
                    act.wait_ge(ends_kept, 4 * k + v - 1)
                act.copy(key_t[:, v % 2, :], key_ps[0:GH, 0:P]).then_inc(keys_kept, 1)

            def one_hot_t(k, v):
                s, u = 4 * k + v, v % 2
                for q in range(2):
                    act.wait_ge(lo_turned, 2 * s + q + 1)
                    if not start(k, v):
                        act.wait_ge(hot_t_ready, 2 * s - 1 + q)
                    act.activation(off2[:, q], lo_ps[:], ACT.Square, bias=neg_row[:, 0:1]).then_inc(squared, 1)
                for q in range(2):
                    act.wait_ge(squared, 2 * s + q + 1)
                    if not early(k, v):
                        act.wait_ge(q_ready, 2 * s - 3 + q)
                    act.activation(hot_t[:, u, 4 * q:4 * q + 4, :], off2[:, q], ACT.Relu, bias=1.0, scale=-1.0).then_inc(hot_t_ready, 1)

            def widen_hot(k, v):
                s, u = 4 * k + v, v % 2
                act.wait_ge(hot_b_ready, s + 1)
                if not early(k, v):
                    act.wait_ge(sums_ready, NB * (s - 1))
                act.copy(hot[:, u], hot_b[:].rearrange("p n t -> p t n")).then_inc(hot_ready, 1)

            def pieces(k, v, b):
                s, u, tiles = 4 * k + v, v % 2, banks[b]
                if b == 0 and not early(k, v):
                    act.wait_ge(pieces_out[u], 16 * used(k, v))
                act.wait_ge(summed, G * s + tiles[-1] + 1)
                act.copy(piece[:, u, tiles[0]:tiles[-1] + 1, :],
                         sum_ps[0:1, b, 0:len(tiles) * W].rearrange("a (t w) -> a t w", w=W)).then_inc(piece_kept, 1)

            def step(k, v):
                s, u = 4 * k + v, v % 2
                more = not (last(k, v) or last(*ahead(k, v)))
                if more:
                    keys(*ahead(*ahead(k, v)))
                if not last(k, v):
                    one_hot_t(*ahead(k, v))
                if not last(k, v):
                    widen_hot(*ahead(k, v))
                act.wait_ge(max_ready, s + 1)
                if not early(k, v):
                    act.wait_ge(ends_out[u], 16 * used(k, v))
                act.copy(ends[:, u, 0:2], seg_max[:, u, 0:P:P - 1])
                act.copy(ends[:, u, 2:4], key_t[:, u, 0:P:P - 1]).then_inc(ends_kept, 1)
                act.wait_ge(rel_ready, s + 1)
                if not early(k, v):
                    act.wait_ge(sums_ready, NB * (s - 1))
                act.activation(wv[:, u, :, 0:H], score[:, u], ACT.Exp).then_inc(exp_ready, 1)
                if more:
                    keep_keys(*ahead(*ahead(k, v)))
                if not start(k, v):
                    for b in range(NB):
                        pieces(*behind(k, v), b)

            act.wait_ge(cleared, 1)
            keys(0, 0)
            keys(0, 1)
            keep_keys(0, 0)
            one_hot_t(0, 0)
            widen_hot(0, 0)
            keep_keys(0, 1)
            in_fours(act, step, ST)
            for b in range(NB):
                pieces((ST - 1) // 4, (ST - 1) % 4, b)

        @block.vector
        def _(dve):
            def weigh(k, v):
                u = v % 2
                dve.wait_ge(exp_ready, 4 * k + v + 1)
                dve.tensor_tensor(wv[:, u, :, H:].rearrange("p t (d h) -> p t d h", h=H),
                                  kv[:, v, :, D:].rearrange("p t (d h) -> p t d h", h=H),
                                  bcast(wv[:, u, :, 0:H], 2, DH), ALU.mult).then_inc(weighted, 1)

            def add(bucket, k, v, t):
                s, b, i = 4 * k + v, t // 3, t % 3
                if i == 0:
                    dve.wait_ge(sums_ready, NB * s + b + 1)
                if not (start(k, v) and t < 2):
                    dve.wait_ge(summed, G * s + t - 1)
                a = acc[:, t % 2, ds(bucket[t], 1), :].rearrange("p b w -> p (b w)")
                dve.tensor_tensor(a, sum_ps[:, b, i * W:(i + 1) * W], a, ALU.add).then_inc(summed, 1)

            def segments(k, v):
                s, u = 4 * k + v, v % 2
                dve.wait_ge(keys_kept, s + 1)
                dve.tensor_tensor(reset[:, u, 1:P], key_t[:, u, 1:P], key_t[:, u, 0:P - 1], ALU.is_equal).then_inc(same_ready, 1)
                dve.wait_ge(shifted, s + 1)
                dve.tensor_tensor(begun[:], key_ps[0:GH, P:P + 1], key_t[:, u, 0:1], ALU.is_equal).then_inc(begun_ready, 1)
                dve.wait_ge(same_ready, s + 1)
                dve.tensor_scalar(reset[:, u, 1:P], reset[:, u, 1:P], 1.0, BIG, ALU.subtract, ALU.mult).then_inc(reset_ready, 1)
                dve.wait_ge(begun_ready, s + 1)
                dve.tensor_scalar(carried[:], key_t[:, u, :], key_t[:, u, 0:1], begun[:, 0:1], ALU.is_equal, ALU.mult
                                  ).then_inc(carried_ready, 1)

            def keep_rows(k, v):
                dve.wait_ge(carried_turned, 4 * k + v + 1)
                dve.tensor_scalar(keep[:], key_ps[:, 192:192 + GH:H], -1.0, 1.0, ALU.mult, ALU.add).then_inc(keep_ready, 1)

            def clear_carried(k, v):
                dve.wait_ge(keep_ready, 4 * k + v + 1)
                dve.tensor_tensor(row_k[:], rec[:, v, :, H + 1], keep[:], ALU.mult).then_inc(row_ready, 1)

            def one_hot(k, v):
                s = 4 * k + v
                dve.wait_ge(row_ready, s + 1)
                if not start(k, v):
                    dve.wait_ge(hot_ready, s)
                dve.tensor_tensor(hot_b[:], c["iota_g"][:], bcast(row_k[:], 1, P), ALU.is_equal).then_inc(hot_b_ready, 1)

            def step(k, v):
                s, u = 4 * k + v, v % 2
                more, begin = not last(k, v), start(k, v)
                if more:
                    segments(*ahead(k, v))
                if not begin:
                    bk, bv = behind(k, v)
                    weigh(bk, bv)
                if not (fixed(k) and 4 * k + v == 0):
                    bucket = buckets(nc, c, mybir.EngineType.DVE, s - 1, 0, 4)
                dve.wait_ge(kv_in[v], 16 * G * (k + 1))
                for q in range(2):
                    dve.wait_ge(q_ready, 2 * s + q + 1)
                    dve.tensor_tensor(prod[:, q], q_ps[:, q], kv[:, v, 4 * q:4 * q + 4, 0:D], ALU.mult).then_inc(prod_ready, 1)
                    if not begin:
                        bucket = bucket + buckets(nc, c, mybir.EngineType.DVE, s - 1, 4 + 2 * q, 6 + 2 * q)
                for q in range(2):
                    dve.wait_ge(prod_ready, 2 * s + q + 1)
                    dve.tensor_reduce(score[:, u, 4 * q:4 * q + 4, :], prod[:, q].rearrange("p t (h d) -> p t h d", h=H),
                                      AX.X, ALU.add).then_inc(dot_ready, 1)
                if more:
                    keep_rows(*ahead(k, v))
                dve.wait_ge(dot_ready, 2 * s + 2)
                dve.tensor_tensor(score[:, u], score[:, u], rec[:, v, :, 0:H].bitcast(F32), ALU.add).then_inc(score_ready, 1)
                if more:
                    clear_carried(*ahead(k, v))
                if more:
                    one_hot(*ahead(k, v))
                if not begin:
                    add(bucket, bk, bv, 0)
                    add(bucket, bk, bv, 1)
                dve.wait_ge(scores_turned, s + 1)
                dve.tensor_tensor_scan(run_max[:], reset[:, u, 0:P], seg_ps[0:GH, 0:P], -BIG, ALU.add, ALU.max).then_inc(run_ready, 1)
                if not begin:
                    add(bucket, bk, bv, 2)
                dve.wait_ge(run_ready, s + 1)
                if not early(k, v):
                    dve.wait_ge(ends_kept, s - 1)
                dve.tensor_tensor_scan(seg_max[:, u, ::-1], reset[:, u, P:0:-1], run_max[:, ::-1], -BIG, ALU.add, ALU.max
                                       ).then_inc(max_ready, 1)
                if not begin:
                    add(bucket, bk, bv, 3)
                    add(bucket, bk, bv, 4)
                    add(bucket, bk, bv, 5)
                dve.wait_ge(max_turned, s + 1)
                dve.tensor_tensor(score[:, u], score[:, u], seg_ps[:, 192:192 + GH].rearrange("p (t h) -> p t h", t=G), ALU.subtract
                                  ).then_inc(rel_ready, 1)
                if not begin:
                    add(bucket, bk, bv, 6)
                    add(bucket, bk, bv, 7)

            dve.tensor_scalar(neg_row[:], c["rown"][:], -1.0, None, ALU.mult)
            dve.memset(reset[:], -BIG)
            dve.memset(key_t[:, 1, :], -5.0).then_inc(cleared, 1)
            dve.wait_ge(cleared, 1)
            segments(0, 0)
            keep_rows(0, 0)
            clear_carried(0, 0)
            one_hot(0, 0)
            in_fours(dve, step, ST)
            k, v = (ST - 1) // 4, (ST - 1) % 4
            weigh(k, v)
            bucket = buckets(nc, c, mybir.EngineType.DVE, ST - 1, 0, G)
            for t in range(G):
                add(bucket, k, v, t)


def merge(nc, c, acc, x, x_rows, piece_dram, ends_dram, merge_dram):
    TP = MT * P
    with ExitStack() as ctx:
        sb, psum, sem = allocators(nc, ctx, "merge")
        ends = sb("ends", [H, T, 4], F32)
        top = sb("top", [H, 2 * T], F32)
        reset = sb("reset", [H, 2 * T + 1], F32)
        run_max = sb("run_max", [H, 2 * T], F32)
        seg_max = sb("seg_max", [H, 2 * T], F32)
        scale = run_max
        carry = sb("carry", [H, T + 1], F32)
        whole = sb("whole", [H, T], F32)
        begins = sb("begins", [H, T], F32)
        rows = sb("row_table", [H, 4, TP], F32)
        spare = sb("spare", [H, T], F32)
        last_row = sb("last_row", [H, T], F32)
        cols = sb("cols", [P, 3, MT, H], F32)
        index = sb("index", [P, MT], I32)
        piece = sb("piece", [P, MT, W], F32)
        part = sb("part", [P, MT, MW], F32)
        goes_on = sb("goes_on", [P, TP], F32)
        run = sb("run", [P, TP], F32)
        run_rest = sb("run_rest", [MW - P, TP], F32)
        total = part
        col_ps = psum("col_ps", [P, 512], F32)
        part_ps = psum("part_ps", [P, 1024], F32)
        rest_ps = psum("rest_ps", [P, 1024], F32)
        total_ps = psum("total_ps", [P, 3, 512], F32)
        goes_on_ps = total_ps.rearrange("p a b -> p (a b)")
        flags_placed, top_ready, parts_turned, runs_ready = map(sem, ("flags_placed", "top_ready", "parts_turned", "runs_ready"))
        ends_in, piece_in, cleared, done, exp_ready, rows_ready, cols_ready, part_ready, total_ready, total_kept, scattered = map(
            sem, ("ends_in", "piece_in", "cleared", "done", "exp_ready", "rows_ready", "cols_ready",
                  "part_ready", "total_ready", "total_kept", "scattered"))
        rel_ready, x_in, x_cleared, spread, goes_on_ready = map(sem, ("rel_ready", "x_in", "x_cleared", "spread", "goes_on_ready"))
        block = ctx.enter_context(nc.Block())
        full = T // P
        rest = T - full * P

        @block.sync
        def _(sp):
            sp.dma_start(ends[:], ends_dram).then_inc(ends_in, 16)
            sp.wait_ge(cleared, 2)
            sp.dma_start(piece[:, 0:full, :], piece_dram[0:full * P, :].rearrange("(j p) w -> p j w", p=P)).then_inc(piece_in, 16)
            if rest:
                sp.dma_start(piece[0:rest, full:MT, :], piece_dram[full * P:T, :].rearrange("(j p) w -> p j w", j=1)
                             ).then_inc(piece_in, 16)
            sp.wait_ge(x_cleared, 1)
            whole_rows = x[0:(B - 1) * BN, :].rearrange("(j p) d -> p j d", p=BN)
            sp.dma_start(x_rows[1:65, 0:B - 1, :], whole_rows[0:64]).then_inc(x_in, 16)
            sp.dma_start(x_rows[65:P, 0:B - 1, :], whole_rows[64:BN]).then_inc(x_in, 16)
            sp.dma_start(x_rows[1:1 + N - (B - 1) * BN, B - 1, :], x[(B - 1) * BN:N, :]).then_inc(x_in, 16)
            sp.wait_ge(x_in, 48)

        @block.gpsimd
        def _(pool):
            pool.iota(spare[:], [[1, T]], base=TRASH, channel_multiplier=0, allow_small_or_imprecise_dtypes=True)
            pool.iota(rows[:, 2, :], [[1, TP]], base=TRASH, channel_multiplier=0,
                      allow_small_or_imprecise_dtypes=True).then_inc(cleared, 1)
            pool.memset(x_rows[:], 0.0).then_inc(x_cleared, 1)
            with pool.Fori(0, B // FB) as i:
                half = lambda m: acc[:, m, ds(i * FB, FB), :]
                pool.tensor_tensor(half(0), half(0), half(1), ALU.add)
            pool.wait_ge(x_in, 48)
            with pool.Fori(0, B // FB) as i:
                residual = x_rows[:, ds(i * FB, FB), :]
                pool.tensor_tensor(residual, residual, bcast(c["b_rows"][:, 3 * D:], 1, FB), ALU.add)
            pool.wait_ge(total_kept, MT)
            for j in range(MT):
                pool.indirect_dma_start(merge_dram[:, :], bass.IndirectOffsetOnAxis(ap=index[:, j:j + 1], axis=0),
                                        total[:, j, :], None).then_inc(scattered, 16)
            pool.wait_ge(scattered, 16 * MT)

        @block.scalar
        def _(act):
            act.wait_ge(ends_in, 16)
            act.copy(top[:].rearrange("h (t e) -> h t e", e=2), ends[:, :, 0:2]).then_inc(top_ready, 1)
            act.wait_ge(spread, 1)
            act.copy(goes_on[:], goes_on_ps[:, 0:TP]).then_inc(goes_on_ready, 1)
            act.wait_ge(rel_ready, 1)
            act.activation(scale[:], scale[:], ACT.Exp).then_inc(exp_ready, 1)

        @block.tensor
        def _(pe):
            pe.wait_ge(flags_placed, 1)
            pe.matmul(goes_on_ps[:, 0:512], c["ones"][0:1, :], rows[0:1, 3, 0:512], start=True, stop=True)
            pe.matmul(goes_on_ps[:, 512:TP], c["ones"][0:1, :], rows[0:1, 3, 512:], start=True, stop=True).then_inc(spread, 1)
            pe.wait_ge(rows_ready, 1)
            for m in range(3):
                for j in range(MT):
                    mm = pe.transpose(col_ps[:, (m * MT + j) * H:(m * MT + j + 1) * H], rows[:, m, j * P:(j + 1) * P],
                                      c["ident"][0:H, 0:H])
            mm.then_inc(cols_ready, 1)
            pe.wait_ge(part_ready, 1)
            for j in range(MT):
                pe.transpose(part_ps[:, j * P:(j + 1) * P], part[:, j, 0:P], c["ident"][:])
                mm = pe.transpose(rest_ps[0:MW - P, j * P:(j + 1) * P], part[:, j, P:MW], c["ident"][:])
            mm.then_inc(parts_turned, 1)
            pe.wait_ge(goes_on_ready, 1)
            pe.wait_ge(runs_ready, 2)
            for j in range(MT):
                at = (j % 3) * MW
                pe.transpose(total_ps[:, j // 3, at:at + P], run[:, j * P:(j + 1) * P], c["ident"][:])
                mm = pe.transpose(total_ps[:, j // 3, at + P:at + MW], run_rest[:, j * P:(j + 1) * P],
                                  c["ident"][0:MW - P, 0:MW - P])
            mm.then_inc(total_ready, 1)

        @block.vector
        def _(dve):
            n = [0]

            def then(ins):
                n[0] += 1
                ins.then_inc(done, 1)
                dve.wait_ge(done, n[0])

            dve.memset(rows[:, 1, 0:1], 0.0)
            dve.memset(rows[:, 3, 0:1], 0.0)
            dve.memset(carry[:, 0:T + 1:T], 0.0)
            dve.memset(reset[:, 2 * T:], -BIG)
            if rest:
                dve.memset(rows[:, 0:2, T:], 0.0)
                dve.memset(rows[:, 3, T:], 0.0)
                then(dve.memset(piece[:, full:MT, :], 0.0))
            dve.sem_inc(cleared, 1)
            dve.wait_ge(ends_in, 16)
            first, last = ends[:, :, 2], ends[:, :, 3]
            dve.tensor_tensor(carry[:, 1:T], ends[:, 1:T, 2], ends[:, 0:T - 1, 3], ALU.is_equal)
            dve.tensor_tensor(rows[:, 3, 1:T], ends[:, 1:T, 2], ends[:, 0:T - 1, 2], ALU.is_equal)
            then(dve.tensor_tensor(whole[:], first, last, ALU.is_equal))
            dve.sem_inc(flags_placed, 1)
            dve.tensor_scalar(reset[:, 0:2 * T:2], carry[:, 0:T], 1.0, BIG, ALU.subtract, ALU.mult)
            dve.tensor_scalar(reset[:, 1:2 * T:2], whole[:], 1.0, BIG, ALU.subtract, ALU.mult)
            then(dve.tensor_tensor(begins[:], whole[:], carry[:, 0:T], ALU.mult))
            dve.wait_ge(top_ready, 1)
            then(dve.tensor_tensor_scan(run_max[:], reset[:, 0:2 * T], top[:], -BIG, ALU.add, ALU.max))
            then(dve.tensor_tensor_scan(seg_max[:, ::-1], reset[:, 2 * T:0:-1], run_max[:, ::-1], -BIG, ALU.add, ALU.max))
            dve.tensor_tensor(scale[:], top[:], seg_max[:], ALU.subtract).then_inc(rel_ready, 1)
            then(dve.tensor_scalar(begins[:], begins[:], -1.0, 1.0, ALU.mult, ALU.add))
            dve.wait_ge(cleared, 2)
            then(dve.tensor_tensor(last_row[:], whole[:], carry[:, 1:T + 1], ALU.mult))
            then(dve.tensor_scalar(last_row[:], last_row[:], -1.0, 1.0, ALU.mult, ALU.add))
            then(dve.tensor_tensor(last_row[:], last_row[:], carry[:, 0:T], ALU.mult))
            then(dve.scalar_tensor_tensor(last_row[:], first, 0.0, last_row[:], ALU.is_ge, ALU.mult))
            then(dve.scalar_tensor_tensor(whole[:], first, 1.0, spare[:], ALU.add, ALU.subtract))
            then(dve.tensor_tensor(whole[:], whole[:], last_row[:], ALU.mult))
            then(dve.tensor_tensor(rows[:, 2, 0:T], whole[:], spare[:], ALU.add))
            dve.wait_ge(exp_ready, 1)
            dve.tensor_tensor(rows[:, 0, 0:T], scale[:, 0::2], carry[:, 0:T], ALU.mult)
            then(dve.tensor_scalar(rows[:, 1, 1:T], scale[:, 1:2 * T - 1:2], 1.0, None, ALU.subtract))
            then(dve.tensor_tensor(rows[:, 1, 1:T], rows[:, 1, 1:T], begins[:, 0:T - 1], ALU.mult))
            then(dve.tensor_tensor(rows[:, 1, 1:T], rows[:, 1, 1:T], carry[:, 1:T], ALU.mult))
            dve.sem_inc(rows_ready, 1)
            dve.wait_ge(cols_ready, 1)
            then(dve.tensor_copy(cols[:].rearrange("p m j h -> p (m j h)"), col_ps[:, 0:3 * MT * H]))
            dve.tensor_copy(index[:], cols[:, 2, :, 0])
            dve.wait_ge(piece_in, 16 + (16 if rest else 0))
            dve.tensor_copy(part[:, :, 0:H], cols[:, 1])
            dve.tensor_tensor(part[:, :, H:].rearrange("p j (d h) -> p j d h", h=H),
                              piece[:].rearrange("p j (d h) -> p j d h", h=H),
                              bcast(cols[:, 0], 2, W // H), ALU.mult).then_inc(part_ready, 1)
            dve.wait_ge(parts_turned, 1)
            dve.wait_ge(goes_on_ready, 1)
            dve.tensor_tensor_scan(run[:], goes_on[:], part_ps[:, 0:TP], 0.0, ALU.mult, ALU.add).then_inc(runs_ready, 1)
            dve.tensor_tensor_scan(run_rest[:], goes_on[0:MW - P, :], rest_ps[0:MW - P, 0:TP], 0.0, ALU.mult, ALU.add
                                   ).then_inc(runs_ready, 1)
            dve.wait_ge(total_ready, 1)
            for j in range(MT):
                dve.tensor_copy(total[:, j, :], total_ps[:, j // 3, (j % 3) * MW:(j % 3 + 1) * MW]).then_inc(total_kept, 1)


def finish(nc, c, acc, x_rows, merge_dram, out):
    S = B // FB
    head = 2 * FB
    ahead = lambda k, u: (k, 1) if u == 0 else (k + 1, 0)
    behind = lambda k, u: (k, 0) if u == 1 else (k - 1, 1)
    fixed = lambda k: isinstance(k, int)
    start = lambda k, u: fixed(k) and 2 * k + u == 0
    early = lambda k, u: fixed(k) and 2 * k + u < 2
    end = lambda k, u: fixed(k) and 2 * k + u == S - 1
    with ExitStack() as ctx:
        sb, psum, sem = allocators(nc, ctx, "finish")
        add = sb("add", [P, B, MW], F32)
        factor = sb("factor", [P, B, H], F32)
        both = sb("both", [P, 2, FB, W], F32)
        share = sb("share", [P, FB, H], F32)
        mixed = sb("mixed", [P, FB, D], F32)
        mixed_t = sb("mixed_t", [P, FB, P], F32)
        res = sb("res", [P, 2, FB, D], F32)
        stats = sb("stats", [P, FB, 6], F32)
        moments = sb("moments", [P, 2, FB, 2], F32)
        dev = sb("dev", [P, FB], F32)
        scale = sb("scale", [P, FB], F32)
        offset = sb("offset", [P, FB], F32)
        eps = sb("eps", [P, 1], F32)
        y = sb("y", [P, 2, FB, D], F32)
        turn_ps = psum("turn_ps", [P, 8, P], F32)
        out_ps = psum("out_ps", [P, 8, D], F32)
        offset_ready = sem("offset_ready")
        add_in = [sem(f"add_in{i}") for i in range(2)]
        y_out = [sem(f"y_out{u}") for u in range(2)]
        eps_set, factor_ready, scaled, both_ready, share_ready, inverse_ready, mixed_ready = map(
            sem, ("eps_set", "factor_ready", "scaled", "both_ready", "share_ready",
                  "inverse_ready", "mixed_ready"))
        turned, turn_kept, projected, res_ready, stats_ready, moments_ready, dev_ready, scale_ready, y_ready = map(
            sem, ("turned", "turn_kept", "projected", "res_ready", "stats_ready", "moments_ready", "dev_ready", "scale_ready", "y_ready"))
        block = ctx.enter_context(nc.Block())
        by_head = lambda ap: ap.rearrange("p j (d h) -> p j d h", h=H)

        @block.sync
        def _(sp):
            rows = lambda b, n: bass.AP(merge_dram.tensor, b * BN * MW, [[MW, P], [BN * MW, n], [1, MW]])
            sp.dma_start(add[:, 0:head, :], rows(0, head)).then_inc(add_in[0], 16)
            sp.dma_start(add[:, head:B, :], rows(head, B - head)).then_inc(add_in[1], 16)

        @block.gpsimd
        def _(pool):
            def step(k, u):
                s = 2 * k + u
                at = ds(s * FB, FB)
                if not early(k, u):
                    pool.wait_ge(mixed_ready, s - 1)
                    pool.sem_inc(c["carrier"], 1)
                pool.tensor_tensor(by_head(both[:, u]), by_head(acc[:, 0, at, :]), bcast(factor[:, at, :], 2, W // H), ALU.mult
                                   ).then_inc(scaled, 1)
                pool.wait_ge(scaled, s + 1)
                pool.sem_inc(c["carrier"], 1)
                pool.tensor_tensor(both[:, u], both[:, u], add[:, at, H:], ALU.add).then_inc(both_ready, 1)

            for i, (b0, b1) in enumerate(((0, head), (head, B))):
                pool.wait_ge(add_in[i], 16)
                pool.tensor_scalar(factor[:, b0:b1, :], add[:, b0:b1, 0:H], 1.0, None, ALU.add).then_inc(factor_ready, 1)
                pool.wait_ge(factor_ready, i + 1)
                if i == 0:
                    for u in range(2):
                        step(0, u)
            with pool.Fori(1, S // 2) as k:
                step(k, 0)
                step(k, 1)

        @block.tensor
        def _(pe):
            def step(k, u):
                s = 2 * k + u
                pe.wait_ge(mixed_ready, s + 1)
                if not start(k, u):
                    pe.wait_ge(turn_kept, s)
                for j in range(FB):
                    mm = pe.transpose(turn_ps[:, j, :], mixed[:, j, :], c["ident"][:])
                mm.then_inc(turned, 1)
                pe.wait_ge(turn_kept, s + 1)
                if not start(k, u):
                    pe.wait_ge(res_ready, s)
                for j in range(FB):
                    mm = pe.matmul(out_ps[:, j, :], mixed_t[:, j, :], c["w_out"][:], start=True, stop=True)
                mm.then_inc(projected, 1)

            in_pairs(pe, step, S)

        @block.scalar
        def _(act):
            def turn(k, u):
                s = 2 * k + u
                act.wait_ge(turned, s + 1)
                if not start(k, u):
                    act.wait_ge(projected, s)
                act.copy(mixed_t[:], turn_ps[:, 0:FB, :]).then_inc(turn_kept, 1)

            def norm(k, u):
                act.wait_ge(offset_ready, 2 * k + u + 1)
                if not early(k, u):
                    act.wait_ge(y_out[u], 32 * k)
                    act.sem_inc(c["carrier"], 1)
                for j in range(FB):
                    ins = act.activation(y[:, u, j, :], res[:, u, j, :], ACT.Identity, bias=offset[:, j:j + 1], scale=scale[:, j:j + 1])
                ins.then_inc(y_ready, 1)

            def store(k, u):
                act.wait_ge(y_ready, 2 * k + u + 1)
                for p, rows, j in bucket_rows(out, 2 * k + u, end(k, u)):
                    act.dma_start(rows, y[p, u, j, :]).then_inc(y_out[u], 16)

            def step(k, u):
                s = 2 * k + u
                if not start(k, u):
                    norm(*behind(k, u))
                if not end(k, u):
                    turn(*ahead(k, u))
                if not start(k, u):
                    store(*behind(k, u))
                act.wait_ge(moments_ready, FB * (s + 1))
                if not start(k, u):
                    act.wait_ge(scale_ready, s)
                act.activation(dev[:], moments[:, u, :, 1], ACT.Sqrt, bias=eps[:, 0:1]).then_inc(dev_ready, 1)

            act.wait_ge(eps_set, 1)
            turn(0, 0)
            in_pairs(act, step, S, head=2)
            norm(S // 2 - 1, 1)
            store(S // 2 - 1, 1)
            act.wait_ge(y_out[0], 16 * S)
            act.wait_ge(y_out[1], 16 * S + 16)

        @block.vector
        def _(dve):
            def shares(k, u):
                dve.wait_ge(both_ready, 2 * k + u + 1)
                if not start(k, u):
                    dve.wait_ge(mixed_ready, 2 * k + u)
                dve.tensor_scalar(share[:], both[:, u, :, 0:H], 1e-10, None, ALU.add).then_inc(share_ready, 1)

            def inverse(k, u):
                dve.wait_ge(share_ready, 2 * k + u + 1)
                dve.reciprocal(share[:], share[:]).then_inc(inverse_ready, 1)

            def mix(k, u):
                s = 2 * k + u
                dve.wait_ge(inverse_ready, s + 1)
                if not start(k, u):
                    dve.wait_ge(turned, s)
                dve.tensor_tensor(by_head(mixed[:]), by_head(both[:, u, :, H:]), bcast(share[:], 2, DH), ALU.mult
                                  ).then_inc(mixed_ready, 1)

            def rescale(k, u):
                dve.wait_ge(dev_ready, 2 * k + u + 1)
                if not start(k, u):
                    dve.wait_ge(y_ready, 2 * k + u)
                dve.reciprocal(scale[:], dev[:]).then_inc(scale_ready, 1)

            def offsets(k, u):
                dve.wait_ge(scale_ready, 2 * k + u + 1)
                dve.scalar_tensor_tensor(offset[:], moments[:, u, :, 0], -1.0, scale[:], ALU.mult, ALU.mult).then_inc(offset_ready, 1)

            def step(k, u):
                s = 2 * k + u
                if not end(k, u):
                    shares(*ahead(k, u))
                if not start(k, u):
                    rescale(*behind(k, u))
                if not end(k, u):
                    inverse(*ahead(k, u))
                    if not start(k, u):
                        offsets(*behind(k, u))
                    mix(*ahead(k, u))
                elif not start(k, u):
                    offsets(*behind(k, u))
                dve.wait_ge(projected, s + 1)
                if not early(k, u):
                    dve.wait_ge(y_ready, s - 1)
                dve.tensor_tensor(res[:, u], out_ps[:, 0:FB, :], x_rows[:, ds(s * FB, FB), :], ALU.add).then_inc(res_ready, 1)
                dve.wait_ge(res_ready, s + 1)
                if not start(k, u):
                    dve.wait_ge(moments_ready, FB * s)
                    dve.sem_inc(c["carrier"], 1)
                for j in range(FB):
                    dve.bn_stats(stats[:, j, :], res[:, u, j, :]).then_inc(stats_ready, 1)
                dve.wait_ge(stats_ready, FB * s + FB)
                dve.sem_inc(c["carrier"], 1)
                for j in range(FB):
                    dve.bn_aggr(moments[:, u, j, :], stats[:, j, :]).then_inc(moments_ready, 1)

            dve.memset(eps[:], EPS).then_inc(eps_set, 1)
            shares(0, 0)
            inverse(0, 0)
            mix(0, 0)
            in_pairs(dve, step, S, head=2)
            rescale(S // 2 - 1, 1)
            offsets(S // 2 - 1, 1)


_INS = ["x", "src", "dst", "edge_attr_128"] + [f"L0_gnn_{m}_{p}" for m in ("q", "k", "v", "out", "eb") for p in "wb"]


def kernel(**inputs):
    import numpy as np
    import concourse.bacc as bacc
    from concourse.bass_utils import run_bass_kernel_spmd

    nc = bacc.Bacc("TRN2", target_bir_lowering=False, num_devices=1)
    arrays = {f"in_{name}": np.ascontiguousarray(inputs[name]) for name in _INS}
    args = [nc.dram_tensor(name, a.shape, mybir.dt.from_np(a.dtype), kind="ExternalInput").ap() for name, a in arrays.items()]
    out = nc.dram_tensor("out", (N, D), F32, kind="ExternalOutput").ap()
    build(nc, *args, out)
    return run_bass_kernel_spmd(nc, [arrays], core_ids=[0]).results[0]["out"]
```
